# Optimizing a Trainium2 kernel written in Bass

```python
import numpy as np
import jax
import jax.numpy as jnp

def _softmax(x, axis=-1):
    return jax.nn.softmax(x, axis=axis)

def _gelu(x):
    return jax.nn.gelu(x, approximate=True)

def _silu(x):
    return jax.nn.silu(x)

def _sigmoid(x):
    return jax.nn.sigmoid(x)

def _layernorm(x, axis=-1, eps=1e-05):
    m = jnp.mean(x, axis=axis, keepdims=True)
    v = jnp.var(x, axis=axis, keepdims=True)
    return (x - m) / jnp.sqrt(v + eps)

def _scatter_add(tgt, idx, src, axis=0):
    return tgt.at[idx].add(src)

def _segment_sum(src, seg, n):
    return jax.ops.segment_sum(src, seg, n)
kernel_name = 'mk_gnn_preln_d2_gnn_r32_f248a9'

def setup_inputs(seed: int=0):
    np.random.seed(seed)
    _w = jnp.asarray

    def _rec_inputs():
        import jax
        import jax.numpy as jnp
        _gk = jax.random.key(seed)
        x = -0.000202 + 1 * jax.random.normal(jax.random.fold_in(_gk, 1), (50000, 128), jnp.float32)
        src = jax.random.randint(jax.random.fold_in(_gk, 2), (50000,), 0, 50000, jnp.int32)
        dst = jnp.minimum((50000 * jax.random.uniform(jax.random.fold_in(_gk, 3), (50000,)) ** 2.0).astype(jnp.int32), 49999)
        _o = jnp.argsort(dst, stable=True)
        src = src[_o]
        dst = dst[_o]
        edge_attr_64 = -8.4373e-05 + 1.00001 * jax.random.normal(jax.random.fold_in(_gk, 12), (50000, 64), jnp.float32)
        return (x, src, dst, edge_attr_64)
    x, src, dst, edge_attr_64 = _rec_inputs()

    def _L0_gnn_setup():
        import jax, jax.numpy as jnp
        import numpy as np
        N_NODES = 50000
        N_EDGES = 25000
        D_IN = 128
        D_OUT = 128
        ALPHA = 0.2
        key = jax.random.key(seed)
        k1, k2, k3, k4 = jax.random.split(key, 4)
        x = jax.random.normal(k1, (N_NODES, D_IN), dtype=jnp.float32)
        W = jax.random.normal(k2, (D_IN, D_OUT), dtype=jnp.float32) * (1.414 / np.sqrt(D_IN))
        a = jax.random.normal(k3, (2 * D_OUT, 1), dtype=jnp.float32) * 0.1
        edge_index = jax.random.randint(k4, (2, N_EDGES), 0, N_NODES, dtype=jnp.int64)
        return {'x': x, 'W': W, 'a': a, 'edge_index': edge_index}
    _L0_gnn_all = _L0_gnn_setup()
    _L0_gnn_in = {k: v for k, v in _L0_gnn_all.items() if k in ('W', 'a')}
    del _L0_gnn_all

    def _L1_gnn_setup():
        import jax, jax.numpy as jnp
        import numpy as np
        N_NODES = 50000
        N_EDGES = 25000
        NODE_DIM = 128
        EDGE_DIM = 64
        HID = 256
        LN_EPS = 1e-05
        key = jax.random.key(seed)
        ks = jax.random.split(key, 16)

        def lin(k, fan_in, fan_out):
            bound = 1.0 / np.sqrt(fan_in)
            kw, kb = jax.random.split(k)
            W = jax.random.uniform(kw, (fan_in, fan_out), jnp.float32, -bound, bound)
            b = jax.random.uniform(kb, (fan_out,), jnp.float32, -bound, bound)
            return (W, b)
        W1, b1 = lin(ks[0], 2 * NODE_DIM + EDGE_DIM, HID)
        W2, b2 = lin(ks[1], HID, NODE_DIM)
        U1, b3 = lin(ks[2], 2 * NODE_DIM, HID)
        U2, b4 = lin(ks[3], HID, NODE_DIM)
        return {'node_features': jax.random.normal(ks[4], (N_NODES, NODE_DIM), jnp.float32), 'edge_features': jax.random.normal(ks[5], (N_EDGES, EDGE_DIM), jnp.float32), 'W1': W1, 'b1': b1, 'W2': W2, 'b2': b2, 'U1': U1, 'b3': b3, 'U2': U2, 'b4': b4, 'gamma': jnp.ones((NODE_DIM,), jnp.float32), 'beta': jnp.zeros((NODE_DIM,), jnp.float32), 'src': jax.random.randint(ks[6], (N_EDGES,), 0, N_NODES), 'dst': jax.random.randint(ks[7], (N_EDGES,), 0, N_NODES)}
    _L1_gnn_all = _L1_gnn_setup()
    _L1_gnn_in = {k: v for k, v in _L1_gnn_all.items() if k in ('W1', 'b1', 'W2', 'b2', 'U1', 'b3', 'U2', 'b4', 'gamma', 'beta')}
    del _L1_gnn_all
    return {'x': x, 'src': src, 'dst': dst, 'edge_attr_64': edge_attr_64, 'L0_gnn_W': _L0_gnn_in['W'], 'L0_gnn_a': _L0_gnn_in['a'], 'L1_gnn_W1': _L1_gnn_in['W1'], 'L1_gnn_b1': _L1_gnn_in['b1'], 'L1_gnn_W2': _L1_gnn_in['W2'], 'L1_gnn_b2': _L1_gnn_in['b2'], 'L1_gnn_U1': _L1_gnn_in['U1'], 'L1_gnn_b3': _L1_gnn_in['b3'], 'L1_gnn_U2': _L1_gnn_in['U2'], 'L1_gnn_b4': _L1_gnn_in['b4'], 'L1_gnn_gamma': _L1_gnn_in['gamma'], 'L1_gnn_beta': _L1_gnn_in['beta']}

def reference(x, src, dst, edge_attr_64, L0_gnn_W, L0_gnn_a, L1_gnn_W1, L1_gnn_b1, L1_gnn_W2, L1_gnn_b2, L1_gnn_U1, L1_gnn_b3, L1_gnn_U2, L1_gnn_b4, L1_gnn_gamma, L1_gnn_beta):
    import jax
    import jax.numpy as jnp

    def _L0_gnn_ref(x, W, a, edge_index):
        import jax, jax.numpy as jnp
        import numpy as np
        N_NODES = 50000
        N_EDGES = 25000
        D_IN = 128
        D_OUT = 128
        ALPHA = 0.2
        h = x @ W
        src, dst = (edge_index[0], edge_index[1])
        a1 = a[:D_OUT, 0]
        a2 = a[D_OUT:, 0]
        s1 = h @ a1
        s2 = h @ a2
        e = jax.nn.leaky_relu(s1[src] + s2[dst], negative_slope=ALPHA)
        attention = jax.nn.softmax(e)
        msgs = attention[:, None] * h[src]
        output = jax.ops.segment_sum(msgs, dst, num_segments=N_NODES)
        return output

    def _L1_gnn_ref(node_features, edge_features, W1, b1, W2, b2, U1, b3, U2, b4, gamma, beta, src, dst):
        import jax, jax.numpy as jnp
        import numpy as np
        N_NODES = 50000
        N_EDGES = 25000
        NODE_DIM = 128
        EDGE_DIM = 64
        HID = 256
        LN_EPS = 1e-05
        N = node_features.shape[0]
        msg_in = jnp.concatenate([node_features[src], node_features[dst], edge_features], axis=-1)
        m = jax.nn.gelu(msg_in @ W1 + b1, approximate=False) @ W2 + b2
        msum = jax.ops.segment_sum(m, dst, num_segments=N)
        cnt = jax.ops.segment_sum(jnp.ones((m.shape[0],), m.dtype), dst, num_segments=N)
        agg = msum / jnp.maximum(cnt, 1.0)[:, None]
        comb = jnp.concatenate([node_features, agg], axis=-1)
        upd = jax.nn.gelu(comb @ U1 + b3, approximate=False) @ U2 + b4
        x = upd + node_features
        mu = jnp.mean(x, axis=-1, keepdims=True)
        var = jnp.mean(jnp.square(x - mu), axis=-1, keepdims=True)
        return (x - mu) / jnp.sqrt(var + LN_EPS) * gamma + beta
    edge_index = jnp.stack([src, dst])
    h = jnp.maximum(_layernorm(x, axis=-1), 0.0)
    x = x + _L0_gnn_ref(h, L0_gnn_W, L0_gnn_a, edge_index)
    h = jnp.maximum(_layernorm(x, axis=-1), 0.0)
    x = x + _L1_gnn_ref(h, edge_attr_64, L1_gnn_W1, L1_gnn_b1, L1_gnn_W2, L1_gnn_b2, L1_gnn_U1, L1_gnn_b3, L1_gnn_U2, L1_gnn_b4, L1_gnn_gamma, L1_gnn_beta, src, dst)
    return x

_drawn_inputs = setup_inputs


def setup_inputs(seed=0):
    import zlib

    import numpy as np

    out = dict(_drawn_inputs(seed))
    spreads = {'L1_gnn_gamma': (1.0, 0.2), 'L1_gnn_beta': (0.0, 0.1)}
    factors = {'edge_attr_64': 8.0,
     'L0_gnn_W': 8.0,
     'L0_gnn_a': 8.0,
     'L1_gnn_W1': 5.132,
     'L1_gnn_b1': 38.745,
     'L1_gnn_W2': 4.869,
     'L1_gnn_b2': 64.0,
     'L1_gnn_b3': 5.023}
    for name, (base, spread) in spreads.items():
        noise = np.random.default_rng([zlib.crc32(name.encode()), seed]).standard_normal(out[name].shape)
        drawn = base * np.exp(spread * noise) if base else spread * noise
        out[name] = jnp.asarray(drawn.astype(out[name].dtype))
    for name, factor in factors.items():
        out[name] = (out[name] * factor).astype(out[name].dtype)
    return out
```

```python
from contextlib import ExitStack

import numpy as np

import concourse.bass as bass
from concourse import mybir

ALU = mybir.AluOpType
ACT = mybir.ActivationFunctionType
AX = mybir.AxisListType
F32 = mybir.dt.float32
F16 = mybir.dt.float16
BF16 = mybir.dt.bfloat16
I32 = mybir.dt.int32
RMAX = bass.bass_isa.ReduceOp.max
RADD = bass.bass_isa.ReduceOp.add

P = 128
N = 50000
E = 50000
D = 128
DE = 64
HID = 256
EPS = 1e-5
ALPHA = 0.2

NB = 392
NPAD = NB * P
NX = 392
S = NB + NX
XT = 512
SENT = NPAD
EPAD = NB * P
NT = 400
DT = (E + 2 * P + P - 1) // P * P
FAR = 60000.0


def gnn_kernel(nc, x, srcdst, dst, edge_t, edge_rows, W, a, W1, b1, W2, b2, U1, b3, U2, b4, gamma, beta, out):
    outer = ExitStack()

    here = []

    def sem(name):
        here.append(nc.alloc_semaphore(name))
        return here[-1]

    def end_section():
        nc.clear_and_free_semaphores(list(here))
        here.clear()
        nc.all_engine_barrier()

    def dram(name, shape, dt=F32):
        return nc.dram_tensor(name, shape, dt).ap()

    def sb_in(ctx):
        return lambda name, shape, dt=F32: ctx.enter_context(nc.sbuf_tensor(name, shape, dt))

    def past(eng, s, count):
        if isinstance(count, int) and count <= 0:
            return
        eng.wait_ge(s, count)

    def looped(eng, body, count):
        body(0)
        with eng.Fori(1, count) as i:
            body(i)

    passed = outer.enter_context(nc.semaphore("passed"))

    def held(eng, s, count):
        if isinstance(count, int):
            return past(eng, s, count)
        eng.wait_ge(s, count)
        eng.sem_inc(passed, 1)

    def pipelined(eng, emit, count, peeled=1):
        for i in range(peeled):
            for q in range(2):
                emit(i, q, lambda lag, p=2 * i + q: p - lag >= 0)
        with eng.Fori(peeled, count) as i:
            for q in range(2):
                emit(i, q, lambda lag: True)
        for q in range(2):
            emit(count, q, lambda lag, q=q: q - lag < 0)

    def before(i, q, lag):
        slot = (q - lag) % 2
        turn = (q - lag - slot) // 2
        return 2 * i + (q - lag), slot, i + (turn + 1)

    with outer:
        h_proj = dram("h_proj", [NPAD, D])
        s_src = dram("s_src", [NPAD, 1])
        s_dst = dram("s_dst", [NPAD, 1])
        far_list = dram("far_list", [2, XT], I32)
        x1b = dram("x1b", [NPAD, D])
        h1 = dram("h1", [NPAD + P, D])
        part0 = dram("part0", [NX + 1, P, D])
        GW = HID + 4
        part1 = dram("part1", [NX + 1, P, GW])

        sb = sb_in(outer)
        ident = sb("ident", [P, P])
        iota_f = sb("iota_f", [P, P])
        ctl = sb("ctl", [1, 3, NB + XT], I32)
        trips = sb("trips", [1, 4], I32)
        base = sb("base", [P, NB + XT])
        same = sb("same", [P, XT])
        idx = sb("idx", [P, S, 2], I32)
        dloc = sb("dloc", [P, S])
        wgt = sb("wgt", [P, S])

        with ExitStack() as ctx:
            sb = sb_in(ctx)
            ps = ctx.enter_context(nc.psum_tensor("ps_start", [P, NT], F32))
            i400 = sb("i400", [P, NT], I32)
            t400 = sb("t400", [P, NT])
            h400 = sb("h400", [P, NT], F16)
            dsts = sb("dsts", [P, NB], I32)
            bid = sb("bid", [P, NB], I32)
            bidf = sb("bidf", [P, NB])
            onesb = sb("onesb", [P, P], BF16)
            zerob = sb("zerob", [P, NT], BF16)
            above = sb("above", [P, 8, NT], BF16)
            st = sb("st", [P, NT])
            n1 = sb("n1", [P, NB])
            ni = sb("ni", [P, NB], I32)
            nx = sb("nx", [P, NB])
            zeros = sb("zeros", [P, NB])
            xend = sb("xend", [P, NB])
            shift = sb("shift", [P, NB])
            last = sb("last", [P, NB])
            junk = sb("junk", [P, NB])
            dstn = sb("dstn", [P, NB], I32)
            down = sb("down", [P, 2])
            xi = sb("xi", [P, 4], I32)
            xf = sb("xf", [P, 4])
            blkx = sb("blkx", [P, 4])
            valid = sb("valid", [P, 4])
            sx = sb("sx", [P, 4])
            sx2 = sb("sx2", [P, 4])
            lists = sb("lists", [P, 2, 4], I32)
            farb = sb("farb", [P, XT], I32)
            ti = sb("ti", [1, 2])
            ti2 = sb("ti2", [1, 2], I32)
            ztile = sb("ztile", [P, GW])

            c_in = sem("c_in")
            c_const = sem("c_const")
            c_ch = sem("c_ch")
            c_above = sem("c_above")
            c_mm = sem("c_mm")
            c_list = sem("c_list")
            c_far = sem("c_far")
            c_zero = sem("c_zero")
            c_z = sem("c_z")
            c_down = sem("c_down")

            with nc.Block() as block:
                @block.gpsimd
                def _(pool):
                    nc.gpsimd.iota(i400[:, :], [[1, NT]], 0, 0).then_inc(c_const, 1)
                    nc.gpsimd.iota(xi[:, :], [[1, 4]], 0, 4).then_inc(c_const, 1)
                    nc.gpsimd.memset(ident[:, :], 0.0).then_inc(c_const, 1)
                    nc.gpsimd.memset(zeros[:, :], 0.0).then_inc(c_const, 1)
                    nc.gpsimd.memset(onesb[:, :], 1.0).then_inc(c_const, 1)
                    nc.gpsimd.memset(zerob[:, :], 0.0).then_inc(c_const, 1)
                    nc.gpsimd.memset(ztile[:, :], 0.0).then_inc(c_z, 1)
                    pool.wait_ge(c_const, 3)
                    nc.gpsimd.affine_select(out=ident[:, :], in_=ident[:, :], compare_op=ALU.not_equal, fill=1.0,
                                            base=0, pattern=[[-1, P]], channel_multiplier=1)
                    nc.gpsimd.memset(idx[:, :, :], 0)
                    pool.wait_ge(c_down, 1)
                    nc.gpsimd.partition_all_reduce(down[:, 1:2], down[:, 0:1], P, RADD).then_inc(c_down, 1)

                @block.sync
                def _(sp):
                    sp.dma_start(dsts[:, :], dst[0:NPAD].rearrange("(p c) -> p c", c=NB)).then_inc(c_in, 16)
                    sp.dma_start(dstn[:, :], dst[1:NPAD + 1].rearrange("(p c) -> p c", c=NB)).then_inc(c_in, 16)
                    sp.wait_ge(c_z, 1)
                    sp.dma_start(part0[0], ztile[:, 0:D]).then_inc(c_zero, 16)
                    sp.dma_start(part1[0], ztile[:, :]).then_inc(c_zero, 16)
                    sp.dma_start(h1[NPAD:NPAD + P], ztile[:, 0:D]).then_inc(c_zero, 16)
                    sp.wait_ge(c_list, 1)
                    sp.dma_start(far_list[0].rearrange("(p j) -> p j", j=4), lists[:, 0, :]).then_inc(c_far, 16)
                    sp.dma_start(far_list[1].rearrange("(p j) -> p j", j=4), lists[:, 1, :]).then_inc(c_far, 16)
                    sp.wait_ge(c_far, 32)
                    sp.dma_start(ctl[0:1, 0:2, NB:NB + XT], far_list.rearrange("(o k) x -> o k x", o=1)).then_inc(c_far, 16)
                    sp.dma_start(farb[:, :], far_list[1:2, :].to_broadcast([P, XT])).then_inc(c_far, 16)
                    sp.wait_ge(c_far, 64)
                    sp.wait_ge(c_zero, 48)

                @block.tensor
                def _(pe):
                    pe.wait_ge(c_const, 6)
                    nc.tensor.matmul(ps[:, :], onesb[:, :], zerob[:, :], start=True, stop=False)

                    def body(i):
                        for j in range(8):
                            pe.wait_ge(c_above, 8 * i + j + 1)
                            nc.tensor.matmul(ps[:, :], onesb[:, :], above[:, j, :], start=False, stop=False).then_inc(c_mm, 1)
                    looped(pe, body, NB // 8)
                    nc.tensor.matmul(ps[:, :], onesb[:, :], zerob[:, :], start=False, stop=True).then_inc(c_mm, 1)

                @block.vector
                def _(dve):
                    count = [0]

                    def link(ins):
                        count[0] += 1
                        ins.then_inc(c_ch, 1)
                        dve.wait_ge(c_ch, count[0])

                    dve.wait_ge(c_const, 4)
                    dve.wait_ge(c_in, 32)
                    nc.vector.tensor_copy(t400[:, :], i400[:, :])
                    nc.vector.tensor_copy(h400[:, :], i400[:, :])
                    nc.vector.tensor_copy(iota_f[:, :], i400[:, 0:P])
                    nc.vector.tensor_copy(xf[:, :], xi[:, :])
                    nc.vector.memset(dloc[:, :], FAR)
                    link(nc.vector.tensor_scalar(bid[:, :], dsts[:, :], 7, None, ALU.arith_shift_right))
                    link(nc.vector.tensor_copy(bidf[:, :], bid[:, :]))
                    link(nc.vector.tensor_tensor(junk[:, :], dsts[:, :], dstn[:, :], ALU.is_gt))
                    nc.vector.tensor_reduce(down[:, 0:1], junk[:, :], AX.X, ALU.add).then_inc(c_down, 1)

                    def body(i):
                        for j in range(8):
                            past(dve, c_mm, 8 * (i - 1) + j + 1)
                            nc.vector.tensor_scalar(above[:, j, :], h400[:, :], bidf[:, bass.ds(8 * i + j, 1)], None,
                                                    ALU.is_gt).then_inc(c_above, 1)
                    looped(dve, body, NB // 8)
                    dve.wait_ge(c_mm, NB + 1)
                    link(nc.vector.tensor_copy(st[:, :], ps[:, :]))
                    link(nc.vector.tensor_tensor(n1[:, :], st[:, 1:NB + 1], st[:, 0:NB], ALU.subtract))
                    link(nc.vector.tensor_scalar(n1[:, :], n1[:, :], -1.0, 0.0, ALU.add, ALU.max))
                    link(nc.vector.tensor_copy(ni[:, :], n1[:, :]))
                    link(nc.vector.tensor_scalar(ni[:, :], ni[:, :], 7, None, ALU.arith_shift_right))
                    link(nc.vector.tensor_copy(nx[:, :], ni[:, :]))
                    link(nc.vector.tensor_tensor_scan(xend[:, :], nx[:, :], zeros[:, :], 0.0, ALU.add, ALU.add))
                    link(nc.vector.tensor_scalar(last[:, :], nx[:, :], 0.0, None, ALU.is_gt))
                    link(nc.vector.tensor_tensor(last[:, :], last[:, :], xend[:, :], ALU.mult))
                    link(nc.vector.tensor_tensor(shift[:, :], xend[:, :], nx[:, :], ALU.subtract))
                    link(nc.vector.tensor_scalar(shift[:, :], shift[:, :], -float(P), float(P), ALU.mult, ALU.add))
                    link(nc.vector.tensor_tensor(shift[:, :], shift[:, :], st[:, 0:NB], ALU.add))
                    for j in range(4):
                        link(nc.vector.tensor_scalar(junk[:, :], xend[:, :], xf[:, j:j + 1], 0.0, ALU.is_le, ALU.add,
                                                     accum_out=blkx[:, j:j + 1]))
                        link(nc.vector.scalar_tensor_tensor(junk[:, :], t400[:, 0:NB], blkx[:, j:j + 1], shift[:, :],
                                                            ALU.is_equal, ALU.mult, accum_out=sx[:, j:j + 1]))
                    link(nc.vector.tensor_scalar(valid[:, :], blkx[:, :], float(NB), None, ALU.is_lt))
                    link(nc.vector.tensor_scalar(sx2[:, :], xf[:, :], float(P), -float(E), ALU.mult, ALU.add))
                    link(nc.vector.tensor_tensor(sx[:, :], sx[:, :], sx2[:, :], ALU.add))
                    link(nc.vector.tensor_tensor(sx[:, :], sx[:, :], valid[:, :], ALU.mult))
                    link(nc.vector.tensor_scalar(sx[:, :], sx[:, :], float(E), None, ALU.add))
                    link(nc.vector.tensor_copy(lists[:, 0, :], sx[:, :]))
                    link(nc.vector.tensor_scalar(blkx[:, :], blkx[:, :], float(NB - 1), None, ALU.min))
                    nc.vector.tensor_copy(lists[:, 1, :], blkx[:, :]).then_inc(c_list, 1)
                    nc.vector.tensor_copy(ctl[0:1, 0, 0:NB], st[0:1, 0:NB])
                    nc.vector.tensor_copy(ctl[0:1, 1, 0:NB], t400[0:1, 0:NB])
                    nc.vector.tensor_copy(ctl[0:1, 2, 0:NB], last[0:1, :])
                    nc.vector.tensor_scalar(base[:, 0:NB], t400[:, 0:NB], float(P), None, ALU.mult)
                    link(nc.vector.tensor_scalar(ti[:, 0:1], xend[0:1, NB - 1:NB], float(NB + 7), None, ALU.add))
                    link(nc.vector.tensor_scalar(ti[:, 1:2], xend[0:1, NB - 1:NB], -1.0, 4.0, ALU.add, ALU.max))
                    link(nc.vector.tensor_copy(ti2[:, :], ti[:, :]))
                    nc.vector.tensor_scalar(trips[:, 0:1], ti2[:, 0:1], 3, None, ALU.arith_shift_right)
                    nc.vector.tensor_scalar(trips[:, 1:2], ti2[:, 1:2], 2, None, ALU.arith_shift_right)
                    dve.wait_ge(c_down, 2)
                    nc.vector.tensor_scalar(trips[:, 2:3], down[0:1, 1:2], 1.0, None, ALU.min)
                    dve.wait_ge(c_far, 64)
                    nc.vector.tensor_scalar(base[:, NB:NB + XT], farb[:, :], float(P), None, ALU.mult)
                    nc.vector.memset(same[:, 0:1], 0.0)
                    nc.vector.tensor_tensor(same[:, 1:XT], farb[:, 1:XT], farb[:, 0:XT - 1], ALU.is_equal)


        end_section()

        def unordered(eng):
            return eng.value_load(trips[0:1, 2:3], min_val=0, max_val=1)

        srcdst_s = dram("srcdst_s", [EPAD, 2], I32)
        edge_s = dram("edge_s", [EPAD, DE])
        edge_ts = dram("edge_ts", [DE, EPAD])
        with ExitStack() as ctx:
            sb = sb_in(ctx)
            CT = 56
            CC = CT * P
            pairs = sb("pairs", [P, NB, 2], I32)
            dcol = sb("dcol", [P, NB])
            rowi = sb("rowi", [P, CC], I32)
            rowf = sb("rowf", [P, CC])
            jnk = sb("jnk", [P, CC], BF16)
            below = sb("below", [P, NB])
            ties = sb("ties", [P, NB])
            place = sb("place", [P, NB])
            placei = sb("placei", [P, NB], I32)
            ltri = sb("ltri", [P, P])
            pi = sb("pi", [P, 1], I32)
            pf = sb("pf", [P, 1])
            pl1 = sb("pl1", [P, 1], I32)
            pr1 = sb("pr1", [P, 2], I32)
            er1 = sb("er1", [P, DE])
            et1 = sb("et1", [DE, P])
            psE = ctx.enter_context(nc.psum_tensor("psEs", [DE, P], F32))
            g_in = sem("g_in")
            g_row = sem("g_row")
            g_chunk = sem("g_chunk")
            g_ch = sem("g_ch")
            g_pi = sem("g_pi")
            g_er = sem("g_er")
            g_cp = sem("g_cp")
            g_sc = sem("g_sc")
            g_lr = sem("g_lr")
            g_tp = sem("g_tp")
            g_ev = sem("g_ev")
            g_st = sem("g_st")

            with nc.Block() as block:
                @block.sync
                def _(sp):
                    with sp.If(unordered(sp) == 1):
                        sp.dma_start(pairs[:, :, :], srcdst.rearrange("(c p) k -> p c k", p=P)).then_inc(g_in, 16)
                        for c in range(NB // CT):
                            past(sp, g_chunk, c)
                            sp.dma_start(rowi[:, :], dst[c * CC:(c + 1) * CC].rearrange("(o n) -> o n", o=1)
                                         .to_broadcast([P, CC])).then_inc(g_row, 16)

                @block.gpsimd
                def _(pool):
                    with pool.If(unordered(pool) == 1):
                        nc.gpsimd.iota(pi[:, :], [[0, 1]], 0, 1).then_inc(g_pi, 1)

                @block.vector
                def _(dve):
                    with dve.If(unordered(dve) == 1):
                        done = [0]

                        def link(ins):
                            done[0] += 1
                            ins.then_inc(g_ch, 1)
                            dve.wait_ge(g_ch, done[0])

                        dve.wait_ge(g_pi, 1)
                        link(nc.vector.tensor_copy(pf[:, :], pi[:, :]))
                        link(nc.vector.tensor_scalar(ltri[:, :], iota_f[:, :], pf[:, :], None, ALU.is_lt))
                        dve.wait_ge(g_in, 16)
                        link(nc.vector.tensor_copy(dcol[:, :], pairs[:, :, 1]))
                        link(nc.vector.memset(place[:, :], 0.0))

                        def compare(t):
                            return nc.vector.tensor_scalar(jnk[:, :], rowf[:, :], dcol[:, bass.ds(t, 1)], 0.0, ALU.is_lt,
                                                           ALU.add, accum_out=below[:, bass.ds(t, 1)])
                        for c in range(NB // CT):
                            t0 = c * CT
                            dve.wait_ge(g_row, 16 * (c + 1))
                            link(nc.vector.tensor_copy(rowf[:, :], rowi[:, :]))
                            if c > 0:
                                with dve.Fori(0, t0) as t:
                                    compare(t)
                            with dve.Fori(0, CT) as i:
                                tile = rowf[:, bass.ds(P * i, P)]
                                compare(i + t0)
                                nc.vector.scalar_tensor_tensor(jnk[:, 0:P], tile, dcol[:, bass.ds(i + t0, 1)], ltri[:, :],
                                                               ALU.is_equal, ALU.mult,
                                                               accum_out=ties[:, bass.ds(i + t0, 1)]).then_inc(g_ch, 1)
                                dve.wait_ge(g_ch, done[0] + 2 * i + 1)
                                nc.vector.tensor_scalar(tile, tile, -0.5, None, ALU.add).then_inc(g_ch, 1)
                                dve.wait_ge(g_ch, done[0] + 2 * i + 2)
                            done[0] += 2 * CT
                            if t0 + CT < NB:
                                with dve.Fori(t0 + CT, NB) as t:
                                    compare(t)
                            link(nc.vector.memset(pf[:, :], 0.0))
                            link(nc.vector.tensor_tensor(place[:, :], place[:, :], below[:, :], ALU.add))
                            nc.vector.memset(pf[:, :], 0.0).then_inc(g_chunk, 1)
                        link(nc.vector.tensor_tensor(place[:, :], place[:, :], ties[:, :], ALU.add))
                        link(nc.vector.tensor_copy(placei[:, :], place[:, :]))

            with nc.Block() as block:
                @block.gpsimd
                def _(pool):
                    with pool.If(unordered(pool) == 1):
                        with pool.Fori(0, NB) as i:
                            pool.dma_start(er1[:, :], edge_rows[bass.ds(P * i, P), :]).then_inc(g_er, 16)
                            nc.gpsimd.tensor_copy(pl1[:, :], placei[:, bass.ds(i, 1)]).then_inc(g_cp, 1)
                            nc.gpsimd.tensor_copy(pr1[:, :], pairs[:, bass.ds(i, 1), :].rearrange("p o k -> p (o k)")).then_inc(g_cp, 1)
                            held(pool, g_er, 16 * i + 16)
                            held(pool, g_cp, 2 * i + 2)
                            nc.gpsimd.indirect_dma_start(
                                out=srcdst_s[:, :], out_offset=bass.IndirectOffsetOnAxis(ap=pl1[:, 0:1], axis=0),
                                in_=pr1[:, :], in_offset=None).then_inc(g_sc, 16)
                            nc.gpsimd.indirect_dma_start(
                                out=edge_s[:, :], out_offset=bass.IndirectOffsetOnAxis(ap=pl1[:, 0:1], axis=0),
                                in_=er1[:, :], in_offset=None).then_inc(g_sc, 16)
                            held(pool, g_sc, 32 * i + 32)
                        pool.sem_inc(passed, 1)

            with nc.Block() as block:
                @block.sync
                def _(sp):
                    with sp.If(unordered(sp) == 1):
                        with sp.Fori(0, NB) as i:
                            held(sp, g_st, 16 * i)
                            sp.dma_start(er1[:, :], edge_s[bass.ds(P * i, P), :]).then_inc(g_lr, 16)
                            held(sp, g_ev, i + 1)
                            sp.dma_start(edge_ts[:, bass.ds(P * i, P)], et1[:, :]).then_inc(g_st, 16)
                        sp.wait_ge(g_st, 16 * NB)
                        sp.sem_inc(passed, 1)

                @block.tensor
                def _(pe):
                    with pe.If(unordered(pe) == 1):
                        with pe.Fori(0, NB) as i:
                            held(pe, g_lr, 16 * i + 16)
                            nc.tensor.transpose(psE[:, :], er1[:, :], ident[:, :]).then_inc(g_tp, 1)
                        pe.sem_inc(passed, 1)

                @block.vector
                def _(dve):
                    with dve.If(unordered(dve) == 1):
                        with dve.Fori(0, NB) as i:
                            dve.wait_ge(g_tp, i + 1)
                            nc.vector.tensor_copy(et1[:, :], psE[:, :]).then_inc(g_ev, 1)
                        dve.sem_inc(passed, 1)


        end_section()

        s12 = outer.enter_context(nc.sbuf_tensor("s12", [P, 2, NB], F32))
        with ExitStack() as ctx:
            sb = sb_in(ctx)
            xb = [sb(f"xb{q}", [P, 4, D]) for q in range(2)]
            hb = [sb(f"hb{q}", [P, 4, D]) for q in range(2)]
            hT = [sb(f"hT{q}", [P, 4, P]) for q in range(2)]
            pj = [sb(f"pj{q}", [P, 4, D]) for q in range(2)]
            stat = [sb(f"stat{q}", [P, 4, 6]) for q in range(2)]
            mv = [sb(f"mv{q}", [P, 4, 2]) for q in range(2)]
            std = [sb(f"std{q}", [P, 4]) for q in range(2)]
            rstd = [sb(f"rstd{q}", [P, 4]) for q in range(2)]
            nmr = [sb(f"nmr{q}", [P, 4]) for q in range(2)]
            Wsb = sb("Wsb", [P, D])
            WT = sb("WT", [P, D])
            asb = sb("asb", [P, 2])
            Wa = sb("Wa", [P, 2])
            eps = sb("eps", [P, 1])
            sT = sb("sT", [98, 8, P])
            psT = [ctx.enter_context(nc.psum_tensor(f"psT{q}", [P, 4, P], F32)) for q in range(2)]
            psW = [ctx.enter_context(nc.psum_tensor(f"psW{q}", [P, 4, P], F32)) for q in range(2)]
            psS = [ctx.enter_context(nc.psum_tensor(f"psS{q}", [P, 4, 2], F32)) for q in range(2)]
            psE = [ctx.enter_context(nc.psum_tensor(f"psE{q}", [P, 4, P], F32)) for q in range(2)]
            w_in = sem("a_w_in")
            x_in = [sem(f"a_x_in{q}") for q in range(2)]
            p_out = [sem(f"a_p_out{q}") for q in range(2)]
            wprep = sem("a_wprep")
            wt_ps = sem("a_wt_ps")
            stats = sem("a_stats")
            aggr = sem("a_aggr")
            stdev = sem("a_stdev")
            recip = sem("a_recip")
            shifted = sem("a_shifted")
            normed = sem("a_normed")
            turned = sem("a_turned")
            ht_ready = sem("a_ht_ready")
            projected = sem("a_projected")
            evacuated = sem("a_evacuated")
            s_turned = sem("a_s_turned")
            s_copied = sem("a_s_copied")
            s_stored = sem("a_s_stored")
            x_g = x.rearrange("(g j p) d -> g p j d", j=4, p=P)
            proj_g = h_proj.rearrange("(g j p) d -> g p j d", j=4, p=P)
            ITER = NB // 8

            with nc.Block() as block:
                @block.sync
                def _(sp):
                    sp.dma_start(Wsb[:, :], W).then_inc(w_in, 16)
                    sp.dma_start(asb[:, :], a).then_inc(w_in, 16)

                    def body(i):
                        for q in range(2):
                            past(sp, normed, 2 * (i - 1) + q + 1)
                            sp.dma_start(xb[q][:, :, :], x_g[bass.ds(2 * i + q, 1)].rearrange("g p j d -> (g p) j d")).then_inc(x_in[q], 16)
                    looped(sp, body, ITER)
                    sp.wait_ge(s_copied, 8)
                    for k, table in enumerate((s_src, s_dst)):
                        sp.dma_start(table.rearrange("(t c p) o -> c t (p o)", t=4, p=P), sT[:, 4 * k:4 * k + 4, :]).then_inc(s_stored, 16)
                    sp.wait_ge(s_stored, 32)

                @block.scalar
                def _(act):
                    act.wait_ge(wt_ps, 1)
                    nc.scalar.copy(WT[:, :], psE[0][:, 0, :]).then_inc(wprep, 1)
                    act.wait_ge(wt_ps, 2)
                    nc.scalar.copy(Wa[:, :], psE[1][:, 0, 0:2]).then_inc(wprep, 1)

                    def body(i):
                        for q in range(2):
                            g = 2 * i + q
                            act.wait_ge(aggr, g + 1)
                            nc.scalar.activation(std[q][:, :], mv[q][:, :, 1], ACT.Sqrt, bias=eps[:, :]).then_inc(stdev, 1)
                        for q in range(2):
                            g = 2 * i + q
                            act.wait_ge(shifted, g + 1)
                            past(act, turned, g - 1)
                            for j in range(4):
                                ins = nc.scalar.activation(hb[q][:, j, :], xb[q][:, j, :], ACT.Relu, bias=nmr[q][:, j:j + 1],
                                                           scale=rstd[q][:, j:j + 1])
                            ins.then_inc(normed, 1)
                        for q in range(2):
                            g = 2 * i + q
                            act.wait_ge(turned, g + 1)
                            past(act, projected, g - 1)
                            nc.scalar.copy(hT[q][:, :, :], psT[q][:, :, :]).then_inc(ht_ready, 1)
                            act.wait_ge(evacuated, g + 1)
                            act.dma_start(proj_g[bass.ds(g, 1)].rearrange("g p j d -> (g p) j d"), pj[q][:, :, :]).then_inc(p_out[q], 16)
                    looped(act, body, ITER)
                    for q in range(2):
                        act.wait_ge(p_out[q], 16 * ITER)

                @block.vector
                def _(dve):
                    nc.vector.memset(eps[:, :], EPS)

                    def body(i):
                        for q in range(2):
                            g = 2 * i + q
                            dve.wait_ge(x_in[q], 16 * (i + 1))
                            past(dve, aggr, g - 1)
                            for j in range(4):
                                ins = nc.vector.bn_stats(stat[q][:, j, :], xb[q][:, j, :])
                            ins.then_inc(stats, 1)
                        for q in range(2):
                            g = 2 * i + q
                            past(dve, shifted, g - 1)
                            held(dve, stats, g + 1)
                            for j in range(4):
                                ins = nc.vector.bn_aggr(mv[q][:, j, :], stat[q][:, j, :])
                            ins.then_inc(aggr, 1)
                        for q in range(2):
                            g = 2 * i + q
                            dve.wait_ge(stdev, g + 1)
                            past(dve, normed, g - 1)
                            nc.vector.reciprocal(rstd[q][:, :], std[q][:, :]).then_inc(recip, 1)
                        for q in range(2):
                            g = 2 * i + q
                            dve.wait_ge(recip, g + 1)
                            nc.vector.scalar_tensor_tensor(nmr[q][:, :], mv[q][:, :, 0], -1.0, rstd[q][:, :], ALU.mult,
                                                           ALU.mult).then_inc(shifted, 1)
                        for q in range(2):
                            g = 2 * i + q
                            dve.wait_ge(projected, g + 1)
                            past(dve, p_out[q], 16 * i)
                            nc.vector.tensor_copy(s12[:, :, bass.ds(4 * g, 4)], psS[q][:, :, :].rearrange("p j k -> p k j"))
                            nc.vector.tensor_copy(pj[q][:, :, :], psW[q][:, :, :]).then_inc(evacuated, 1)
                    looped(dve, body, ITER)
                    for t in range(8):
                        dve.wait_ge(s_turned, 4 * (t // 4) + 4)
                        nc.vector.tensor_copy(sT[:, t, :], psE[t // 4][0:98, t % 4, :]).then_inc(s_copied, 1)

                @block.tensor
                def _(pe):
                    pe.wait_ge(w_in, 32)
                    nc.tensor.transpose(psE[0][:, 0, :], Wsb[:, :], ident[:, :]).then_inc(wt_ps, 1)
                    pe.wait_ge(wprep, 1)
                    nc.tensor.matmul(psE[1][:, 0, 0:2], WT[:, :], asb[:, :], start=True, stop=True).then_inc(wt_ps, 1)
                    pe.wait_ge(wprep, 2)

                    def body(i):
                        for q in range(2):
                            g = 2 * i + q
                            pe.wait_ge(normed, g + 1)
                            past(pe, ht_ready, g - 1)
                            for j in range(4):
                                ins = nc.tensor.transpose(psT[q][:, j, :], hb[q][:, j, :], ident[:, :])
                            ins.then_inc(turned, 1)
                        for q in range(2):
                            g = 2 * i + q
                            pe.wait_ge(ht_ready, g + 1)
                            past(pe, evacuated, g - 1)
                            for j in range(4):
                                nc.tensor.matmul(psW[q][:, j, :], hT[q][:, j, :], Wsb[:, :], start=True, stop=True)
                                ins = nc.tensor.matmul(psS[q][:, j, :], hT[q][:, j, :], Wa[:, :], start=True, stop=True)
                            ins.then_inc(projected, 1)
                    looped(pe, body, ITER)
                    pe.wait_ge(evacuated, 2 * ITER)
                    for t in range(8):
                        nc.tensor.transpose(psE[t // 4][0:98, t % 4, :], s12[:, t // 4, 98 * (t % 4):98 * (t % 4) + 98],
                                            ident[:, :]).then_inc(s_turned, 1)

        end_section()

        with ExitStack() as ctx:
            sb = sb_in(ctx)
            K = 8
            idx8 = sb("idx8", [P, K, 2], I32)
            g8 = sb("g8", [P, K])
            row8 = sb("row8", [P, K, P])
            jnk8 = sb("jnk8", [P, K, P])
            s1e = sb("s1e", [P, S])
            s2e = sb("s2e", [P, S])
            ok = sb("ok", [P, S])
            tmp = sb("tmp", [P, S])
            sm = sb("sm", [P, 6])
            e_idx = [sem(f"e_idx{j}") for j in range(K)]
            e_row = [sem(f"e_row{j}") for j in range(K)]
            e_got = [sem(f"e_got{j}") for j in range(K)]
            e_init = sem("e_init")
            e_loc = sem("e_loc")
            e_kept = sem("e_kept")
            e_done = sem("e_done")
            e_ch = sem("e_ch")
            e_red = sem("e_red")
            e_exp = sem("e_exp")

            with nc.Block() as block:
                def groups(eng):
                    return eng.value_load(trips[0:1, 0:1], min_val=NB // K, max_val=S // K)

                @block.sync
                def _(sp):
                    def body(i, srcdst):
                        for j in range(K):
                            start = sp.value_load(ctl[0:1, 0, bass.ds(K * i + j, 1)], min_val=0, max_val=E)
                            held(sp, e_kept, i)
                            held(sp, e_got[j], 16 * i)
                            sp.dma_start(idx8[:, j, :], srcdst[bass.ds(start, P), :]).then_inc(e_idx[j], 16)
                    n = groups(sp)
                    with sp.If(unordered(sp) == 0):
                        looped(sp, lambda i: body(i, srcdst), n)
                        sp.sem_inc(passed, 1)
                    with sp.Else():
                        looped(sp, lambda i: body(i, srcdst_s), n)
                        sp.sem_inc(passed, 1)

                @block.scalar
                def _(act):
                    def body(i):
                        for j in range(K):
                            blk = act.value_load(ctl[0:1, 1, bass.ds(K * i + j, 1)], min_val=0, max_val=NB - 1)
                            past(act, e_done, i)
                            act.dma_start(row8[:, j, :], s_dst.rearrange("(b p) o -> b (p o)", p=P)[bass.ds(blk, 1), :]
                                          .to_broadcast([P, P])).then_inc(e_row[j], 16)
                    looped(act, body, groups(act))
                    act.wait_ge(e_red, 2)
                    nc.scalar.activation(wgt[:, :], tmp[:, :], ACT.Exp, bias=sm[:, 2:3], accum_out=sm[:, 3:4]).then_inc(e_exp, 1)

                @block.gpsimd
                def _(pool):
                    def body(i):
                        for j in range(K):
                            past(pool, e_done, i)
                            held(pool, e_idx[j], 16 * (i + 1))
                            nc.gpsimd.indirect_dma_start(
                                out=g8[:, j:j + 1], out_offset=None, in_=s_src[:, :],
                                in_offset=bass.IndirectOffsetOnAxis(ap=idx8[:, j, 0:1], axis=0)).then_inc(e_got[j], 16)
                    looped(pool, body, groups(pool))
                    pool.wait_ge(e_ch, 7)
                    nc.gpsimd.partition_all_reduce(sm[:, 1:2], sm[:, 0:1], P, RMAX).then_inc(e_red, 1)
                    pool.wait_ge(e_exp, 1)
                    nc.gpsimd.partition_all_reduce(sm[:, 4:5], sm[:, 3:4], P, RADD).then_inc(e_red, 1)

                @block.vector
                def _(dve):
                    nc.vector.memset(s1e[:, :], 0.0).then_inc(e_init, 1)
                    nc.vector.memset(s2e[:, :], 0.0).then_inc(e_init, 1)
                    dve.wait_ge(e_init, 2)

                    def body(i):
                        for j in range(K):
                            dve.wait_ge(e_idx[j], 16 * (i + 1))
                        nc.vector.tensor_copy(idx[:, bass.ds(K * i, K), :], idx8[:, :, :])
                        nc.vector.tensor_tensor(dloc[:, bass.ds(K * i, K)], idx8[:, :, 1], base[:, bass.ds(K * i, K)],
                                                ALU.subtract).then_inc(e_kept, 1)
                        dve.wait_ge(e_kept, i + 1)
                        for j in range(K):
                            dve.wait_ge(e_row[j], 16 * (i + 1))
                            nc.vector.scalar_tensor_tensor(jnk8[:, j, :], iota_f[:, :], dloc[:, bass.ds(K * i + j, 1)],
                                                           row8[:, j, :], ALU.is_equal, ALU.mult,
                                                           accum_out=s2e[:, bass.ds(K * i + j, 1)])
                        for j in range(K):
                            dve.wait_ge(e_got[j], 16 * (i + 1))
                        nc.vector.tensor_copy(s1e[:, bass.ds(K * i, K)], g8[:, :]).then_inc(e_done, 1)
                    n = groups(dve)
                    looped(dve, body, n)
                    dve.wait_ge(e_done, n)
                    count = [0]

                    def link(ins):
                        count[0] += 1
                        ins.then_inc(e_ch, 1)
                        dve.wait_ge(e_ch, count[0])
                    link(nc.vector.tensor_tensor(tmp[:, :], s1e[:, :], s2e[:, :], ALU.add))
                    link(nc.vector.scalar_tensor_tensor(s1e[:, :], tmp[:, :], ALPHA, tmp[:, :], ALU.mult, ALU.max))
                    link(nc.vector.tensor_scalar(ok[:, :], dloc[:, :], float(P), None, ALU.is_lt))
                    link(nc.vector.tensor_tensor(s1e[:, :], s1e[:, :], ok[:, :], ALU.mult))
                    link(nc.vector.tensor_scalar(ok[:, :], ok[:, :], -1.0, 3.0e38, ALU.add, ALU.mult))
                    link(nc.vector.tensor_tensor(tmp[:, :], s1e[:, :], ok[:, :], ALU.add))
                    link(nc.vector.tensor_reduce(sm[:, 0:1], tmp[:, :], AX.X, ALU.max))
                    dve.wait_ge(e_red, 1)
                    nc.vector.tensor_scalar(sm[:, 2:3], sm[:, 1:2], -1.0, None, ALU.mult).then_inc(e_red, 1)
                    dve.wait_ge(e_red, 3)
                    link(nc.vector.reciprocal(sm[:, 5:6], sm[:, 4:5]))
                    nc.vector.tensor_scalar(wgt[:, :], wgt[:, :], sm[:, 5:6], None, ALU.mult)

        end_section()

        for far in (True, False):
            with ExitStack() as ctx:
                sb = sb_in(ctx)
                t = "f" if far else "m"
                step0 = NB if far else 0
                K = 4
                idx4 = sb(f"idx4{t}", [P, K], I32)
                got = sb(f"got{t}", [P, K, D])
                oh = sb(f"oh{t}", [P, K, P])
                acc = sb(f"acc{t}", [P, K, D])
                psA = [ctx.enter_context(nc.psum_tensor(f"psA{t}{k}", [P, D], F32)) for k in range(K)]
                l_idx = sem(f"l_idx{t}")
                l_got = [sem(f"l_got{t}{k}") for k in range(K)]
                l_oh = sem(f"l_oh{t}")
                l_mm = sem(f"l_mm{t}")
                l_sum = sem(f"l_sum{t}")
                l_st = sem(f"l_st{t}")
                l_init = sem(f"l_init{t}")
                if not far:
                    x4 = sb("x4", [P, K, D])
                    part = sb("part", [P, K, D])
                    xs = sb("xs", [P, K, D])
                    xo = sb("xo", [P, K, D])
                    ho = sb("ho", [P, K, D])
                    betaB = sb("betaB", [P, D])
                    stat = sb("stat4", [P, K, 6])
                    mv = sb("mv4", [P, K, 2])
                    std = sb("std4", [P, K])
                    rstd = sb("rstd4", [P, K])
                    nmr = sb("nmr4", [P, K])
                    eps = sb("eps4", [P, 1])
                    l_x = sem("l_x")
                    l_part = sem("l_part")
                    l_c = sem("l_c")
                    l_tot = sem("l_tot")
                    l_new = sem("l_new")
                    l_stat = sem("l_stat")
                    l_aggr = sem("l_aggr")
                    l_std = sem("l_std")
                    l_rec = sem("l_rec")
                    l_shift = sem("l_shift")
                    l_h = sem("l_h")
                    l_ho = sem("l_ho")
                    x_g = x.rearrange("(g j p) d -> g p j d", j=K, p=P)
                    x1_g = x1b.rearrange("(g j p) d -> g p j d", j=K, p=P)
                    h1_g = h1[0:NPAD].rearrange("(g j p) d -> g p j d", j=K, p=P)

                with nc.Block() as block:
                    def trip(eng):
                        return eng.value_load(trips[0:1, 1:2], min_val=1, max_val=NX // K - 1) + 1 if far else NB // K

                    @block.gpsimd
                    def _(pool):
                        def body(i):
                            for k in range(K):
                                if k == 0:
                                    for m in range(K):
                                        held(pool, l_got[m], 16 * i)
                                    nc.gpsimd.tensor_copy(idx4[:, :], idx[:, bass.ds(K * i + step0, K), 0]).then_inc(l_idx, 1)
                                past(pool, l_mm, K * (i - 1) + k + 1)
                                held(pool, l_idx, i + 1)
                                nc.gpsimd.indirect_dma_start(
                                    out=got[:, k, :], out_offset=None, in_=h_proj[:, :],
                                    in_offset=bass.IndirectOffsetOnAxis(ap=idx4[:, k:k + 1], axis=0)).then_inc(l_got[k], 16)
                        looped(pool, body, trip(pool))

                    @block.tensor
                    def _(pe):
                        def body(i):
                            for k in range(K):
                                pe.wait_ge(l_oh, K * i + k + 1)
                                pe.wait_ge(l_got[k], 16 * (i + 1))
                                past(pe, l_sum, K * (i - 1) + k + 1)
                                nc.tensor.matmul(psA[k][:, :], oh[:, k, :], got[:, k, :], start=True, stop=True).then_inc(l_mm, 1)
                        looped(pe, body, trip(pe))

                    def attention(dve, i, k):
                        past(dve, l_mm, K * (i - 1) + k + 1)
                        s = bass.ds(K * i + (k + step0), 1)
                        nc.vector.tensor_scalar(oh[:, k, :], iota_f[:, :], dloc[:, s], wgt[:, s], ALU.is_equal,
                                                ALU.mult).then_inc(l_oh, 1)

                    if far:
                        @block.vector
                        def _(dve):
                            nc.vector.memset(acc[:, K - 1, :], 0.0).then_inc(l_init, 1)
                            dve.wait_ge(l_init, 1)

                            def body(i):
                                for k in range(K):
                                    attention(dve, i, k)
                                past(dve, l_st, 16 * i)
                                for k in range(K):
                                    dve.wait_ge(l_mm, K * i + k + 1)
                                    past(dve, l_sum, K * i + k)
                                    nc.vector.scalar_tensor_tensor(acc[:, k, :], acc[:, (k - 1) % K, :],
                                                                   same[:, bass.ds(K * i + k, 1)], psA[k][:, :],
                                                                   ALU.mult, ALU.add).then_inc(l_sum, 1)
                            looped(dve, body, trip(dve))

                        @block.sync
                        def _(sp):
                            def body(i):
                                sp.wait_ge(l_sum, K * (i + 1))
                                sp.dma_start(part0[bass.ds(K * i + 1, K)].rearrange("x p d -> p x d"), acc[:, :, :]).then_inc(l_st, 16)
                            n = trip(sp)
                            looped(sp, body, n)
                            held(sp, l_st, 16 * n)
                    else:
                        @block.sync
                        def _(sp):
                            sp.dma_start(betaB[:, :], beta.rearrange("(o d) -> o d", o=1).to_broadcast([P, D])).then_inc(l_c, 16)

                            def body(i):
                                past(sp, l_tot, K * i)
                                sp.dma_start(x4[:, :, :], x_g[bass.ds(i, 1)].rearrange("g p j d -> (g p) j d")).then_inc(l_x, 16)
                                for k in range(K):
                                    slot = sp.value_load(ctl[0:1, 2, bass.ds(K * i + k, 1)], min_val=0, max_val=NX)
                                    sp.dma_start(part[:, k, :], part0[bass.ds(slot, 1)].rearrange("x p d -> (x p) d")).then_inc(l_part, 16)
                            looped(sp, body, trip(sp))

                        @block.scalar
                        def _(act):
                            def body(i):
                                act.wait_ge(l_aggr, i + 1)
                                nc.scalar.activation(std[:, :], mv[:, :, 1], ACT.Sqrt, bias=eps[:, :]).then_inc(l_std, 1)
                                act.wait_ge(l_new, i + 1)
                                act.dma_start(x1_g[bass.ds(i, 1)].rearrange("g p j d -> (g p) j d"), xo[:, :, :]).then_inc(l_st, 16)
                                act.wait_ge(l_shift, i + 1)
                                past(act, l_ho, 16 * i)
                                for k in range(K):
                                    ins = nc.scalar.activation(ho[:, k, :], xs[:, k, :], ACT.Relu, bias=nmr[:, k:k + 1],
                                                               scale=rstd[:, k:k + 1])
                                ins.then_inc(l_h, 1)
                                act.wait_ge(l_h, i + 1)
                                act.dma_start(h1_g[bass.ds(i, 1)].rearrange("g p j d -> (g p) j d"), ho[:, :, :]).then_inc(l_ho, 16)
                            looped(act, body, NB // K)
                            act.wait_ge(l_st, 16 * (NB // K))
                            act.wait_ge(l_ho, 16 * (NB // K))

                        @block.vector
                        def _(dve):
                            nc.vector.memset(eps[:, :], EPS)
                            dve.wait_ge(l_c, 16)

                            def body(i):
                                for k in range(K):
                                    attention(dve, i, k)
                                dve.wait_ge(l_x, 16 * (i + 1))
                                dve.wait_ge(l_part, 16 * K * (i + 1))
                                past(dve, l_sum, K * i)
                                for k in range(K):
                                    nc.vector.tensor_tensor(acc[:, k, :], x4[:, k, :], part[:, k, :], ALU.add).then_inc(l_tot, 1)
                                past(dve, l_h, i)
                                for k in range(K):
                                    dve.wait_ge(l_tot, K * i + k + 1)
                                    dve.wait_ge(l_mm, K * i + k + 1)
                                    nc.vector.tensor_tensor(xs[:, k, :], psA[k][:, :], acc[:, k, :], ALU.add).then_inc(l_sum, 1)
                                for k in range(K):
                                    dve.wait_ge(l_sum, K * i + k + 1)
                                    nc.vector.bn_stats(stat[:, k, :], xs[:, k, :]).then_inc(l_stat, 1)
                                past(dve, l_st, 16 * i)
                                nc.vector.tensor_tensor(xo[:, :, :], xs[:, :, :],
                                                        betaB[:, :].rearrange("p (o d) -> p o d", o=1).to_broadcast([P, K, D]),
                                                        ALU.add).then_inc(l_new, 1)
                                held(dve, l_stat, K * (i + 1))
                                for k in range(K):
                                    ins = nc.vector.bn_aggr(mv[:, k, :], stat[:, k, :])
                                ins.then_inc(l_aggr, 1)
                                dve.wait_ge(l_std, i + 1)
                                nc.vector.reciprocal(rstd[:, :], std[:, :]).then_inc(l_rec, 1)
                                dve.wait_ge(l_rec, i + 1)
                                nc.vector.scalar_tensor_tensor(nmr[:, :], mv[:, :, 0], -1.0, rstd[:, :], ALU.mult,
                                                               ALU.mult).then_inc(l_shift, 1)
                            looped(dve, body, NB // K)
            end_section()

        weights = ExitStack()
        with weights:
            sb = sb_in(weights)
            W1s = sb("W1s", [P, 2, HID])
            W1e = sb("W1e", [DE + 1, HID])
            W2s = sb("W2s", [P, 2, D])
            U1s = sb("U1s", [P, 2, HID])
            U2s = sb("U2s", [P, 2, D])
            b2B = sb("b2B", [P, D])
            b3c = sb("b3c", [P, 2])
            b4B = sb("b4B", [P, D])
            gammaB = sb("gammaB", [P, D])
            ones = sb("ones", [P, 2])
            half = sb("half", [P, 2])
            m_w = outer.enter_context(nc.semaphore("m_w"))
            idx5 = [sb(f"idx5{q}", [P, 2, 2], I32) for q in range(2)]
            got = [sb(f"got5{q}", [P, 2, 2, D]) for q in range(2)]
            ef = [sb(f"ef{q}", [DE + 1, 2, P]) for q in range(2)]
            oh = [sb(f"oh5{q}", [P, 2, P]) for q in range(2)]
            gT = [sb(f"gT{q}", [P, 2, 2, P]) for q in range(2)]
            G = [sb(f"G{q}", [P, 2, HID]) for q in range(2)]
            acc4 = sb("acc4", [P, 4, GW])

            for far in (True, False):
                with ExitStack() as ctx:
                    sb = sb_in(ctx)
                    t = "f" if far else "m"
                    step0 = NB if far else 0
                    ITER = NB // 4
                    peel = 1 if far else 2

                    def pb(name, shape, ctx=ctx, t=t):
                        return ctx.enter_context(nc.psum_tensor(f"{name}{t}", shape, F32))
                    psT = pb("psT5", [P, 2, 2, P])
                    psH = [pb(f"psH{k}", [P, HID]) for k in range(2)]
                    psG = [pb(f"psG{k}", [P, HID + 2]) for k in range(2)]

                    def m(name, t=t):
                        return sem(f"m_{name}{t}")
                    m_idx, m_oh, m_turn, m_gT = m("idx"), m("oh"), m("turn"), m("gT")
                    m_hid, m_gelu, m_sum, m_sumd = m("hid"), m("gelu"), m("sum"), m("sumd")
                    m_got = [m(f"got{q}") for q in range(2)]
                    m_ef = [m(f"ef{q}") for q in range(2)]
                    m_st = [m(f"st{q}") for q in range(2)]
                    m_init = m("init")
                    if not far:
                        hb = [sb(f"hb5{q}", [P, 2, D]) for q in range(2)]
                        h4 = [sb(f"h4{q}", [P, 2, D]) for q in range(2)]
                        xb5 = [sb(f"xb5{q}", [P, 2, D]) for q in range(2)]
                        part = [sb(f"part5{q}", [P, 2, GW]) for q in range(2)]
                        gt = [sb(f"gt{q}", [P, 2, HID + 1]) for q in range(2)]
                        cn = [sb(f"cn{q}", [P, 2]) for q in range(2)]
                        inv = [sb(f"inv{q}", [P, 2]) for q in range(2)]
                        some = [sb(f"some{q}", [P, 2]) for q in range(2)]
                        b2m = [sb(f"b2m{q}", [P, 2, D]) for q in range(2)]
                        ag = [sb(f"ag{q}", [P, 2, D]) for q in range(2)]
                        nT = [sb(f"nT{q}", [P, 4, P]) for q in range(2)]
                        uT = [sb(f"uT{q}", [P, 2, 2 * P]) for q in range(2)]
                        v = [sb(f"v{q}", [P, 2, D]) for q in range(2)]
                        y = [sb(f"y{q}", [P, 2, D]) for q in range(2)]
                        o = [sb(f"o{q}", [P, 2, D]) for q in range(2)]
                        stat = [sb(f"stat5{q}", [P, 2, 6]) for q in range(2)]
                        mv = [sb(f"mv5{q}", [P, 2, 2]) for q in range(2)]
                        rstd = [sb(f"rstd5{q}", [P, 2]) for q in range(2)]
                        ve = [sb(f"ve{q}", [P, 2]) for q in range(2)]
                        psM = pb("psM", [P, 2, D])
                        psN = pb("psN", [P, 4, P])
                        psU = pb("psU", [P, 2, 2 * P])
                        m_hb = [m(f"hb{q}") for q in range(2)]
                        m_xb = [m(f"xb{q}") for q in range(2)]
                        m_pt = [m(f"pt{q}") for q in range(2)]
                        m_cnt, m_inv, m_b2m = m("cnt"), m("inv"), m("b2m")
                        m_w2, m_ag, m_nt, m_nT = m("w2"), m("ag"), m("nt"), m("nT")
                        m_u, m_uT, m_v, m_vd = m("u"), m("uT"), m("v"), m("vd")
                        m_h4, m_stat, m_aggr, m_ve, m_rstd = m("h4"), m("stat"), m("aggr"), m("ve"), m("rstd")
                        m_y, m_o = m("y"), m("o")
                        hb_g = h1[0:NPAD].rearrange("(g j p) d -> g p j d", j=2, p=P)
                        xb_g = x1b.rearrange("(g j p) d -> g p j d", j=2, p=P)
                        out_g = out.rearrange("(g j p) d -> g p j d", j=2, p=P)

                    with nc.Block() as block:
                        def trip(eng):
                            return eng.value_load(trips[0:1, 1:2], min_val=1, max_val=NX // 4 - 1) + 1 if far else ITER

                        @block.sync
                        def _(sp):
                            if far:
                                sp.dma_start(W1s[:, :, :], W1[0:2 * D].rearrange("(c p) h -> p c h", p=P)).then_inc(m_w, 16)
                                sp.dma_start(W1e[0:DE, :], W1[2 * D:2 * D + DE]).then_inc(m_w, 16)
                                sp.dma_start(W1e[DE:DE + 1, :], b1.rearrange("(o h) -> o h", o=1)).then_inc(m_w, 16)
                                sp.dma_start(W2s[:, :, :], W2.rearrange("(c p) d -> p c d", p=P)).then_inc(m_w, 16)
                                sp.dma_start(U1s[:, :, :], U1.rearrange("(c p) h -> p c h", p=P)).then_inc(m_w, 16)
                                sp.dma_start(U2s[:, :, :], U2.rearrange("(c p) d -> p c d", p=P)).then_inc(m_w, 16)
                                sp.dma_start(b3c[:, :], b3).then_inc(m_w, 16)
                                for row, vec in ((b2B, b2), (b4B, b4), (gammaB, gamma)):
                                    sp.dma_start(row[:, :], vec.rearrange("(o d) -> o d", o=1).to_broadcast([P, D])).then_inc(m_w, 16)

                            def emit(i, q, live, edge_t):
                                p, _, _ = before(i, q, 0)
                                if live(0):
                                    for k in range(2):
                                        start = sp.value_load(ctl[0:1, 0, bass.ds(2 * p + (k + step0), 1)], min_val=0, max_val=E)
                                        if k == 0:
                                            held(sp, m_hid, 2 * (p - 2) + 2)
                                        sp.dma_start(ef[q][0:DE, k, :], edge_t[:, bass.ds(start, P)]).then_inc(m_ef[q], 16)
                                    if not far:
                                        past(sp, m_nt, p - 1)
                                        held(sp, m_h4, p - 1)
                                        sp.dma_start(hb[q][:, :, :], hb_g[bass.ds(p, 1)].rearrange("g p j d -> (g p) j d")).then_inc(m_hb[q], 16)
                                        for k in range(2):
                                            slot = sp.value_load(ctl[0:1, 2, bass.ds(2 * p + k, 1)], min_val=0, max_val=NX)
                                            if k == 0:
                                                held(sp, m_sumd, 2 * (p - 2) + 2)
                                            sp.dma_start(part[q][:, k, :], part1[bass.ds(slot, 1)].rearrange("x p d -> (x p) d")).then_inc(m_pt[q], 16)
                                if not far and live(1):
                                    p1, q1, _ = before(i, q, 1)
                                    held(sp, m_o, p1 - 1)
                                    sp.dma_start(xb5[q1][:, :, :], xb_g[bass.ds(p1, 1)].rearrange("g p j d -> (g p) j d")).then_inc(m_xb[q1], 16)
                                if far and live(1):
                                    p1, q1, _ = before(i, q, 1)
                                    held(sp, m_sumd, 2 * p1 + 2)
                                    sp.dma_start(part1[bass.ds(2 * p1 + 1, 2)].rearrange("x p d -> p x d"),
                                                 acc4[:, 2 * q1:2 * q1 + 2, :]).then_inc(m_st[q1], 16)
                            n = trip(sp)
                            with sp.If(unordered(sp) == 0):
                                pipelined(sp, lambda i, q, live: emit(i, q, live, edge_t), n, peel)
                                sp.sem_inc(passed, 1)
                            with sp.Else():
                                pipelined(sp, lambda i, q, live: emit(i, q, live, edge_ts), n, peel)
                                sp.sem_inc(passed, 1)
                            if far:
                                for q in range(2):
                                    held(sp, m_st[q], 16 * n)

                        @block.gpsimd
                        def _(pool):
                            if far:
                                nc.gpsimd.memset(ones[:, :], 1.0).then_inc(m_init, 1)
                                nc.gpsimd.memset(half[:, :], -0.5).then_inc(m_init, 1)
                                nc.gpsimd.memset(acc4[:, :, :], 0.0).then_inc(m_init, 1)

                            def emit(i, q, live):
                                p, _, turn = before(i, q, 0)
                                if live(0):
                                    held(pool, m_got[q], 64 * (turn - 1))
                                    nc.gpsimd.tensor_copy(idx5[q][:, :, :], idx[:, bass.ds(2 * p + step0, 2), :]).then_inc(m_idx, 1)
                                    past(pool, m_turn, p - 1)
                                    held(pool, m_idx, p + 1)
                                    for k in range(2):
                                        for c in range(2):
                                            nc.gpsimd.indirect_dma_start(
                                                out=got[q][:, k, c, :], out_offset=None, in_=h1[:, :],
                                                in_offset=bass.IndirectOffsetOnAxis(ap=idx5[q][:, k, c:c + 1], axis=0)).then_inc(m_got[q], 16)
                                if far:
                                    return
                                if live(1):
                                    p1, q1, turn1 = before(i, q, 1)
                                    past(pool, m_vd, p1 - 1)
                                    held(pool, m_hb[q1], 16 * turn1)
                                    nc.gpsimd.tensor_tensor(h4[q1][:, :, :], hb[q1][:, :, :],
                                                            b4B[:, :].rearrange("p (o d) -> p o d", o=1).to_broadcast([P, 2, D]),
                                                            ALU.add).then_inc(m_h4, 1)
                                if live(2):
                                    p2, q2, _ = before(i, q, 2)
                                    past(pool, m_o, p2 - 1)
                                    held(pool, m_ve, p2 + 1)
                                    nc.gpsimd.tensor_tensor(rstd[q2][:, :], ve[q2][:, :], half[:, :], ALU.pow).then_inc(m_rstd, 1)
                            pipelined(pool, emit, trip(pool), peel)

                        @block.tensor
                        def _(pe):
                            if far:
                                pe.wait_ge(m_w, 160)
                                pe.wait_ge(m_init, 5)

                            def hidden(i, q, k):
                                p, _, turn = before(i, q, 0)
                                if k == 0:
                                    pe.wait_ge(m_gT, p + 1)
                                    pe.wait_ge(m_ef[q], 32 * turn)
                                past(pe, m_gelu, 2 * p + (k - 1))
                                nc.tensor.matmul(psH[k][:, :], gT[q][:, k, 0, :], W1s[:, 0, :], start=True, stop=False)
                                nc.tensor.matmul(psH[k][:, :], gT[q][:, k, 1, :], W1s[:, 1, :], start=False, stop=False)
                                nc.tensor.matmul(psH[k][:, :], ef[q][:, k, :], W1e[:, :], start=False, stop=True).then_inc(m_hid, 1)

                            def emit(i, q, live):
                                p, _, turn = before(i, q, 0)
                                p1, q1, turn1 = before(i, q, 1)
                                p2, q2, turn2 = before(i, q, 2)
                                if live(0):
                                    pe.wait_ge(m_got[q], 64 * turn)
                                    past(pe, m_gT, p)
                                    for k in range(2):
                                        for c in range(2):
                                            ins = nc.tensor.transpose(psT[:, k, c, :], got[q][:, k, c, :], ident[:, :])
                                    ins.then_inc(m_turn, 1)
                                if live(1):
                                    for k in range(2):
                                        pe.wait_ge(m_gelu, 2 * p1 + (k + 1))
                                        pe.wait_ge(m_oh, p1 + 1)
                                        past(pe, m_sumd, 2 * p1 + (k - 1))
                                        for c in range(2):
                                            nc.tensor.matmul(psG[k][:, c * P:(c + 1) * P], G[q1][:, k, c * P:(c + 1) * P],
                                                             oh[q1][:, k, :], start=True, stop=True)
                                        nc.tensor.matmul(psG[k][:, HID:HID + 2], oh[q1][:, k, :], ones[:, :], start=True,
                                                         stop=True).then_inc(m_sum, 1)
                                if live(0):
                                    hidden(i, q, 0)
                                if not far and live(1):
                                    pe.wait_ge(m_sumd, 2 * p1 + 2)
                                    past(pe, m_vd, p1 - 1)
                                    for k in range(2):
                                        for c in range(2):
                                            ins = nc.tensor.matmul(psM[:, k, :], gt[q1][:, k, c * P:(c + 1) * P], W2s[:, c, :],
                                                                   start=(c == 0), stop=(c == 1))
                                    ins.then_inc(m_w2, 1)
                                if live(0):
                                    hidden(i, q, 1)
                                if far:
                                    return
                                if live(1):
                                    pe.wait_ge(m_ag, p1 + 1)
                                    pe.wait_ge(m_hb[q1], 16 * turn1)
                                    past(pe, m_nT, p1)
                                    for k in range(2):
                                        nc.tensor.transpose(psN[:, k, :], hb[q1][:, k, :], ident[:, :])
                                    for k in range(2):
                                        ins = nc.tensor.transpose(psN[:, 2 + k, :], ag[q1][:, k, :], ident[:, :])
                                    ins.then_inc(m_nt, 1)
                                if live(2):
                                    pe.wait_ge(m_uT, p2 + 1)
                                    if live(1):
                                        pe.wait_ge(m_ag, p1 + 1)
                                    else:
                                        past(pe, m_vd, p2)
                                    for k in range(2):
                                        for c in range(2):
                                            ins = nc.tensor.matmul(psM[:, k, :], uT[q2][:, c, k * P:(k + 1) * P], U2s[:, c, :],
                                                                   start=(c == 0), stop=(c == 1))
                                    ins.then_inc(m_v, 1)
                                if live(1):
                                    pe.wait_ge(m_nT, p1 + 1)
                                    past(pe, m_uT, p1)
                                    for c in range(2):
                                        nc.tensor.matmul(psU[:, c, :], U1s[:, 0, c * P:(c + 1) * P], nT[q1][:, 0:2, :],
                                                         start=True, stop=False)
                                        ins = nc.tensor.matmul(psU[:, c, :], U1s[:, 1, c * P:(c + 1) * P], nT[q1][:, 2:4, :],
                                                               start=False, stop=True)
                                    ins.then_inc(m_u, 1)
                            pipelined(pe, emit, trip(pe), peel)

                        @block.scalar
                        def _(act):
                            def emit(i, q, live):
                                p, _, _ = before(i, q, 0)
                                p1, q1, _ = before(i, q, 1)
                                p2, q2, turn2 = before(i, q, 2)
                                if live(0):
                                    act.wait_ge(m_turn, p + 1)
                                    past(act, m_hid, 2 * (p - 2) + 2)
                                    nc.scalar.copy(gT[q][:, :, :, :], psT[:, :, :, :]).then_inc(m_gT, 1)
                                    for k in range(2):
                                        act.wait_ge(m_hid, 2 * p + (k + 1))
                                        past(act, m_sum, 2 * (p - 2) + 2)
                                        nc.scalar.activation(G[q][:, k, :], psH[k][:, :], ACT.Gelu).then_inc(m_gelu, 1)
                                if far:
                                    return
                                if live(1):
                                    act.wait_ge(m_nt, p1 + 1)
                                    past(act, m_u, p1 - 1)
                                    nc.scalar.copy(nT[q1][:, :, :], psN[:, :, :]).then_inc(m_nT, 1)
                                    act.wait_ge(m_u, p1 + 1)
                                    past(act, m_v, p1 - 1)
                                    for c in range(2):
                                        ins = nc.scalar.activation(uT[q1][:, c, :], psU[:, c, :], ACT.Gelu, bias=b3c[:, c:c + 1])
                                    ins.then_inc(m_uT, 1)
                                if live(2):
                                    act.wait_ge(m_o, p2 + 1)
                                    act.dma_start(out_g[bass.ds(p2, 1)].rearrange("g p j d -> (g p) j d"), o[q2][:, :, :]).then_inc(m_st[q2], 16)
                            pipelined(act, emit, trip(act), peel)
                            if not far:
                                for q in range(2):
                                    act.wait_ge(m_st[q], 16 * ITER)

                        @block.vector
                        def _(dve):
                            if far:
                                nc.vector.memset(ef[0][DE:DE + 1, :, :], 1.0).then_inc(m_init, 1)
                                nc.vector.memset(ef[1][DE:DE + 1, :, :], 1.0).then_inc(m_init, 1)
                                dve.wait_ge(m_init, 5)

                            def emit(i, q, live):
                                p, _, _ = before(i, q, 0)
                                p1, q1, turn1 = before(i, q, 1)
                                p2, q2, turn2 = before(i, q, 2)
                                if live(0):
                                    past(dve, m_sum, 2 * (p - 2) + 2)
                                    for k in range(2):
                                        ins = nc.vector.tensor_scalar(oh[q][:, k, :], iota_f[:, :],
                                                                      dloc[:, bass.ds(2 * p + (k + step0), 1)], None, ALU.is_equal)
                                    ins.then_inc(m_oh, 1)
                                if far and live(1):
                                    past(dve, m_st[q1], 16 * (turn1 - 1))
                                    for k in range(2):
                                        dve.wait_ge(m_sum, 2 * p1 + (k + 1))
                                        past(dve, m_sumd, 2 * p1 + k)
                                        a4 = 2 * q1 + k
                                        nc.vector.scalar_tensor_tensor(acc4[:, a4, 0:HID + 1], acc4[:, (a4 - 1) % 4, 0:HID + 1],
                                                                       same[:, bass.ds(2 * p1 + k, 1)], psG[k][:, 0:HID + 1],
                                                                       ALU.mult, ALU.add).then_inc(m_sumd, 1)
                                if far:
                                    return
                                if live(1):
                                    dve.wait_ge(m_pt[q1], 32 * turn1)
                                    past(dve, m_w2, p1 - 1)
                                    for k in range(2):
                                        dve.wait_ge(m_sum, 2 * p1 + (k + 1))
                                        nc.vector.tensor_tensor(gt[q1][:, k, :], psG[k][:, 0:HID + 1], part[q1][:, k, 0:HID + 1],
                                                                ALU.add).then_inc(m_sumd, 1)
                                    dve.wait_ge(m_sumd, 2 * p1 + 2)
                                    nc.vector.tensor_scalar(cn[q1][:, :], gt[q1][:, :, HID], 1.0, None, ALU.max).then_inc(m_cnt, 1)
                                    nc.vector.tensor_scalar(some[q1][:, :], gt[q1][:, :, HID], 1.0, None, ALU.min).then_inc(m_cnt, 1)
                                if live(1):
                                    dve.wait_ge(m_cnt, 2 * p1 + 2)
                                    nc.vector.reciprocal(inv[q1][:, :], cn[q1][:, :]).then_inc(m_inv, 1)
                                    for k in range(2):
                                        ins = nc.vector.tensor_scalar(b2m[q1][:, k, :], b2B[:, :], some[q1][:, k:k + 1], None, ALU.mult)
                                    ins.then_inc(m_b2m, 1)
                                    dve.wait_ge(m_inv, p1 + 1)
                                    dve.wait_ge(m_b2m, p1 + 1)
                                    dve.wait_ge(m_w2, p1 + 1)
                                    past(dve, m_nt, p1 - 1)
                                    for k in range(2):
                                        ins = nc.vector.scalar_tensor_tensor(ag[q1][:, k, :], psM[:, k, :], inv[q1][:, k:k + 1],
                                                                             b2m[q1][:, k, :], ALU.mult, ALU.add)
                                    ins.then_inc(m_ag, 1)
                                if live(2):
                                    dve.wait_ge(m_v, p2 + 1)
                                    dve.wait_ge(m_h4, p2 + 1)
                                    nc.vector.tensor_tensor(v[q2][:, :, :], psM[:, :, :], h4[q2][:, :, :], ALU.add).then_inc(m_vd, 1)
                                    dve.wait_ge(m_vd, p2 + 1)
                                    for k in range(2):
                                        ins = nc.vector.bn_stats(stat[q2][:, k, :], v[q2][:, k, :])
                                    ins.then_inc(m_stat, 1)
                                    held(dve, m_stat, p2 + 1)
                                    for k in range(2):
                                        ins = nc.vector.bn_aggr(mv[q2][:, k, :], stat[q2][:, k, :])
                                    ins.then_inc(m_aggr, 1)
                                    dve.wait_ge(m_aggr, p2 + 1)
                                    nc.vector.tensor_scalar(ve[q2][:, :], mv[q2][:, :, 1], EPS, None, ALU.add).then_inc(m_ve, 1)
                                    for k in range(2):
                                        ins = nc.vector.scalar_tensor_tensor(y[q2][:, k, :], v[q2][:, k, :], mv[q2][:, k, 0:1],
                                                                             gammaB[:, :], ALU.subtract, ALU.mult)
                                    ins.then_inc(m_y, 1)
                                    dve.wait_ge(m_y, p2 + 1)
                                    dve.wait_ge(m_rstd, p2 + 1)
                                    dve.wait_ge(m_xb[q2], 16 * turn2)
                                    past(dve, m_st[q2], 16 * (turn2 - 1))
                                    for k in range(2):
                                        ins = nc.vector.scalar_tensor_tensor(o[q2][:, k, :], y[q2][:, k, :], rstd[q2][:, k:k + 1],
                                                                             xb5[q2][:, k, :], ALU.mult, ALU.add)
                                    ins.then_inc(m_o, 1)
                            pipelined(dve, emit, trip(dve), peel)
                end_section()



_OUT = "out_dram"


def kernel(**inputs):
    import concourse.bacc as _bacc
    from concourse.bass_utils import run_bass_kernel_spmd as _run

    def padded(v, rows, fill):
        return np.concatenate([v, np.full((rows - v.shape[0],) + v.shape[1:], fill, v.dtype)])

    g = {k: np.asarray(v) for k, v in inputs.items()}
    src, dst = padded(g["src"], EPAD, 0), padded(g["dst"], DT, SENT)
    arrays = {
        "x": padded(g["x"], NPAD, 0),
        "srcdst": np.stack([src, dst[:EPAD]], axis=1),
        "dst": dst,
        "edge_t": np.ascontiguousarray(padded(g["edge_attr_64"], EPAD, 0).T),
        "edge_rows": padded(g["edge_attr_64"], EPAD, 0),
        "W": g["L0_gnn_W"], "a": g["L0_gnn_a"].reshape(2, D).T,
        "W1": g["L1_gnn_W1"], "b1": g["L1_gnn_b1"], "W2": g["L1_gnn_W2"], "b2": g["L1_gnn_b2"],
        "U1": g["L1_gnn_U1"], "b3": g["L1_gnn_b3"].reshape(2, P).T, "U2": g["L1_gnn_U2"], "b4": g["L1_gnn_b4"],
        "gamma": g["L1_gnn_gamma"], "beta": g["L1_gnn_beta"],
    }
    nc = _bacc.Bacc("TRN2", target_bir_lowering=False, num_devices=1)
    named, args = {}, []
    for name, v in arrays.items():
        named[f"in_{name}"] = np.ascontiguousarray(v)
        args.append(nc.dram_tensor(f"in_{name}", v.shape, mybir.dt.from_np(v.dtype), kind="ExternalInput").ap())
    args.append(nc.dram_tensor(_OUT, (NPAD, D), F32, kind="ExternalOutput").ap())
    gnn_kernel(nc, *args)
    r = _run(nc, [named], core_ids=[0])
    return r.results[0][_OUT][:N]
```

```python
from contextlib import ExitStack

import numpy as np

import concourse.bass as bass
from concourse import mybir

ALU = mybir.AluOpType
ACT = mybir.ActivationFunctionType
AX = mybir.AxisListType
F32 = mybir.dt.float32
F16 = mybir.dt.float16
BF16 = mybir.dt.bfloat16
I32 = mybir.dt.int32
RMAX = bass.bass_isa.ReduceOp.max
RADD = bass.bass_isa.ReduceOp.add

P = 128
N = 50000
E = 50000
D = 128
DP = D + 2
DE = 64
HID = 256
EPS = 1e-5
ALPHA = 0.2

NB = 392
NPAD = NB * P
NX = 392
S = NB + NX
XT = 512
SENT = NPAD
EPAD = NB * P
NT = 400
DT = (E + 2 * P + P - 1) // P * P
FAR = 60000.0


def gnn_kernel(nc, x, srcdst, dst, edge_t, edge_rows, W, a, W1, b1, W2, b2, U1, b3, U2, b4, gamma, beta, out):
    outer = ExitStack()

    here = []

    def sem(name):
        here.append(nc.alloc_semaphore(name))
        return here[-1]

    def end_section():
        nc.clear_and_free_semaphores(list(here))
        here.clear()
        nc.all_engine_barrier()

    def dram(name, shape, dt=F32):
        return nc.dram_tensor(name, shape, dt).ap()

    def sb_in(ctx):
        return lambda name, shape, dt=F32: ctx.enter_context(nc.sbuf_tensor(name, shape, dt))

    def past(eng, s, count):
        if isinstance(count, int) and count <= 0:
            return
        eng.wait_ge(s, count)

    def looped(eng, body, count):
        body(0)
        with eng.Fori(1, count) as i:
            body(i)

    passed = outer.enter_context(nc.semaphore("passed"))

    def held(eng, s, count):
        if isinstance(count, int):
            return past(eng, s, count)
        eng.wait_ge(s, count)
        eng.sem_inc(passed, 1)

    def pipelined(eng, emit, count, peeled=1):
        for i in range(peeled):
            for q in range(2):
                emit(i, q, lambda lag, p=2 * i + q: p - lag >= 0)
        with eng.Fori(peeled, count) as i:
            for q in range(2):
                emit(i, q, lambda lag: True)
        for d in range(4):
            emit(count + d // 2, d % 2, lambda lag, d=d: d - lag < 0)

    def before(i, q, lag):
        slot = (q - lag) % 2
        turn = (q - lag - slot) // 2
        return 2 * i + (q - lag), slot, i + (turn + 1)

    with outer:
        h_proj = dram("h_proj", [NPAD, DP])
        s_dst = dram("s_dst", [NPAD, 1])
        edge_proj = dram("edge_proj", [S, P, D])
        far_list = dram("far_list", [2, XT], I32)
        x1b = dram("x1b", [NPAD, D])
        h1 = dram("h1", [NPAD + P, D])
        part0 = dram("part0", [NX + 1, P, D])
        GW = HID + 4
        part1 = dram("part1", [NX + 1, P, GW])

        sb = sb_in(outer)
        ident = sb("ident", [P, P])
        iota_f = sb("iota_f", [P, P])
        ctl = sb("ctl", [1, 3, NB + XT], I32)
        trips = sb("trips", [1, 4], I32)
        base = sb("base", [P, NB + XT])
        same = sb("same", [P, XT])
        idx = sb("idx", [P, S, 2], I32)
        dloc = sb("dloc", [P, S])
        wgt = sb("wgt", [P, S])

        with ExitStack() as ctx:
            sb = sb_in(ctx)
            ps = ctx.enter_context(nc.psum_tensor("ps_start", [P, NT], F32))
            i400 = sb("i400", [P, NT], I32)
            t400 = sb("t400", [P, NT])
            h400 = sb("h400", [P, NT], F16)
            dsts = sb("dsts", [P, NB], I32)
            bid = sb("bid", [P, NB], I32)
            bidf = sb("bidf", [P, NB])
            onesb = sb("onesb", [P, P], BF16)
            zerob = sb("zerob", [P, NT], BF16)
            above = sb("above", [P, 8, NT], BF16)
            st = sb("st", [P, NT])
            n1 = sb("n1", [P, NB])
            ni = sb("ni", [P, NB], I32)
            nx = sb("nx", [P, NB])
            zeros = sb("zeros", [P, NB])
            xend = sb("xend", [P, NB])
            shift = sb("shift", [P, NB])
            last = sb("last", [P, NB])
            junk = sb("junk", [P, NB])
            dstn = sb("dstn", [P, NB], I32)
            down = sb("down", [P, 2])
            xi = sb("xi", [P, 4], I32)
            xf = sb("xf", [P, 4])
            blkx = sb("blkx", [P, 4])
            valid = sb("valid", [P, 4])
            sx = sb("sx", [P, 4])
            sx2 = sb("sx2", [P, 4])
            lists = sb("lists", [P, 2, 4], I32)
            farb = sb("farb", [P, XT], I32)
            ti = sb("ti", [1, 3])
            ti2 = sb("ti2", [1, 3], I32)
            ztile = sb("ztile", [P, GW])

            c_in = sem("c_in")
            c_const = sem("c_const")
            c_ch = sem("c_ch")
            c_above = sem("c_above")
            c_mm = sem("c_mm")
            c_list = sem("c_list")
            c_far = sem("c_far")
            c_zero = sem("c_zero")
            c_z = sem("c_z")
            c_down = sem("c_down")

            with nc.Block() as block:
                @block.gpsimd
                def _(pool):
                    nc.gpsimd.iota(i400[:, :], [[1, NT]], 0, 0).then_inc(c_const, 1)
                    nc.gpsimd.iota(xi[:, :], [[1, 4]], 0, 4).then_inc(c_const, 1)
                    nc.gpsimd.memset(ident[:, :], 0.0).then_inc(c_const, 1)
                    nc.gpsimd.memset(zeros[:, :], 0.0).then_inc(c_const, 1)
                    nc.gpsimd.memset(onesb[:, :], 1.0).then_inc(c_const, 1)
                    nc.gpsimd.memset(zerob[:, :], 0.0).then_inc(c_const, 1)
                    nc.gpsimd.memset(ztile[:, :], 0.0).then_inc(c_z, 1)
                    pool.wait_ge(c_const, 3)
                    nc.gpsimd.affine_select(out=ident[:, :], in_=ident[:, :], compare_op=ALU.not_equal, fill=1.0,
                                            base=0, pattern=[[-1, P]], channel_multiplier=1)
                    nc.gpsimd.memset(idx[:, :, :], 0)
                    pool.wait_ge(c_down, 1)
                    nc.gpsimd.partition_all_reduce(down[:, 1:2], down[:, 0:1], P, RADD).then_inc(c_down, 1)

                @block.sync
                def _(sp):
                    sp.dma_start(dsts[:, :], dst[0:NPAD].rearrange("(p c) -> p c", c=NB)).then_inc(c_in, 16)
                    sp.dma_start(dstn[:, :], dst[1:NPAD + 1].rearrange("(p c) -> p c", c=NB)).then_inc(c_in, 16)
                    sp.wait_ge(c_z, 1)
                    sp.dma_start(part0[0], ztile[:, 0:D]).then_inc(c_zero, 16)
                    sp.dma_start(part1[0], ztile[:, :]).then_inc(c_zero, 16)
                    sp.dma_start(h1[NPAD:NPAD + P], ztile[:, 0:D]).then_inc(c_zero, 16)
                    sp.wait_ge(c_list, 1)
                    sp.dma_start(far_list[0].rearrange("(p j) -> p j", j=4), lists[:, 0, :]).then_inc(c_far, 16)
                    sp.dma_start(far_list[1].rearrange("(p j) -> p j", j=4), lists[:, 1, :]).then_inc(c_far, 16)
                    sp.wait_ge(c_far, 32)
                    sp.dma_start(ctl[0:1, 0:2, NB:NB + XT], far_list.rearrange("(o k) x -> o k x", o=1)).then_inc(c_far, 16)
                    sp.dma_start(farb[:, :], far_list[1:2, :].to_broadcast([P, XT])).then_inc(c_far, 16)
                    sp.wait_ge(c_far, 64)
                    sp.wait_ge(c_zero, 48)

                @block.tensor
                def _(pe):
                    pe.wait_ge(c_const, 6)
                    nc.tensor.matmul(ps[:, :], onesb[:, :], zerob[:, :], start=True, stop=False)

                    def body(i):
                        for j in range(8):
                            pe.wait_ge(c_above, 8 * i + j + 1)
                            nc.tensor.matmul(ps[:, :], onesb[:, :], above[:, j, :], start=False, stop=False).then_inc(c_mm, 1)
                    looped(pe, body, NB // 8)
                    nc.tensor.matmul(ps[:, :], onesb[:, :], zerob[:, :], start=False, stop=True).then_inc(c_mm, 1)

                @block.vector
                def _(dve):
                    count = [0]

                    def link(ins):
                        count[0] += 1
                        ins.then_inc(c_ch, 1)
                        dve.wait_ge(c_ch, count[0])

                    dve.wait_ge(c_const, 4)
                    dve.wait_ge(c_in, 32)
                    nc.vector.tensor_copy(t400[:, :], i400[:, :])
                    nc.vector.tensor_copy(h400[:, :], i400[:, :])
                    nc.vector.tensor_copy(iota_f[:, :], i400[:, 0:P])
                    nc.vector.tensor_copy(xf[:, :], xi[:, :])
                    nc.vector.memset(dloc[:, :], FAR)
                    link(nc.vector.tensor_scalar(bid[:, :], dsts[:, :], 7, None, ALU.arith_shift_right))
                    link(nc.vector.tensor_copy(bidf[:, :], bid[:, :]))
                    link(nc.vector.tensor_tensor(junk[:, :], dsts[:, :], dstn[:, :], ALU.is_gt))
                    nc.vector.tensor_reduce(down[:, 0:1], junk[:, :], AX.X, ALU.add).then_inc(c_down, 1)

                    def body(i):
                        for j in range(8):
                            past(dve, c_mm, 8 * (i - 1) + j + 1)
                            nc.vector.tensor_scalar(above[:, j, :], h400[:, :], bidf[:, bass.ds(8 * i + j, 1)], None,
                                                    ALU.is_gt).then_inc(c_above, 1)
                    looped(dve, body, NB // 8)
                    dve.wait_ge(c_mm, NB + 1)
                    link(nc.vector.tensor_copy(st[:, :], ps[:, :]))
                    link(nc.vector.tensor_tensor(n1[:, :], st[:, 1:NB + 1], st[:, 0:NB], ALU.subtract))
                    link(nc.vector.tensor_scalar(n1[:, :], n1[:, :], -1.0, 0.0, ALU.add, ALU.max))
                    link(nc.vector.tensor_copy(ni[:, :], n1[:, :]))
                    link(nc.vector.tensor_scalar(ni[:, :], ni[:, :], 7, None, ALU.arith_shift_right))
                    link(nc.vector.tensor_copy(nx[:, :], ni[:, :]))
                    link(nc.vector.tensor_tensor_scan(xend[:, :], nx[:, :], zeros[:, :], 0.0, ALU.add, ALU.add))
                    link(nc.vector.tensor_scalar(last[:, :], nx[:, :], 0.0, None, ALU.is_gt))
                    link(nc.vector.tensor_tensor(last[:, :], last[:, :], xend[:, :], ALU.mult))
                    link(nc.vector.tensor_tensor(shift[:, :], xend[:, :], nx[:, :], ALU.subtract))
                    link(nc.vector.tensor_scalar(shift[:, :], shift[:, :], -float(P), float(P), ALU.mult, ALU.add))
                    link(nc.vector.tensor_tensor(shift[:, :], shift[:, :], st[:, 0:NB], ALU.add))
                    for j in range(4):
                        link(nc.vector.tensor_scalar(junk[:, :], xend[:, :], xf[:, j:j + 1], 0.0, ALU.is_le, ALU.add,
                                                     accum_out=blkx[:, j:j + 1]))
                        link(nc.vector.scalar_tensor_tensor(junk[:, :], t400[:, 0:NB], blkx[:, j:j + 1], shift[:, :],
                                                            ALU.is_equal, ALU.mult, accum_out=sx[:, j:j + 1]))
                    link(nc.vector.tensor_scalar(valid[:, :], blkx[:, :], float(NB), None, ALU.is_lt))
                    link(nc.vector.tensor_scalar(sx2[:, :], xf[:, :], float(P), -float(E), ALU.mult, ALU.add))
                    link(nc.vector.tensor_tensor(sx[:, :], sx[:, :], sx2[:, :], ALU.add))
                    link(nc.vector.tensor_tensor(sx[:, :], sx[:, :], valid[:, :], ALU.mult))
                    link(nc.vector.tensor_scalar(sx[:, :], sx[:, :], float(E), None, ALU.add))
                    link(nc.vector.tensor_copy(lists[:, 0, :], sx[:, :]))
                    link(nc.vector.tensor_scalar(blkx[:, :], blkx[:, :], float(NB - 1), None, ALU.min))
                    nc.vector.tensor_copy(lists[:, 1, :], blkx[:, :]).then_inc(c_list, 1)
                    nc.vector.tensor_copy(ctl[0:1, 0, 0:NB], st[0:1, 0:NB])
                    nc.vector.tensor_copy(ctl[0:1, 1, 0:NB], t400[0:1, 0:NB])
                    nc.vector.tensor_copy(ctl[0:1, 2, 0:NB], last[0:1, :])
                    nc.vector.tensor_scalar(base[:, 0:NB], t400[:, 0:NB], float(P), None, ALU.mult)
                    link(nc.vector.tensor_scalar(ti[:, 0:1], xend[0:1, NB - 1:NB], float(NB + 7), None, ALU.add))
                    link(nc.vector.tensor_scalar(ti[:, 1:2], xend[0:1, NB - 1:NB], -1.0, 4.0, ALU.add, ALU.max))
                    link(nc.vector.tensor_scalar(ti[:, 2:3], xend[0:1, NB - 1:NB], -1.0, 8.0, ALU.add, ALU.max))
                    link(nc.vector.tensor_copy(ti2[:, :], ti[:, :]))
                    nc.vector.tensor_scalar(trips[:, 0:1], ti2[:, 0:1], 3, None, ALU.arith_shift_right)
                    nc.vector.tensor_scalar(trips[:, 1:2], ti2[:, 1:2], 2, None, ALU.arith_shift_right)
                    nc.vector.tensor_scalar(trips[:, 3:4], ti2[:, 2:3], 3, None, ALU.arith_shift_right)
                    dve.wait_ge(c_down, 2)
                    nc.vector.tensor_scalar(trips[:, 2:3], down[0:1, 1:2], 1.0, None, ALU.min)
                    dve.wait_ge(c_far, 64)
                    nc.vector.tensor_scalar(base[:, NB:NB + XT], farb[:, :], float(P), None, ALU.mult)
                    nc.vector.memset(same[:, 0:1], 0.0)
                    nc.vector.tensor_tensor(same[:, 1:XT], farb[:, 1:XT], farb[:, 0:XT - 1], ALU.is_equal)


        end_section()

        def unordered(eng):
            return eng.value_load(trips[0:1, 2:3], min_val=0, max_val=1)

        srcdst_s = dram("srcdst_s", [EPAD, 2], I32)
        edge_s = dram("edge_s", [EPAD, DE])
        edge_ts = dram("edge_ts", [DE, EPAD])
        with ExitStack() as ctx:
            sb = sb_in(ctx)
            CT = 56
            CC = CT * P
            pairs = sb("pairs", [P, NB, 2], I32)
            dcol = sb("dcol", [P, NB])
            rowi = sb("rowi", [P, CC], I32)
            rowf = sb("rowf", [P, CC])
            jnk = sb("jnk", [P, CC], BF16)
            jnk2 = sb("jnk2", [P, P], BF16)
            mark = sb("mark", [P, 1])
            below = sb("below", [P, NB])
            ties = sb("ties", [P, NB])
            place = sb("place", [P, NB])
            placei = sb("placei", [P, NB], I32)
            ltri = sb("ltri", [P, P])
            pi = sb("pi", [P, 1], I32)
            pf = sb("pf", [P, 1])
            pl1 = sb("pl1", [P, 1], I32)
            pr1 = sb("pr1", [P, 2], I32)
            er1 = sb("er1", [P, DE])
            et1 = sb("et1", [DE, P])
            psE = ctx.enter_context(nc.psum_tensor("psEs", [DE, P], F32))
            g_in = sem("g_in")
            g_row = sem("g_row")
            g_chunk = sem("g_chunk")
            g_ch = sem("g_ch")
            g_pi = sem("g_pi")
            g_er = sem("g_er")
            g_cp = sem("g_cp")
            g_sc = sem("g_sc")
            g_lr = sem("g_lr")
            g_tp = sem("g_tp")
            g_ev = sem("g_ev")
            g_st = sem("g_st")

            with nc.Block() as block:
                @block.sync
                def _(sp):
                    with sp.If(unordered(sp) == 1):
                        sp.dma_start(pairs[:, :, :], srcdst.rearrange("(c p) k -> p c k", p=P)).then_inc(g_in, 16)
                        for c in range(NB // CT):
                            past(sp, g_chunk, c)
                            sp.dma_start(rowi[:, :], dst[c * CC:(c + 1) * CC].rearrange("(o n) -> o n", o=1)
                                         .to_broadcast([P, CC])).then_inc(g_row, 16)

                @block.gpsimd
                def _(pool):
                    with pool.If(unordered(pool) == 1):
                        nc.gpsimd.iota(pi[:, :], [[0, 1]], 0, 1).then_inc(g_pi, 1)

                @block.vector
                def _(dve):
                    with dve.If(unordered(dve) == 1):
                        done = [0]

                        def link(ins):
                            done[0] += 1
                            ins.then_inc(g_ch, 1)
                            dve.wait_ge(g_ch, done[0])

                        dve.wait_ge(g_pi, 1)
                        link(nc.vector.tensor_copy(pf[:, :], pi[:, :]))
                        link(nc.vector.tensor_scalar(ltri[:, :], iota_f[:, :], pf[:, :], None, ALU.is_lt))
                        dve.wait_ge(g_in, 16)
                        link(nc.vector.tensor_copy(dcol[:, :], pairs[:, :, 1]))
                        link(nc.vector.memset(place[:, :], 0.0))

                        def compare(t):
                            return nc.vector.tensor_scalar(jnk[:, :], rowf[:, :], dcol[:, bass.ds(t, 1)], 0.0, ALU.is_lt,
                                                           ALU.add, accum_out=below[:, bass.ds(t, 1)])
                        for c in range(NB // CT):
                            t0 = c * CT
                            dve.wait_ge(g_row, 16 * (c + 1))
                            link(nc.vector.tensor_copy(rowf[:, :], rowi[:, :]))
                            if c > 0:
                                with dve.Fori(0, t0) as t:
                                    compare(t).then_inc(g_ch, 1)
                                    dve.wait_ge(g_ch, done[0] + t + 1)
                                done[0] += t0
                            with dve.Fori(0, CT) as i:
                                tile = rowf[:, bass.ds(P * i, P)]
                                compare(i + t0).then_inc(g_ch, 1)
                                nc.vector.scalar_tensor_tensor(jnk2[:, :], tile, dcol[:, bass.ds(i + t0, 1)], ltri[:, :],
                                                               ALU.is_equal, ALU.mult,
                                                               accum_out=ties[:, bass.ds(i + t0, 1)]).then_inc(g_ch, 1)
                                dve.wait_ge(g_ch, done[0] + 3 * i + 2)
                                nc.vector.tensor_scalar(tile, tile, -0.5, None, ALU.add).then_inc(g_ch, 1)
                                dve.wait_ge(g_ch, done[0] + 3 * i + 3)
                            done[0] += 3 * CT
                            if t0 + CT < NB:
                                with dve.Fori(0, NB - CT - t0) as t:
                                    compare(t + (t0 + CT)).then_inc(g_ch, 1)
                                    dve.wait_ge(g_ch, done[0] + t + 1)
                                done[0] += NB - CT - t0
                            link(nc.vector.tensor_tensor(place[:, :], place[:, :], below[:, :], ALU.add))
                            nc.vector.memset(mark[:, :], 0.0).then_inc(g_chunk, 1)
                        link(nc.vector.tensor_tensor(place[:, :], place[:, :], ties[:, :], ALU.add))
                        link(nc.vector.tensor_copy(placei[:, :], place[:, :]))

            with nc.Block() as block:
                @block.gpsimd
                def _(pool):
                    with pool.If(unordered(pool) == 1):
                        with pool.Fori(0, NB) as i:
                            pool.dma_start(er1[:, :], edge_rows[bass.ds(P * i, P), :]).then_inc(g_er, 16)
                            nc.gpsimd.tensor_copy(pl1[:, :], placei[:, bass.ds(i, 1)]).then_inc(g_cp, 1)
                            nc.gpsimd.tensor_copy(pr1[:, :], pairs[:, bass.ds(i, 1), :].rearrange("p o k -> p (o k)")).then_inc(g_cp, 1)
                            held(pool, g_er, 16 * i + 16)
                            held(pool, g_cp, 2 * i + 2)
                            nc.gpsimd.indirect_dma_start(
                                out=srcdst_s[:, :], out_offset=bass.IndirectOffsetOnAxis(ap=pl1[:, 0:1], axis=0),
                                in_=pr1[:, :], in_offset=None).then_inc(g_sc, 16)
                            nc.gpsimd.indirect_dma_start(
                                out=edge_s[:, :], out_offset=bass.IndirectOffsetOnAxis(ap=pl1[:, 0:1], axis=0),
                                in_=er1[:, :], in_offset=None).then_inc(g_sc, 16)
                            held(pool, g_sc, 32 * i + 32)
                        pool.sem_inc(passed, 1)

            with nc.Block() as block:
                @block.sync
                def _(sp):
                    with sp.If(unordered(sp) == 1):
                        def body(i):
                            held(sp, g_st, 16 * i)
                            sp.dma_start(er1[:, :], edge_s[bass.ds(P * i, P), :]).then_inc(g_lr, 16)
                            held(sp, g_ev, i + 1)
                            sp.dma_start(edge_ts[:, bass.ds(P * i, P)], et1[:, :]).then_inc(g_st, 16)
                        looped(sp, body, NB)
                        sp.wait_ge(g_st, 16 * NB)
                        sp.sem_inc(passed, 1)

                @block.tensor
                def _(pe):
                    with pe.If(unordered(pe) == 1):
                        with pe.Fori(0, NB) as i:
                            held(pe, g_lr, 16 * i + 16)
                            nc.tensor.transpose(psE[:, :], er1[:, :], ident[:, :]).then_inc(g_tp, 1)
                        pe.sem_inc(passed, 1)

                @block.vector
                def _(dve):
                    with dve.If(unordered(dve) == 1):
                        with dve.Fori(0, NB) as i:
                            dve.wait_ge(g_tp, i + 1)
                            nc.vector.tensor_copy(et1[:, :], psE[:, :]).then_inc(g_ev, 1)
                        dve.sem_inc(passed, 1)


        end_section()

        s12 = outer.enter_context(nc.sbuf_tensor("s12", [P, 2, NB], F32))
        with ExitStack() as ctx:
            sb = sb_in(ctx)
            xb = [sb(f"xb{q}", [P, 4, D]) for q in range(2)]
            hb = [sb(f"hb{q}", [P, 4, D]) for q in range(2)]
            hT = [sb(f"hT{q}", [P, 4, P]) for q in range(2)]
            pj = [sb(f"pj{q}", [P, 4, DP]) for q in range(2)]
            stat = [sb(f"stat{q}", [P, 4, 6]) for q in range(2)]
            mv = [sb(f"mv{q}", [P, 4, 2]) for q in range(2)]
            std = [sb(f"std{q}", [P, 4]) for q in range(2)]
            rstd = [sb(f"rstd{q}", [P, 4]) for q in range(2)]
            nmr = [sb(f"nmr{q}", [P, 4]) for q in range(2)]
            Wsb = sb("Wsb", [P, D])
            WT = sb("WT", [P, D])
            asb = sb("asb", [P, 2])
            Wa = sb("Wa", [P, 2])
            eps = sb("eps", [P, 1])
            sT = sb("sT", [98, 4, P])
            psT = [ctx.enter_context(nc.psum_tensor(f"psT{q}", [P, 4, P], F32)) for q in range(2)]
            psW = [ctx.enter_context(nc.psum_tensor(f"psW{q}", [P, 4, P], F32)) for q in range(2)]
            psS = [ctx.enter_context(nc.psum_tensor(f"psS{q}", [P, 4, 2], F32)) for q in range(2)]
            psE = [ctx.enter_context(nc.psum_tensor(f"psE{q}", [P, 4, P], F32)) for q in range(2)]
            w_in = sem("a_w_in")
            x_in = [sem(f"a_x_in{q}") for q in range(2)]
            p_out = [sem(f"a_p_out{q}") for q in range(2)]
            wprep = sem("a_wprep")
            wt_ps = sem("a_wt_ps")
            stats = sem("a_stats")
            aggr = sem("a_aggr")
            stdev = sem("a_stdev")
            recip = sem("a_recip")
            shifted = sem("a_shifted")
            normed = sem("a_normed")
            turned = sem("a_turned")
            ht_ready = sem("a_ht_ready")
            projected = sem("a_projected")
            evacuated = sem("a_evacuated")
            s_turned = sem("a_s_turned")
            s_copied = sem("a_s_copied")
            s_stored = sem("a_s_stored")
            x_g = x.rearrange("(g j p) d -> g p j d", j=4, p=P)
            proj_g = h_proj.rearrange("(g j p) d -> g p j d", j=4, p=P)
            ITER = NB // 8

            with nc.Block() as block:
                @block.sync
                def _(sp):
                    sp.dma_start(Wsb[:, :], W).then_inc(w_in, 16)
                    sp.dma_start(asb[:, :], a).then_inc(w_in, 16)

                    def emit(i, q, live):
                        g, _, _ = before(i, q, 0)
                        g3, q3, _ = before(i, q, 3)
                        if live(0):
                            past(sp, normed, g - 1)
                            sp.dma_start(xb[q][:, :, :], x_g[bass.ds(g, 1)].rearrange("g p j d -> (g p) j d")).then_inc(x_in[q], 16)
                        if live(3):
                            past(sp, evacuated, g3 + 1)
                            sp.dma_start(proj_g[bass.ds(g3, 1)].rearrange("g p j d -> (g p) j d"), pj[q3][:, :, :]).then_inc(p_out[q3], 16)
                    pipelined(sp, emit, ITER, 2)
                    for q in range(2):
                        sp.wait_ge(p_out[q], 16 * ITER)
                    sp.wait_ge(s_copied, 4)
                    sp.dma_start(s_dst.rearrange("(t c p) o -> c t (p o)", t=4, p=P), sT[:, :, :]).then_inc(s_stored, 16)
                    sp.wait_ge(s_stored, 16)

                @block.scalar
                def _(act):
                    act.wait_ge(wt_ps, 1)
                    nc.scalar.copy(WT[:, :], psE[0][:, 0, :]).then_inc(wprep, 1)
                    act.wait_ge(wt_ps, 2)
                    nc.scalar.copy(Wa[:, :], psE[1][:, 0, 0:2]).then_inc(wprep, 1)

                    def emit(i, q, live):
                        g, _, _ = before(i, q, 0)
                        g1, q1, _ = before(i, q, 1)
                        if live(0):
                            act.wait_ge(aggr, g + 1)
                            past(act, recip, g - 1)
                            nc.scalar.activation(std[q][:, :], mv[q][:, :, 1], ACT.Sqrt, bias=eps[:, :]).then_inc(stdev, 1)
                        if live(1):
                            act.wait_ge(turned, g1 + 1)
                            past(act, projected, g1 - 1)
                            nc.scalar.copy(hT[q1][:, :, :], psT[q1][:, :, :]).then_inc(ht_ready, 1)
                        if live(0):
                            act.wait_ge(shifted, g + 1)
                            past(act, turned, g - 1)
                            for j in range(4):
                                ins = nc.scalar.activation(hb[q][:, j, :], xb[q][:, j, :], ACT.Relu, bias=nmr[q][:, j:j + 1],
                                                           scale=rstd[q][:, j:j + 1])
                            ins.then_inc(normed, 1)
                    pipelined(act, emit, ITER, 2)

                @block.vector
                def _(dve):
                    nc.vector.memset(eps[:, :], EPS)

                    def emit(i, q, live):
                        g, _, turn = before(i, q, 0)
                        g2, q2, turn2 = before(i, q, 2)
                        if live(0):
                            dve.wait_ge(x_in[q], 16 * turn)
                            past(dve, aggr, g - 1)
                            for j in range(4):
                                ins = nc.vector.bn_stats(stat[q][:, j, :], xb[q][:, j, :])
                            ins.then_inc(stats, 1)
                            past(dve, shifted, g - 1)
                            held(dve, stats, g + 1)
                            for j in range(4):
                                ins = nc.vector.bn_aggr(mv[q][:, j, :], stat[q][:, j, :])
                            ins.then_inc(aggr, 1)
                        if live(2):
                            dve.wait_ge(projected, g2 + 1)
                            past(dve, p_out[q2], 16 * (turn2 - 1))
                            nc.vector.tensor_copy(s12[:, :, bass.ds(4 * g2, 4)], psS[q2][:, :, :].rearrange("p j k -> p k j"))
                            nc.vector.tensor_copy(pj[q2][:, :, D:DP], psS[q2][:, :, :])
                            nc.vector.tensor_copy(pj[q2][:, :, 0:D], psW[q2][:, :, :]).then_inc(evacuated, 1)
                        if live(0):
                            dve.wait_ge(stdev, g + 1)
                            past(dve, normed, g - 1)
                            nc.vector.reciprocal(rstd[q][:, :], std[q][:, :]).then_inc(recip, 1)
                            dve.wait_ge(recip, g + 1)
                            nc.vector.scalar_tensor_tensor(nmr[q][:, :], mv[q][:, :, 0], -1.0, rstd[q][:, :], ALU.mult,
                                                           ALU.mult).then_inc(shifted, 1)
                    pipelined(dve, emit, ITER, 2)
                    dve.wait_ge(s_turned, 4)
                    for t in range(4):
                        nc.vector.tensor_copy(sT[:, t, :], psE[1][0:98, t, :]).then_inc(s_copied, 1)

                @block.tensor
                def _(pe):
                    pe.wait_ge(w_in, 32)
                    nc.tensor.transpose(psE[0][:, 0, :], Wsb[:, :], ident[:, :]).then_inc(wt_ps, 1)
                    pe.wait_ge(wprep, 1)
                    nc.tensor.matmul(psE[1][:, 0, 0:2], WT[:, :], asb[:, :], start=True, stop=True).then_inc(wt_ps, 1)
                    pe.wait_ge(wprep, 2)

                    def emit(i, q, live):
                        g, _, _ = before(i, q, 0)
                        g1, q1, _ = before(i, q, 1)
                        if live(1):
                            pe.wait_ge(ht_ready, g1 + 1)
                            past(pe, evacuated, g1 - 1)
                            for j in range(4):
                                nc.tensor.matmul(psW[q1][:, j, :], hT[q1][:, j, :], Wsb[:, :], start=True, stop=True)
                                ins = nc.tensor.matmul(psS[q1][:, j, :], hT[q1][:, j, :], Wa[:, :], start=True, stop=True)
                            ins.then_inc(projected, 1)
                        if live(0):
                            pe.wait_ge(normed, g + 1)
                            past(pe, ht_ready, g - 1)
                            for j in range(4):
                                ins = nc.tensor.transpose(psT[q][:, j, :], hb[q][:, j, :], ident[:, :])
                            ins.then_inc(turned, 1)
                    pipelined(pe, emit, ITER, 2)
                    pe.wait_ge(evacuated, 2 * ITER)
                    for t in range(4):
                        nc.tensor.transpose(psE[1][0:98, t, :], s12[:, 1, 98 * t:98 * t + 98],
                                            ident[:, :]).then_inc(s_turned, 1)

        end_section()

        with ExitStack() as ctx:
            sb = sb_in(ctx)
            K = 4
            idx4 = [sb(f"idx4{q}", [P, K, 2], I32) for q in range(2)]
            rows = [sb(f"rows{q}", [P, K, DP]) for q in range(2)]
            sd = [sb(f"sd{q}", [P, K, P]) for q in range(2)]
            jnk = [sb(f"jnks{q}", [P, K, P]) for q in range(2)]
            s1e = sb("s1e", [P, S])
            s2e = sb("s2e", [P, S])
            ok = sb("ok", [P, S])
            tmp = sb("tmp", [P, S])
            sm = sb("sm", [P, 6])
            e_idx = [sem(f"e_idx{q}") for q in range(2)]
            e_sd = [sem(f"e_sd{q}") for q in range(2)]
            e_got = [sem(f"e_got{q}") for q in range(2)]
            e_st = [sem(f"e_st{q}") for q in range(2)]
            e_init = sem("e_init")
            e_kept = sem("e_kept")
            e_sel = sem("e_sel")
            e_s1 = sem("e_s1")
            e_ch = sem("e_ch")
            e_red = sem("e_red")
            e_exp = sem("e_exp")

            with nc.Block() as block:
                def groups(eng):
                    return eng.value_load(trips[0:1, 0:1], min_val=NB // 8, max_val=S // 8)

                @block.sync
                def _(sp):
                    def emit(i, q, live, srcdst):
                        g, _, turn = before(i, q, 0)
                        g2, q2, turn2 = before(i, q, 2)
                        if live(0):
                            for k in range(K):
                                start = sp.value_load(ctl[0:1, 0, bass.ds(K * g + k, 1)], min_val=0, max_val=E)
                                if k == 0:
                                    held(sp, e_kept, g - 1)
                                    held(sp, e_got[q], 64 * (turn - 1))
                                sp.dma_start(idx4[q][:, k, :], srcdst[bass.ds(start, P), :]).then_inc(e_idx[q], 16)
                        if live(2):
                            held(sp, e_got[q2], 64 * turn2)
                            sp.dma_start(edge_proj[bass.ds(K * g2, K)].rearrange("s p d -> p s d"),
                                         rows[q2][:, :, 0:D]).then_inc(e_st[q2], 16)
                    n = groups(sp)
                    with sp.If(unordered(sp) == 0):
                        pipelined(sp, lambda i, q, live: emit(i, q, live, srcdst), n, 2)
                        sp.sem_inc(passed, 1)
                    with sp.Else():
                        pipelined(sp, lambda i, q, live: emit(i, q, live, srcdst_s), n, 2)
                        sp.sem_inc(passed, 1)
                    for q in range(2):
                        held(sp, e_st[q], 16 * n)

                @block.scalar
                def _(act):
                    def emit(i, q, live):
                        g, _, _ = before(i, q, 0)
                        if live(0):
                            for k in range(K):
                                blk = act.value_load(ctl[0:1, 1, bass.ds(K * g + k, 1)], min_val=0, max_val=NB - 1)
                                if k == 0:
                                    past(act, e_sel, g - 1)
                                act.dma_start(sd[q][:, k, :], s_dst.rearrange("(b p) o -> b (p o)", p=P)[bass.ds(blk, 1), :]
                                              .to_broadcast([P, P])).then_inc(e_sd[q], 16)
                    pipelined(act, emit, groups(act), 2)
                    act.wait_ge(e_red, 2)
                    nc.scalar.activation(wgt[:, :], tmp[:, :], ACT.Exp, bias=sm[:, 2:3], accum_out=sm[:, 3:4]).then_inc(e_exp, 1)

                @block.gpsimd
                def _(pool):
                    def emit(i, q, live):
                        g, _, turn = before(i, q, 0)
                        if live(0):
                            past(pool, e_s1, g - 1)
                            past(pool, e_st[q], 16 * (turn - 1))
                            held(pool, e_idx[q], 64 * turn)
                            for k in range(K):
                                nc.gpsimd.indirect_dma_start(
                                    out=rows[q][:, k, :], out_offset=None, in_=h_proj[:, :],
                                    in_offset=bass.IndirectOffsetOnAxis(ap=idx4[q][:, k, 0:1], axis=0)).then_inc(e_got[q], 16)
                    pipelined(pool, emit, groups(pool), 2)
                    pool.wait_ge(e_ch, 7)
                    nc.gpsimd.partition_all_reduce(sm[:, 1:2], sm[:, 0:1], P, RMAX).then_inc(e_red, 1)
                    pool.wait_ge(e_exp, 1)
                    nc.gpsimd.partition_all_reduce(sm[:, 4:5], sm[:, 3:4], P, RADD).then_inc(e_red, 1)

                @block.vector
                def _(dve):
                    nc.vector.memset(s1e[:, :], 0.0).then_inc(e_init, 1)
                    nc.vector.memset(s2e[:, :], 0.0).then_inc(e_init, 1)
                    dve.wait_ge(e_init, 2)

                    def emit(i, q, live):
                        g, _, turn = before(i, q, 0)
                        g2, q2, turn2 = before(i, q, 2)
                        if live(2):
                            dve.wait_ge(e_got[q2], 64 * turn2)
                            nc.vector.tensor_copy(s1e[:, bass.ds(K * g2, K)], rows[q2][:, :, D]).then_inc(e_s1, 1)
                        if live(0):
                            dve.wait_ge(e_idx[q], 64 * turn)
                            nc.vector.tensor_copy(idx[:, bass.ds(K * g, K), :], idx4[q][:, :, :])
                            nc.vector.tensor_tensor(dloc[:, bass.ds(K * g, K)], idx4[q][:, :, 1], base[:, bass.ds(K * g, K)],
                                                    ALU.subtract).then_inc(e_kept, 1)
                            dve.wait_ge(e_kept, g + 1)
                            dve.wait_ge(e_sd[q], 64 * turn)
                            for k in range(K):
                                ins = nc.vector.scalar_tensor_tensor(jnk[q][:, k, :], iota_f[:, :], dloc[:, bass.ds(K * g + k, 1)],
                                                                     sd[q][:, k, :], ALU.is_equal, ALU.mult,
                                                                     accum_out=s2e[:, bass.ds(K * g + k, 1)])
                            ins.then_inc(e_sel, 1)
                    n = groups(dve)
                    pipelined(dve, emit, n, 2)
                    dve.wait_ge(e_s1, 2 * n)
                    dve.wait_ge(e_sel, 2 * n)
                    count = [0]

                    def link(ins):
                        count[0] += 1
                        ins.then_inc(e_ch, 1)
                        dve.wait_ge(e_ch, count[0])
                    link(nc.vector.tensor_tensor(tmp[:, :], s1e[:, :], s2e[:, :], ALU.add))
                    link(nc.vector.scalar_tensor_tensor(s1e[:, :], tmp[:, :], ALPHA, tmp[:, :], ALU.mult, ALU.max))
                    link(nc.vector.tensor_scalar(ok[:, :], dloc[:, :], float(P), None, ALU.is_lt))
                    link(nc.vector.tensor_tensor(s1e[:, :], s1e[:, :], ok[:, :], ALU.mult))
                    link(nc.vector.tensor_scalar(ok[:, :], ok[:, :], -1.0, 3.0e38, ALU.add, ALU.mult))
                    link(nc.vector.tensor_tensor(tmp[:, :], s1e[:, :], ok[:, :], ALU.add))
                    link(nc.vector.tensor_reduce(sm[:, 0:1], tmp[:, :], AX.X, ALU.max))
                    dve.wait_ge(e_red, 1)
                    nc.vector.tensor_scalar(sm[:, 2:3], sm[:, 1:2], -1.0, None, ALU.mult).then_inc(e_red, 1)
                    dve.wait_ge(e_red, 3)
                    link(nc.vector.reciprocal(sm[:, 5:6], sm[:, 4:5]))
                    nc.vector.tensor_scalar(wgt[:, :], wgt[:, :], sm[:, 5:6], None, ALU.mult)

        end_section()

        for far in (True, False):
            with ExitStack() as ctx:
                sb = sb_in(ctx)
                t = "f" if far else "m"
                step0 = NB if far else 0
                K = 4
                rows = [sb(f"rows4{t}{q}", [P, K, D]) for q in range(2)]
                oh = [sb(f"oh{t}{q}", [P, K, P]) for q in range(2)]
                psA = [ctx.enter_context(nc.psum_tensor(f"psA{t}{q}", [P, K, D], F32)) for q in range(2)]
                l_rows = [sem(f"l_rows{t}{q}") for q in range(2)]
                l_oh = sem(f"l_oh{t}")
                l_mm = sem(f"l_mm{t}")
                l_st = [sem(f"l_st{t}{q}") for q in range(2)]
                if far:
                    acc = [sb(f"acc{q}", [P, K, D]) for q in range(2)]
                    l_sum = sem("l_sum")
                    l_init = sem("l_init")
                else:
                    x4 = [sb(f"x4{q}", [P, K, D]) for q in range(2)]
                    part = [sb(f"partm{q}", [P, K, D]) for q in range(2)]
                    xo = [sb(f"xo{q}", [P, K, D]) for q in range(2)]
                    ho = [sb(f"ho{q}", [P, K, D]) for q in range(2)]
                    betaB = sb("betaB", [P, D])
                    stat = [sb(f"stat4{q}", [P, K, 6]) for q in range(2)]
                    mv = [sb(f"mv4{q}", [P, K, 2]) for q in range(2)]
                    std = [sb(f"std4{q}", [P, K]) for q in range(2)]
                    rstd = [sb(f"rstd4{q}", [P, K]) for q in range(2)]
                    nmr = [sb(f"nmr4{q}", [P, K]) for q in range(2)]
                    eps = sb("eps4", [P, 1])
                    l_x = [sem(f"l_x{q}") for q in range(2)]
                    l_part = [sem(f"l_part{q}") for q in range(2)]
                    l_ho = [sem(f"l_ho{q}") for q in range(2)]
                    l_c = sem("l_c")
                    l_new = sem("l_new")
                    l_stat = sem("l_stat")
                    l_aggr = sem("l_aggr")
                    l_std = sem("l_std")
                    l_rec = sem("l_rec")
                    l_shift = sem("l_shift")
                    l_h = sem("l_h")
                    x_g = x.rearrange("(g j p) d -> g p j d", j=K, p=P)
                    x1_g = x1b.rearrange("(g j p) d -> g p j d", j=K, p=P)
                    h1_g = h1[0:NPAD].rearrange("(g j p) d -> g p j d", j=K, p=P)

                with nc.Block() as block:
                    def trip(eng):
                        return eng.value_load(trips[0:1, 3:4], min_val=1, max_val=NX // 8 - 1) + 1 if far else NB // 8

                    def attention(dve, i, q):
                        g, _, _ = before(i, q, 0)
                        past(dve, l_mm, g - 1)
                        for k in range(K):
                            s = bass.ds(K * g + (k + step0), 1)
                            ins = nc.vector.tensor_scalar(oh[q][:, k, :], iota_f[:, :], dloc[:, s], wgt[:, s], ALU.is_equal,
                                                          ALU.mult)
                        ins.then_inc(l_oh, 1)

                    def load_rows(sp, i, q):
                        g, _, _ = before(i, q, 0)
                        held(sp, l_mm, g - 1)
                        sp.dma_start(rows[q][:, :, :], edge_proj[bass.ds(K * g + step0, K)].rearrange("s p d -> p s d")).then_inc(l_rows[q], 16)

                    if far:
                        @block.sync
                        def _(sp):
                            def emit(i, q, live):
                                g1, q1, _ = before(i, q, 1)
                                if live(0):
                                    load_rows(sp, i, q)
                                if live(1):
                                    held(sp, l_sum, K * g1 + K)
                                    sp.dma_start(part0[bass.ds(K * g1 + 1, K)].rearrange("x p d -> p x d"), acc[q1][:, :, :]).then_inc(l_st[q1], 16)
                            n = trip(sp)
                            pipelined(sp, emit, n)
                            for q in range(2):
                                held(sp, l_st[q], 16 * n)

                        @block.tensor
                        def _(pe):
                            def emit(i, q, live):
                                g, _, turn = before(i, q, 0)
                                if live(0):
                                    pe.wait_ge(l_oh, g + 1)
                                    pe.wait_ge(l_rows[q], 16 * turn)
                                    past(pe, l_sum, K * (g - 1))
                                    for k in range(K):
                                        ins = nc.tensor.matmul(psA[q][:, k, :], oh[q][:, k, :], rows[q][:, k, :], start=True, stop=True)
                                    ins.then_inc(l_mm, 1)
                            pipelined(pe, emit, trip(pe))

                        @block.vector
                        def _(dve):
                            nc.vector.memset(acc[1][:, K - 1, :], 0.0).then_inc(l_init, 1)
                            dve.wait_ge(l_init, 1)

                            def emit(i, q, live):
                                g1, q1, turn1 = before(i, q, 1)
                                if live(0):
                                    attention(dve, i, q)
                                if live(1):
                                    dve.wait_ge(l_mm, g1 + 1)
                                    past(dve, l_st[q1], 16 * (turn1 - 1))
                                    for k in range(K):
                                        forerunner = acc[q1][:, k - 1, :] if k else acc[1 - q1][:, K - 1, :]
                                        past(dve, l_sum, K * g1 + k)
                                        nc.vector.scalar_tensor_tensor(acc[q1][:, k, :], forerunner,
                                                                       same[:, bass.ds(K * g1 + k, 1)], psA[q1][:, k, :],
                                                                       ALU.mult, ALU.add).then_inc(l_sum, 1)
                            pipelined(dve, emit, trip(dve))
                    else:
                        @block.sync
                        def _(sp):
                            sp.dma_start(betaB[:, :], beta.rearrange("(o d) -> o d", o=1).to_broadcast([P, D])).then_inc(l_c, 16)

                            def emit(i, q, live):
                                g, _, _ = before(i, q, 0)
                                if live(0):
                                    load_rows(sp, i, q)
                                    sp.dma_start(x4[q][:, :, :], x_g[bass.ds(g, 1)].rearrange("g p j d -> (g p) j d")).then_inc(l_x[q], 16)
                                    for k in range(K):
                                        slot = sp.value_load(ctl[0:1, 2, bass.ds(K * g + k, 1)], min_val=0, max_val=NX)
                                        sp.dma_start(part[q][:, k, :], part0[bass.ds(slot, 1)].rearrange("x p d -> (x p) d")).then_inc(l_part[q], 16)
                            pipelined(sp, emit, NB // 8, 2)

                        @block.tensor
                        def _(pe):
                            def emit(i, q, live):
                                g, _, turn = before(i, q, 0)
                                if live(0):
                                    pe.wait_ge(l_oh, g + 1)
                                    pe.wait_ge(l_rows[q], 16 * turn)
                                    pe.wait_ge(l_x[q], 16 * turn)
                                    pe.wait_ge(l_part[q], 64 * turn)
                                    past(pe, l_h, g - 1)
                                    for k in range(K):
                                        nc.tensor.matmul(psA[q][:, k, :], oh[q][:, k, :], rows[q][:, k, :], start=True, stop=False)
                                        nc.tensor.matmul(psA[q][:, k, :], ident[:, :], part[q][:, k, :], start=False, stop=False)
                                        ins = nc.tensor.matmul(psA[q][:, k, :], ident[:, :], x4[q][:, k, :], start=False, stop=True)
                                    ins.then_inc(l_mm, 1)
                            pipelined(pe, emit, NB // 8, 2)

                        @block.gpsimd
                        def _(pool):
                            def emit(i, q, live):
                                g2, q2, _ = before(i, q, 2)
                                if live(2):
                                    held(pool, l_new, g2 + 1)
                                    pool.dma_start(x1_g[bass.ds(g2, 1)].rearrange("g p j d -> (g p) j d"), xo[q2][:, :, :]).then_inc(l_st[q2], 16)
                                    held(pool, l_h, g2 + 1)
                                    pool.dma_start(h1_g[bass.ds(g2, 1)].rearrange("g p j d -> (g p) j d"), ho[q2][:, :, :]).then_inc(l_ho[q2], 16)
                            pipelined(pool, emit, NB // 8, 2)
                            for q in range(2):
                                pool.wait_ge(l_st[q], 16 * (NB // 8))
                                pool.wait_ge(l_ho[q], 16 * (NB // 8))

                        @block.scalar
                        def _(act):
                            def emit(i, q, live):
                                g1, q1, _ = before(i, q, 1)
                                g2, q2, turn2 = before(i, q, 2)
                                if live(2):
                                    act.wait_ge(l_shift, g2 + 1)
                                    past(act, l_ho[q2], 16 * (turn2 - 1))
                                    for k in range(K):
                                        ins = nc.scalar.activation(ho[q2][:, k, :], psA[q2][:, k, :], ACT.Relu,
                                                                   bias=nmr[q2][:, k:k + 1], scale=rstd[q2][:, k:k + 1])
                                    ins.then_inc(l_h, 1)
                                if live(1):
                                    act.wait_ge(l_aggr, g1 + 1)
                                    past(act, l_rec, g1 - 1)
                                    nc.scalar.activation(std[q1][:, :], mv[q1][:, :, 1], ACT.Sqrt, bias=eps[:, :]).then_inc(l_std, 1)
                            pipelined(act, emit, NB // 8, 2)

                        @block.vector
                        def _(dve):
                            nc.vector.memset(eps[:, :], EPS)
                            dve.wait_ge(l_c, 16)

                            def emit(i, q, live):
                                g1, q1, turn1 = before(i, q, 1)
                                g2, q2, _ = before(i, q, 2)
                                if live(2):
                                    dve.wait_ge(l_std, g2 + 1)
                                    past(dve, l_h, g2 - 1)
                                    nc.vector.reciprocal(rstd[q2][:, :], std[q2][:, :]).then_inc(l_rec, 1)
                                    dve.wait_ge(l_rec, g2 + 1)
                                    nc.vector.scalar_tensor_tensor(nmr[q2][:, :], mv[q2][:, :, 0], -1.0, rstd[q2][:, :], ALU.mult,
                                                                   ALU.mult).then_inc(l_shift, 1)
                                if live(0):
                                    attention(dve, i, q)
                                if live(1):
                                    dve.wait_ge(l_mm, g1 + 1)
                                    past(dve, l_aggr, g1 - 1)
                                    for k in range(K):
                                        ins = nc.vector.bn_stats(stat[q1][:, k, :], psA[q1][:, k, :])
                                    ins.then_inc(l_stat, 1)
                                    past(dve, l_st[q1], 16 * (turn1 - 1))
                                    nc.vector.tensor_tensor(xo[q1][:, :, :], psA[q1][:, :, :],
                                                            betaB[:, :].rearrange("p (o d) -> p o d", o=1).to_broadcast([P, K, D]),
                                                            ALU.add).then_inc(l_new, 1)
                                    past(dve, l_shift, g1 - 1)
                                    held(dve, l_stat, g1 + 1)
                                    for k in range(K):
                                        ins = nc.vector.bn_aggr(mv[q1][:, k, :], stat[q1][:, k, :])
                                    ins.then_inc(l_aggr, 1)
                            pipelined(dve, emit, NB // 8, 2)
            end_section()

        weights = ExitStack()
        with weights:
            sb = sb_in(weights)
            W1s = sb("W1s", [P, 2, HID])
            W1e = sb("W1e", [DE + 1, HID])
            W2s = sb("W2s", [P, 2, D])
            U1s = sb("U1s", [P, 2, HID])
            U2s = sb("U2s", [P, 2, D])
            b2B = sb("b2B", [P, D])
            b3c = sb("b3c", [P, 2])
            b4B = sb("b4B", [P, D])
            gammaB = sb("gammaB", [P, D])
            ones = sb("ones", [P, 2])
            half = sb("half", [P, 2])
            m_w = outer.enter_context(nc.semaphore("m_w"))
            idx5 = [sb(f"idx5{q}", [P, 2, 2], I32) for q in range(2)]
            got = [sb(f"got5{q}", [P, 2, 2, D]) for q in range(2)]
            ef = [sb(f"ef{q}", [DE + 1, 2, P]) for q in range(2)]
            oh = [sb(f"oh5{q}", [P, 2, P]) for q in range(2)]
            gT = [sb(f"gT{q}", [P, 2, 2, P]) for q in range(2)]
            G = [sb(f"G{q}", [P, 2, HID]) for q in range(2)]
            acc4 = sb("acc4", [P, 4, GW])

            for far in (True, False):
                with ExitStack() as ctx:
                    sb = sb_in(ctx)
                    t = "f" if far else "m"
                    step0 = NB if far else 0
                    ITER = NB // 4
                    peel = 1 if far else 3

                    def pb(name, shape, ctx=ctx, t=t):
                        return ctx.enter_context(nc.psum_tensor(f"{name}{t}", shape, F32))
                    psT = pb("psT5", [P, 2, 2, P])
                    psH = [pb(f"psH{k}", [P, HID]) for k in range(2)]
                    psG = [pb(f"psG{k}", [P, HID + 2]) for k in range(2)]

                    def m(name, t=t):
                        return sem(f"m_{name}{t}")
                    m_idx, m_oh, m_turn, m_gT = m("idx"), m("oh"), m("turn"), m("gT")
                    m_hid, m_gelu, m_sum, m_sumd = m("hid"), m("gelu"), m("sum"), m("sumd")
                    m_got = [m(f"got{q}") for q in range(2)]
                    m_ef = [m(f"ef{q}") for q in range(2)]
                    m_st = [m(f"st{q}") for q in range(2)]
                    m_init = m("init")
                    if not far:
                        hb = [sb(f"hb5{q}", [P, 2, D]) for q in range(2)]
                        h4 = [sb(f"h4{q}", [P, 2, D]) for q in range(2)]
                        xb5 = [sb(f"xb5{q}", [P, 2, D]) for q in range(2)]
                        part = [sb(f"part5{q}", [P, 2, GW]) for q in range(2)]
                        gt = [sb(f"gt{q}", [P, 2, HID + 1]) for q in range(2)]
                        cn = [sb(f"cn{q}", [P, 2]) for q in range(2)]
                        inv = [sb(f"inv{q}", [P, 2]) for q in range(2)]
                        some = [sb(f"some{q}", [P, 2]) for q in range(2)]
                        b2m = [sb(f"b2m{q}", [P, 2, D]) for q in range(2)]
                        ag = [sb(f"ag{q}", [P, 2, D]) for q in range(2)]
                        nT = [sb(f"nT{q}", [P, 4, P]) for q in range(2)]
                        uT = [sb(f"uT{q}", [P, 2, 2 * P]) for q in range(2)]
                        v = [sb(f"v{q}", [P, 2, D]) for q in range(2)]
                        y = [sb(f"y{q}", [P, 2, D]) for q in range(2)]
                        o = [sb(f"o{q}", [P, 2, D]) for q in range(2)]
                        stat = [sb(f"stat5{q}", [P, 2, 6]) for q in range(2)]
                        mv = [sb(f"mv5{q}", [P, 2, 2]) for q in range(2)]
                        rstd = [sb(f"rstd5{q}", [P, 2]) for q in range(2)]
                        ve = [sb(f"ve{q}", [P, 2]) for q in range(2)]
                        psM = pb("psM", [P, 2, D])
                        psN = pb("psN", [P, 4, P])
                        psU = pb("psU", [P, 2, 2 * P])
                        m_hb = [m(f"hb{q}") for q in range(2)]
                        m_xb = [m(f"xb{q}") for q in range(2)]
                        m_pt = [m(f"pt{q}") for q in range(2)]
                        m_cnt, m_inv, m_b2m = m("cnt"), m("inv"), m("b2m")
                        m_w2, m_ag, m_nt, m_nT = m("w2"), m("ag"), m("nt"), m("nT")
                        m_u, m_uT, m_v, m_vd = m("u"), m("uT"), m("v"), m("vd")
                        m_h4, m_stat, m_aggr, m_ve, m_rstd = m("h4"), m("stat"), m("aggr"), m("ve"), m("rstd")
                        m_y, m_o = m("y"), m("o")
                        hb_g = h1[0:NPAD].rearrange("(g j p) d -> g p j d", j=2, p=P)
                        xb_g = x1b.rearrange("(g j p) d -> g p j d", j=2, p=P)
                        out_g = out.rearrange("(g j p) d -> g p j d", j=2, p=P)

                    with nc.Block() as block:
                        def trip(eng):
                            return eng.value_load(trips[0:1, 1:2], min_val=1, max_val=NX // 4 - 1) + 1 if far else ITER

                        @block.sync
                        def _(sp):
                            if far:
                                sp.dma_start(W1s[:, :, :], W1[0:2 * D].rearrange("(c p) h -> p c h", p=P)).then_inc(m_w, 16)
                                sp.dma_start(W1e[0:DE, :], W1[2 * D:2 * D + DE]).then_inc(m_w, 16)
                                sp.dma_start(W1e[DE:DE + 1, :], b1.rearrange("(o h) -> o h", o=1)).then_inc(m_w, 16)
                                sp.dma_start(W2s[:, :, :], W2.rearrange("(c p) d -> p c d", p=P)).then_inc(m_w, 16)
                                sp.dma_start(U1s[:, :, :], U1.rearrange("(c p) h -> p c h", p=P)).then_inc(m_w, 16)
                                sp.dma_start(U2s[:, :, :], U2.rearrange("(c p) d -> p c d", p=P)).then_inc(m_w, 16)
                                sp.dma_start(b3c[:, :], b3).then_inc(m_w, 16)
                                for row, vec in ((b2B, b2), (b4B, b4), (gammaB, gamma)):
                                    sp.dma_start(row[:, :], vec.rearrange("(o d) -> o d", o=1).to_broadcast([P, D])).then_inc(m_w, 16)

                            def emit(i, q, live, edge_t):
                                p, _, _ = before(i, q, 0)
                                if live(0):
                                    for k in range(2):
                                        start = sp.value_load(ctl[0:1, 0, bass.ds(2 * p + (k + step0), 1)], min_val=0, max_val=E)
                                        if k == 0:
                                            held(sp, m_hid, 2 * (p - 2) + 2)
                                        sp.dma_start(ef[q][0:DE, k, :], edge_t[:, bass.ds(start, P)]).then_inc(m_ef[q], 16)
                                    if not far:
                                        past(sp, m_nt, p - 1)
                                        held(sp, m_h4, p - 1)
                                        sp.dma_start(hb[q][:, :, :], hb_g[bass.ds(p, 1)].rearrange("g p j d -> (g p) j d")).then_inc(m_hb[q], 16)
                                        for k in range(2):
                                            slot = sp.value_load(ctl[0:1, 2, bass.ds(2 * p + k, 1)], min_val=0, max_val=NX)
                                            if k == 0:
                                                held(sp, m_sumd, 2 * (p - 2) + 2)
                                            sp.dma_start(part[q][:, k, :], part1[bass.ds(slot, 1)].rearrange("x p d -> (x p) d")).then_inc(m_pt[q], 16)
                                if not far and live(2):
                                    p2, q2, _ = before(i, q, 2)
                                    held(sp, m_o, p2 - 1)
                                    sp.dma_start(xb5[q2][:, :, :], xb_g[bass.ds(p2, 1)].rearrange("g p j d -> (g p) j d")).then_inc(m_xb[q2], 16)
                                if far and live(1):
                                    p1, q1, _ = before(i, q, 1)
                                    held(sp, m_sumd, 2 * p1 + 2)
                                    sp.dma_start(part1[bass.ds(2 * p1 + 1, 2)].rearrange("x p d -> p x d"),
                                                 acc4[:, 2 * q1:2 * q1 + 2, :]).then_inc(m_st[q1], 16)
                            n = trip(sp)
                            with sp.If(unordered(sp) == 0):
                                pipelined(sp, lambda i, q, live: emit(i, q, live, edge_t), n, peel)
                                sp.sem_inc(passed, 1)
                            with sp.Else():
                                pipelined(sp, lambda i, q, live: emit(i, q, live, edge_ts), n, peel)
                                sp.sem_inc(passed, 1)
                            if far:
                                for q in range(2):
                                    held(sp, m_st[q], 16 * n)

                        @block.gpsimd
                        def _(pool):
                            if far:
                                nc.gpsimd.memset(ones[:, :], 1.0).then_inc(m_init, 1)
                                nc.gpsimd.memset(half[:, :], -0.5).then_inc(m_init, 1)
                                nc.gpsimd.memset(acc4[:, :, :], 0.0).then_inc(m_init, 1)

                            def emit(i, q, live):
                                p, _, turn = before(i, q, 0)
                                if live(0):
                                    held(pool, m_got[q], 64 * (turn - 1))
                                    nc.gpsimd.tensor_copy(idx5[q][:, :, :], idx[:, bass.ds(2 * p + step0, 2), :]).then_inc(m_idx, 1)
                                    past(pool, m_turn, p - 1)
                                    held(pool, m_idx, p + 1)
                                    for k in range(2):
                                        for c in range(2):
                                            nc.gpsimd.indirect_dma_start(
                                                out=got[q][:, k, c, :], out_offset=None, in_=h1[:, :],
                                                in_offset=bass.IndirectOffsetOnAxis(ap=idx5[q][:, k, c:c + 1], axis=0)).then_inc(m_got[q], 16)
                                if far:
                                    return
                                if live(1):
                                    p1, q1, turn1 = before(i, q, 1)
                                    past(pool, m_vd, p1 - 1)
                                    held(pool, m_hb[q1], 16 * turn1)
                                    nc.gpsimd.tensor_tensor(h4[q1][:, :, :], hb[q1][:, :, :],
                                                            b4B[:, :].rearrange("p (o d) -> p o d", o=1).to_broadcast([P, 2, D]),
                                                            ALU.add).then_inc(m_h4, 1)
                                if live(3):
                                    p3, q3, _ = before(i, q, 3)
                                    past(pool, m_o, p3 - 1)
                                    held(pool, m_ve, p3 + 1)
                                    nc.gpsimd.tensor_tensor(rstd[q3][:, :], ve[q3][:, :], half[:, :], ALU.pow).then_inc(m_rstd, 1)
                            pipelined(pool, emit, trip(pool), peel)

                        @block.tensor
                        def _(pe):
                            if far:
                                pe.wait_ge(m_w, 160)
                                pe.wait_ge(m_init, 5)

                            def hidden(i, q, k):
                                p, _, turn = before(i, q, 0)
                                if k == 0:
                                    pe.wait_ge(m_gT, p + 1)
                                    pe.wait_ge(m_ef[q], 32 * turn)
                                past(pe, m_gelu, 2 * p + (k - 1))
                                nc.tensor.matmul(psH[k][:, :], gT[q][:, k, 0, :], W1s[:, 0, :], start=True, stop=False)
                                nc.tensor.matmul(psH[k][:, :], gT[q][:, k, 1, :], W1s[:, 1, :], start=False, stop=False)
                                nc.tensor.matmul(psH[k][:, :], ef[q][:, k, :], W1e[:, :], start=False, stop=True).then_inc(m_hid, 1)

                            def emit(i, q, live):
                                p, _, turn = before(i, q, 0)
                                p1, q1, turn1 = before(i, q, 1)
                                p2, q2, turn2 = before(i, q, 2)
                                if live(0):
                                    pe.wait_ge(m_got[q], 64 * turn)
                                    past(pe, m_gT, p)
                                    for k in range(2):
                                        for c in range(2):
                                            ins = nc.tensor.transpose(psT[:, k, c, :], got[q][:, k, c, :], ident[:, :])
                                    ins.then_inc(m_turn, 1)
                                if live(1):
                                    for k in range(2):
                                        pe.wait_ge(m_gelu, 2 * p1 + (k + 1))
                                        pe.wait_ge(m_oh, p1 + 1)
                                        past(pe, m_sumd, 2 * p1 + (k - 1))
                                        for c in range(2):
                                            nc.tensor.matmul(psG[k][:, c * P:(c + 1) * P], G[q1][:, k, c * P:(c + 1) * P],
                                                             oh[q1][:, k, :], start=True, stop=True)
                                        nc.tensor.matmul(psG[k][:, HID:HID + 2], oh[q1][:, k, :], ones[:, :], start=True,
                                                         stop=True).then_inc(m_sum, 1)
                                if live(0):
                                    hidden(i, q, 0)
                                if not far and live(1):
                                    pe.wait_ge(m_sumd, 2 * p1 + 2)
                                    past(pe, m_vd, p1 - 1)
                                    for k in range(2):
                                        for c in range(2):
                                            ins = nc.tensor.matmul(psM[:, k, :], gt[q1][:, k, c * P:(c + 1) * P], W2s[:, c, :],
                                                                   start=(c == 0), stop=(c == 1))
                                    ins.then_inc(m_w2, 1)
                                if live(0):
                                    hidden(i, q, 1)
                                if far:
                                    return
                                if live(1):
                                    pe.wait_ge(m_ag, p1 + 1)
                                    pe.wait_ge(m_hb[q1], 16 * turn1)
                                    past(pe, m_nT, p1)
                                    for k in range(2):
                                        nc.tensor.transpose(psN[:, k, :], hb[q1][:, k, :], ident[:, :])
                                    for k in range(2):
                                        ins = nc.tensor.transpose(psN[:, 2 + k, :], ag[q1][:, k, :], ident[:, :])
                                    ins.then_inc(m_nt, 1)
                                if live(2):
                                    pe.wait_ge(m_uT, p2 + 1)
                                    if live(1):
                                        pe.wait_ge(m_ag, p1 + 1)
                                    else:
                                        past(pe, m_vd, p2)
                                    for k in range(2):
                                        for c in range(2):
                                            ins = nc.tensor.matmul(psM[:, k, :], uT[q2][:, c, k * P:(k + 1) * P], U2s[:, c, :],
                                                                   start=(c == 0), stop=(c == 1))
                                    ins.then_inc(m_v, 1)
                                if live(1):
                                    pe.wait_ge(m_nT, p1 + 1)
                                    past(pe, m_uT, p1)
                                    for c in range(2):
                                        nc.tensor.matmul(psU[:, c, :], U1s[:, 0, c * P:(c + 1) * P], nT[q1][:, 0:2, :],
                                                         start=True, stop=False)
                                        ins = nc.tensor.matmul(psU[:, c, :], U1s[:, 1, c * P:(c + 1) * P], nT[q1][:, 2:4, :],
                                                               start=False, stop=True)
                                    ins.then_inc(m_u, 1)
                            pipelined(pe, emit, trip(pe), peel)

                        @block.scalar
                        def _(act):
                            def emit(i, q, live):
                                p, _, _ = before(i, q, 0)
                                p1, q1, _ = before(i, q, 1)
                                p4, q4, _ = before(i, q, 4)
                                if live(0):
                                    act.wait_ge(m_turn, p + 1)
                                    past(act, m_hid, 2 * (p - 2) + 2)
                                    nc.scalar.copy(gT[q][:, :, :, :], psT[:, :, :, :]).then_inc(m_gT, 1)
                                    for k in range(2):
                                        act.wait_ge(m_hid, 2 * p + (k + 1))
                                        past(act, m_sum, 2 * (p - 2) + 2)
                                        nc.scalar.activation(G[q][:, k, :], psH[k][:, :], ACT.Gelu).then_inc(m_gelu, 1)
                                if far:
                                    return
                                if live(1):
                                    act.wait_ge(m_nt, p1 + 1)
                                    past(act, m_u, p1 - 1)
                                    nc.scalar.copy(nT[q1][:, :, :], psN[:, :, :]).then_inc(m_nT, 1)
                                    act.wait_ge(m_u, p1 + 1)
                                    past(act, m_v, p1 - 1)
                                    for c in range(2):
                                        ins = nc.scalar.activation(uT[q1][:, c, :], psU[:, c, :], ACT.Gelu, bias=b3c[:, c:c + 1])
                                    ins.then_inc(m_uT, 1)
                                if live(4):
                                    act.wait_ge(m_o, p4 + 1)
                                    act.dma_start(out_g[bass.ds(p4, 1)].rearrange("g p j d -> (g p) j d"), o[q4][:, :, :]).then_inc(m_st[q4], 16)
                            pipelined(act, emit, trip(act), peel)
                            if not far:
                                for q in range(2):
                                    act.wait_ge(m_st[q], 16 * ITER)

                        @block.vector
                        def _(dve):
                            if far:
                                nc.vector.memset(ef[0][DE:DE + 1, :, :], 1.0).then_inc(m_init, 1)
                                nc.vector.memset(ef[1][DE:DE + 1, :, :], 1.0).then_inc(m_init, 1)
                                dve.wait_ge(m_init, 5)

                            def emit(i, q, live):
                                p, _, _ = before(i, q, 0)
                                p1, q1, turn1 = before(i, q, 1)
                                p2, q2, _ = before(i, q, 2)
                                p3, q3, turn3 = before(i, q, 3)
                                if live(0):
                                    past(dve, m_sum, 2 * (p - 2) + 2)
                                    for k in range(2):
                                        ins = nc.vector.tensor_scalar(oh[q][:, k, :], iota_f[:, :],
                                                                      dloc[:, bass.ds(2 * p + (k + step0), 1)], None, ALU.is_equal)
                                    ins.then_inc(m_oh, 1)
                                if far and live(1):
                                    past(dve, m_st[q1], 16 * (turn1 - 1))
                                    for k in range(2):
                                        dve.wait_ge(m_sum, 2 * p1 + (k + 1))
                                        past(dve, m_sumd, 2 * p1 + k)
                                        a4 = 2 * q1 + k
                                        nc.vector.scalar_tensor_tensor(acc4[:, a4, 0:HID + 1], acc4[:, (a4 - 1) % 4, 0:HID + 1],
                                                                       same[:, bass.ds(2 * p1 + k, 1)], psG[k][:, 0:HID + 1],
                                                                       ALU.mult, ALU.add).then_inc(m_sumd, 1)
                                if far:
                                    return
                                if live(1):
                                    dve.wait_ge(m_pt[q1], 32 * turn1)
                                    past(dve, m_w2, p1 - 1)
                                    for k in range(2):
                                        dve.wait_ge(m_sum, 2 * p1 + (k + 1))
                                        nc.vector.tensor_tensor(gt[q1][:, k, :], psG[k][:, 0:HID + 1], part[q1][:, k, 0:HID + 1],
                                                                ALU.add).then_inc(m_sumd, 1)
                                    dve.wait_ge(m_sumd, 2 * p1 + 2)
                                    nc.vector.tensor_scalar(cn[q1][:, :], gt[q1][:, :, HID], 1.0, None, ALU.max).then_inc(m_cnt, 1)
                                    nc.vector.tensor_scalar(some[q1][:, :], gt[q1][:, :, HID], 1.0, None, ALU.min).then_inc(m_cnt, 1)
                                if live(3):
                                    for k in range(2):
                                        ins = nc.vector.scalar_tensor_tensor(y[q3][:, k, :], v[q3][:, k, :], mv[q3][:, k, 0:1],
                                                                             gammaB[:, :], ALU.subtract, ALU.mult)
                                    ins.then_inc(m_y, 1)
                                    dve.wait_ge(m_y, p3 + 1)
                                    dve.wait_ge(m_rstd, p3 + 1)
                                    dve.wait_ge(m_xb[q3], 16 * turn3)
                                    past(dve, m_st[q3], 16 * (turn3 - 1))
                                    for k in range(2):
                                        ins = nc.vector.scalar_tensor_tensor(o[q3][:, k, :], y[q3][:, k, :], rstd[q3][:, k:k + 1],
                                                                             xb5[q3][:, k, :], ALU.mult, ALU.add)
                                    ins.then_inc(m_o, 1)
                                if live(1):
                                    dve.wait_ge(m_cnt, 2 * p1 + 2)
                                    nc.vector.reciprocal(inv[q1][:, :], cn[q1][:, :]).then_inc(m_inv, 1)
                                    for k in range(2):
                                        ins = nc.vector.tensor_scalar(b2m[q1][:, k, :], b2B[:, :], some[q1][:, k:k + 1], None, ALU.mult)
                                    ins.then_inc(m_b2m, 1)
                                    dve.wait_ge(m_inv, p1 + 1)
                                    dve.wait_ge(m_b2m, p1 + 1)
                                    dve.wait_ge(m_w2, p1 + 1)
                                    past(dve, m_nt, p1 - 1)
                                    for k in range(2):
                                        ins = nc.vector.scalar_tensor_tensor(ag[q1][:, k, :], psM[:, k, :], inv[q1][:, k:k + 1],
                                                                             b2m[q1][:, k, :], ALU.mult, ALU.add)
                                    ins.then_inc(m_ag, 1)
                                if live(2):
                                    dve.wait_ge(m_v, p2 + 1)
                                    dve.wait_ge(m_h4, p2 + 1)
                                    nc.vector.tensor_tensor(v[q2][:, :, :], psM[:, :, :], h4[q2][:, :, :], ALU.add).then_inc(m_vd, 1)
                                    dve.wait_ge(m_vd, p2 + 1)
                                    for k in range(2):
                                        ins = nc.vector.bn_stats(stat[q2][:, k, :], v[q2][:, k, :])
                                    ins.then_inc(m_stat, 1)
                                    held(dve, m_stat, p2 + 1)
                                    for k in range(2):
                                        ins = nc.vector.bn_aggr(mv[q2][:, k, :], stat[q2][:, k, :])
                                    ins.then_inc(m_aggr, 1)
                                    dve.wait_ge(m_aggr, p2 + 1)
                                    nc.vector.tensor_scalar(ve[q2][:, :], mv[q2][:, :, 1], EPS, None, ALU.add).then_inc(m_ve, 1)
                            pipelined(dve, emit, trip(dve), peel)
                end_section()



_OUT = "out_dram"


def kernel(**inputs):
    import concourse.bacc as _bacc
    from concourse.bass_utils import run_bass_kernel_spmd as _run

    def padded(v, rows, fill):
        return np.concatenate([v, np.full((rows - v.shape[0],) + v.shape[1:], fill, v.dtype)])

    g = {k: np.asarray(v) for k, v in inputs.items()}
    src, dst = padded(g["src"], EPAD, 0), padded(g["dst"], DT, SENT)
    arrays = {
        "x": padded(g["x"], NPAD, 0),
        "srcdst": np.stack([src, dst[:EPAD]], axis=1),
        "dst": dst,
        "edge_t": np.ascontiguousarray(padded(g["edge_attr_64"], EPAD, 0).T),
        "edge_rows": padded(g["edge_attr_64"], EPAD, 0),
        "W": g["L0_gnn_W"], "a": g["L0_gnn_a"].reshape(2, D).T,
        "W1": g["L1_gnn_W1"], "b1": g["L1_gnn_b1"], "W2": g["L1_gnn_W2"], "b2": g["L1_gnn_b2"],
        "U1": g["L1_gnn_U1"], "b3": g["L1_gnn_b3"].reshape(2, P).T, "U2": g["L1_gnn_U2"], "b4": g["L1_gnn_b4"],
        "gamma": g["L1_gnn_gamma"], "beta": g["L1_gnn_beta"],
    }
    nc = _bacc.Bacc("TRN2", target_bir_lowering=False, num_devices=1)
    named, args = {}, []
    for name, v in arrays.items():
        named[f"in_{name}"] = np.ascontiguousarray(v)
        args.append(nc.dram_tensor(f"in_{name}", v.shape, mybir.dt.from_np(v.dtype), kind="ExternalInput").ap())
    args.append(nc.dram_tensor(_OUT, (NPAD, D), F32, kind="ExternalOutput").ap())
    gnn_kernel(nc, *args)
    r = _run(nc, [named], core_ids=[0])
    return r.results[0][_OUT][:N]
```

```python
from contextlib import ExitStack

import numpy as np

import concourse.bass as bass
from concourse import mybir

ALU = mybir.AluOpType
ACT = mybir.ActivationFunctionType
AX = mybir.AxisListType
F32 = mybir.dt.float32
BF16 = mybir.dt.bfloat16
I32 = mybir.dt.int32
RMAX = bass.bass_isa.ReduceOp.max
RADD = bass.bass_isa.ReduceOp.add

P = 128
N = 50000
E = 50000
D = 128
DP = D + 2
DE = 64
HID = 256
EPS = 1e-5
ALPHA = 0.2

NB = 392
NPAD = NB * P
NX = 400
S = NB + NX
XT = 512
SENT = NPAD
EPAD = NB * P
HI, LO = 13, 32
NT = HI * LO
G7 = 7
DT = (E + 2 * P + P - 1) // P * P
FAR = 60000.0


def gnn_kernel(nc, x, srcdst, dst, edge_t, edge_rows, W, a, W1, b1, W2, b2, U1, b3, U2, b4, gamma, beta, out):
    outer = ExitStack()

    here = []

    def sem(name):
        here.append(nc.alloc_semaphore(name))
        return here[-1]

    def end_section():
        nc.clear_and_free_semaphores(list(here))
        here.clear()
        nc.all_engine_barrier()

    def dram(name, shape, dt=F32):
        return nc.dram_tensor(name, shape, dt).ap()

    def sb_in(ctx):
        return lambda name, shape, dt=F32: ctx.enter_context(nc.sbuf_tensor(name, shape, dt))

    def past(eng, s, count):
        if isinstance(count, int) and count <= 0:
            return
        eng.wait_ge(s, count)

    def looped(eng, body, count):
        body(0)
        with eng.Fori(1, count) as i:
            body(i)

    passed = outer.enter_context(nc.semaphore("passed"))

    def held(eng, s, count):
        if isinstance(count, int):
            return past(eng, s, count)
        eng.wait_ge(s, count)
        eng.sem_inc(passed, 1)

    def pipelined(eng, emit, count, peeled=1, unroll=2, extra=0):
        for i in range(peeled):
            for q in range(unroll):
                emit(i, q, lambda lag, p=unroll * i + q: p - lag >= 0)
        with eng.Fori(peeled, count) as i:
            for q in range(unroll):
                emit(i, q, lambda lag: True)
        for d in range(extra + 5):
            emit(count + d // unroll, d % unroll, lambda lag, d=d: d - lag < extra)

    def before(i, q, lag, unroll=2):
        slot = (q - lag) % unroll
        turn = (q - lag - slot) // unroll
        return unroll * i + (q - lag), slot, i + (turn + 1)

    with outer:
        h_proj = dram("h_proj", [NPAD, DP])
        s_dst = dram("s_dst", [NPAD, 1])
        edge_proj = dram("edge_proj", [S, P, D])
        far_list = dram("far_list", [2, XT], I32)
        x1b = dram("x1b", [NPAD, D])
        h1 = dram("h1", [NPAD + P, D])
        part0 = dram("part0", [NX + 1, P, D])
        GW = HID + 4
        part1 = dram("part1", [NX + 1, P, GW])

        sb = sb_in(outer)
        ident = sb("ident", [P, P])
        iota_f = sb("iota_f", [P, P])
        ctl = sb("ctl", [1, 3, NB + XT], I32)
        trips = sb("trips", [1, 3], I32)
        some_far = sb("some_far", [1, NB // 4], I32)
        base = sb("base", [P, NB + XT])
        same = sb("same", [P, XT])
        idx = sb("idx", [P, S, 2], I32)
        dloc = sb("dloc", [P, S])
        wgt = sb("wgt", [P, S])

        with ExitStack() as ctx:
            sb = sb_in(ctx)
            ps = ctx.enter_context(nc.psum_tensor("ps_start", [P, NT], F32))
            ps_hist = ctx.enter_context(nc.psum_tensor("ps_hist", [G7 * HI, G7, LO], F32))
            ramp_i = sb("ramp_i", [P, NT], I32)
            ramp = sb("ramp", [P, NT])
            dsts = sb("dsts", [P, NB], I32)
            bid = sb("bid", [P, NB], I32)
            bidf = sb("bidf", [P, NB])
            hi = sb("hi", [P, NB], I32)
            hif = sb("hif", [P, NB])
            lof = sb("lof", [P, NB])
            is_hi = sb("is_hi", [P, NB, HI], BF16)
            is_lo = sb("is_lo", [P, NB, LO], BF16)
            zerob = sb("zerob", [P, G7 * LO], BF16)
            own = sb("own", [G7 * HI, G7])
            own_hi = sb("own_hi", [G7 * HI, HI])
            hist7 = sb("hist7", [G7 * HI, G7, LO])
            hist = sb("hist", [G7 * HI, LO])
            spread = sb("spread", [G7 * HI, HI, LO])
            onesf = sb("onesf", [G7 * HI, P])
            per = sb("per", [P, NB])
            st = sb("st", [P, NB])
            n1 = sb("n1", [P, NB])
            ni = sb("ni", [P, NB], I32)
            nx = sb("nx", [P, NB])
            zeros = sb("zeros", [P, NB])
            xend = sb("xend", [P, NB])
            shift = sb("shift", [P, NB])
            last = sb("last", [P, NB])
            junk = sb("junk", [P, NB])
            dstn = sb("dstn", [P, NB], I32)
            down = sb("down", [P, 2])
            xi = sb("xi", [P, 4], I32)
            xf = sb("xf", [P, 4])
            blkx = sb("blkx", [P, 4])
            valid = sb("valid", [P, 4])
            sx = sb("sx", [P, 4])
            sx2 = sb("sx2", [P, 4])
            lists = sb("lists", [P, 2, 4], I32)
            farb = sb("farb", [P, XT], I32)
            ti = sb("ti", [1, 2])
            ti2 = sb("ti2", [1, 2], I32)
            any4 = sb("any4", [1, NB // 4])
            ztile = sb("ztile", [P, GW])

            c_in = sem("c_in")
            c_const = sem("c_const")
            c_ch = sem("c_ch")
            c_hot = sem("c_hot")
            c_mm = sem("c_mm")
            c_list = sem("c_list")
            c_far = sem("c_far")
            c_zero = sem("c_zero")
            c_z = sem("c_z")
            c_down = sem("c_down")

            with nc.Block() as block:
                @block.gpsimd
                def _(pool):
                    nc.gpsimd.iota(ramp_i[:, :], [[1, NT]], 0, 0).then_inc(c_const, 1)
                    nc.gpsimd.iota(xi[:, :], [[1, 4]], 0, 4).then_inc(c_const, 1)
                    nc.gpsimd.memset(ident[:, :], 0.0).then_inc(c_const, 1)
                    nc.gpsimd.memset(zeros[:, :], 0.0).then_inc(c_const, 1)
                    nc.gpsimd.memset(onesf[:, :], 1.0).then_inc(c_const, 1)
                    nc.gpsimd.memset(zerob[:, :], 0.0).then_inc(c_const, 1)
                    nc.gpsimd.memset(ztile[:, :], 0.0).then_inc(c_z, 1)
                    pool.wait_ge(c_const, 3)
                    nc.gpsimd.affine_select(out=ident[:, :], in_=ident[:, :], compare_op=ALU.not_equal, fill=1.0,
                                            base=0, pattern=[[-1, P]], channel_multiplier=1).then_inc(c_const, 1)
                    nc.gpsimd.memset(idx[:, :, :], 0)
                    pool.wait_ge(c_down, 1)
                    nc.gpsimd.partition_all_reduce(down[:, 1:2], down[:, 0:1], P, RADD).then_inc(c_down, 1)

                @block.sync
                def _(sp):
                    sp.dma_start(dsts[:, :], dst[0:NPAD].rearrange("(p c) -> p c", c=NB)).then_inc(c_in, 16)
                    sp.dma_start(dstn[:, :], dst[1:NPAD + 1].rearrange("(p c) -> p c", c=NB)).then_inc(c_in, 16)
                    sp.wait_ge(c_z, 1)
                    sp.dma_start(part0[0], ztile[:, 0:D]).then_inc(c_zero, 16)
                    sp.dma_start(part1[0], ztile[:, :]).then_inc(c_zero, 16)
                    sp.dma_start(h1[NPAD:NPAD + P], ztile[:, 0:D]).then_inc(c_zero, 16)
                    sp.wait_ge(c_list, 1)
                    sp.dma_start(far_list[0].rearrange("(p j) -> p j", j=4), lists[:, 0, :]).then_inc(c_far, 16)
                    sp.dma_start(far_list[1].rearrange("(p j) -> p j", j=4), lists[:, 1, :]).then_inc(c_far, 16)
                    sp.wait_ge(c_far, 32)
                    sp.dma_start(ctl[0:1, 0:2, NB:NB + XT], far_list.rearrange("(o k) x -> o k x", o=1)).then_inc(c_far, 16)
                    sp.dma_start(farb[:, :], far_list[1:2, :].to_broadcast([P, XT])).then_inc(c_far, 16)
                    sp.wait_ge(c_far, 64)
                    sp.wait_ge(c_zero, 48)

                @block.tensor
                def _(pe):
                    pe.wait_ge(c_const, 6)
                    zeros7 = zerob[:, 0:G7 * HI], zerob[:, :]
                    hist_out = ps_hist[:, :, :].rearrange("p g l -> p (g l)")
                    nc.tensor.matmul(hist_out, *zeros7, start=True, stop=False)
                    for quarter in range(4):
                        pe.wait_ge(c_hot, quarter + 1)
                        for c in range(NB // 4 * quarter, NB // 4 * (quarter + 1), G7):
                            nc.tensor.matmul(hist_out, is_hi[:, c:c + G7, :].rearrange("p g h -> p (g h)"),
                                             is_lo[:, c:c + G7, :].rearrange("p g l -> p (g l)"), start=False, stop=False)
                    nc.tensor.matmul(hist_out, *zeros7, start=False, stop=True).then_inc(c_mm, 1)
                    pe.wait_ge(c_hot, 5)
                    nc.tensor.matmul(ps[:, :], onesf[:, :], spread[:, :, :].rearrange("p h l -> p (h l)"), start=True,
                                     stop=True).then_inc(c_mm, 1)

                @block.vector
                def _(dve):
                    count = [0]

                    def link(ins):
                        count[0] += 1
                        ins.then_inc(c_ch, 1)
                        dve.wait_ge(c_ch, count[0])

                    dve.wait_ge(c_const, 4)
                    dve.wait_ge(c_in, 32)
                    nc.vector.tensor_copy(ramp[:, :], ramp_i[:, :])
                    nc.vector.tensor_copy(iota_f[:, :], ramp_i[:, 0:P])
                    nc.vector.tensor_copy(xf[:, :], xi[:, :])
                    nc.vector.memset(dloc[:, :], FAR)
                    link(nc.vector.tensor_scalar(bid[:, :], dsts[:, :], 7, None, ALU.arith_shift_right))
                    nc.vector.tensor_scalar(hi[:, :], bid[:, :], 5, None, ALU.arith_shift_right).then_inc(c_ch, 1)
                    count[0] += 1
                    link(nc.vector.tensor_copy(bidf[:, :], bid[:, :]))
                    link(nc.vector.tensor_copy(hif[:, :], hi[:, :]))
                    link(nc.vector.scalar_tensor_tensor(lof[:, :], hif[:, :], -float(LO), bidf[:, :], ALU.mult, ALU.add))
                    for quarter in range(4):
                        n = NB // 4
                        cs = slice(n * quarter, n * quarter + n)
                        for hot, part_of, width in ((is_hi, hif, HI), (is_lo, lof, LO)):
                            ins = nc.vector.tensor_tensor(
                                hot[:, cs, :], part_of[:, cs].rearrange("p (c o) -> p c o", o=1).to_broadcast([P, n, width]),
                                ramp[:, 0:width].rearrange("p (o d) -> p o d", o=1).to_broadcast([P, n, width]), ALU.is_equal)
                        ins.then_inc(c_hot, 1)
                    link(nc.vector.tensor_tensor(junk[:, :], dsts[:, :], dstn[:, :], ALU.is_gt))
                    nc.vector.tensor_reduce(down[:, 0:1], junk[:, :], AX.X, ALU.add).then_inc(c_down, 1)

                    dve.wait_ge(c_const, 7)
                    of_g = ident[0:G7 * HI, 0:G7 * HI]
                    nc.vector.tensor_reduce(own[:, :], of_g.rearrange("p (g h) -> p g h", h=HI), AX.X, ALU.add)
                    nc.vector.tensor_reduce(own_hi[:, :], of_g.rearrange("p (g h) -> p h g", h=HI), AX.X, ALU.add)
                    dve.wait_ge(c_mm, 1)
                    link(nc.vector.tensor_copy(hist7[:, :, :], ps_hist[:, :, :]))
                    link(nc.vector.tensor_tensor(hist7[:, :, :], hist7[:, :, :],
                                                 own[:, :].rearrange("p (g o) -> p g o", o=1).to_broadcast([G7 * HI, G7, LO]), ALU.mult))
                    link(nc.vector.tensor_reduce(hist[:, :], hist7[:, :, :].rearrange("p g l -> p l g"), AX.X, ALU.add))
                    nc.vector.tensor_tensor(
                        spread[:, :, :], own_hi[:, :].rearrange("p (c o) -> p c o", o=1).to_broadcast([G7 * HI, HI, LO]),
                        hist[:, :].rearrange("p (o d) -> p o d", o=1).to_broadcast([G7 * HI, HI, LO]), ALU.mult).then_inc(c_hot, 1)
                    dve.wait_ge(c_mm, 2)
                    link(nc.vector.tensor_copy(per[:, :], ps[:, 0:NB]))
                    link(nc.vector.tensor_tensor_scan(st[:, :], per[:, :], zeros[:, :], 0.0, ALU.add, ALU.add))
                    link(nc.vector.tensor_tensor(st[:, :], st[:, :], per[:, :], ALU.subtract))
                    link(nc.vector.tensor_scalar(n1[:, :], per[:, :], -1.0, 0.0, ALU.add, ALU.max))
                    link(nc.vector.tensor_copy(ni[:, :], n1[:, :]))
                    link(nc.vector.tensor_scalar(ni[:, :], ni[:, :], 7, None, ALU.arith_shift_right))
                    link(nc.vector.tensor_copy(nx[:, :], ni[:, :]))
                    link(nc.vector.tensor_tensor_scan(xend[:, :], nx[:, :], zeros[:, :], 0.0, ALU.add, ALU.add))
                    link(nc.vector.tensor_scalar(last[:, :], nx[:, :], 0.0, None, ALU.is_gt))
                    link(nc.vector.tensor_tensor(last[:, :], last[:, :], xend[:, :], ALU.mult))
                    link(nc.vector.tensor_tensor(shift[:, :], xend[:, :], nx[:, :], ALU.subtract))
                    link(nc.vector.tensor_scalar(shift[:, :], shift[:, :], -float(P), float(P), ALU.mult, ALU.add))
                    link(nc.vector.tensor_tensor(shift[:, :], shift[:, :], st[:, 0:NB], ALU.add))
                    for j in range(4):
                        link(nc.vector.tensor_scalar(junk[:, :], xend[:, :], xf[:, j:j + 1], 0.0, ALU.is_le, ALU.add,
                                                     accum_out=blkx[:, j:j + 1]))
                        link(nc.vector.scalar_tensor_tensor(junk[:, :], ramp[:, 0:NB], blkx[:, j:j + 1], shift[:, :],
                                                            ALU.is_equal, ALU.mult, accum_out=sx[:, j:j + 1]))
                    link(nc.vector.tensor_scalar(valid[:, :], blkx[:, :], float(NB), None, ALU.is_lt))
                    link(nc.vector.tensor_scalar(sx2[:, :], xf[:, :], float(P), -float(E), ALU.mult, ALU.add))
                    link(nc.vector.tensor_tensor(sx[:, :], sx[:, :], sx2[:, :], ALU.add))
                    link(nc.vector.tensor_tensor(sx[:, :], sx[:, :], valid[:, :], ALU.mult))
                    link(nc.vector.tensor_scalar(sx[:, :], sx[:, :], float(E), None, ALU.add))
                    link(nc.vector.tensor_copy(lists[:, 0, :], sx[:, :]))
                    link(nc.vector.tensor_scalar(blkx[:, :], blkx[:, :], float(NB - 1), None, ALU.min))
                    nc.vector.tensor_copy(lists[:, 1, :], blkx[:, :]).then_inc(c_list, 1)
                    nc.vector.tensor_copy(ctl[0:1, 0, 0:NB], st[0:1, 0:NB])
                    nc.vector.tensor_copy(ctl[0:1, 1, 0:NB], ramp[0:1, 0:NB])
                    nc.vector.tensor_copy(ctl[0:1, 2, 0:NB], last[0:1, :])
                    link(nc.vector.tensor_reduce(any4[:, :], last[0:1, :].rearrange("p (g b) -> p g b", b=4), AX.X, ALU.max))
                    nc.vector.tensor_scalar(some_far[:, :], any4[:, :], 1.0, None, ALU.min)
                    nc.vector.tensor_scalar(base[:, 0:NB], ramp[:, 0:NB], float(P), None, ALU.mult)
                    link(nc.vector.tensor_scalar(ti[:, 0:1], xend[0:1, NB - 1:NB], -1.0, 32.0, ALU.add, ALU.max))
                    link(nc.vector.tensor_scalar(ti[:, 1:2], xend[0:1, NB - 1:NB], -1.0, 16.0, ALU.add, ALU.max))
                    link(nc.vector.tensor_copy(ti2[:, :], ti[:, :]))
                    nc.vector.tensor_scalar(trips[:, 0:1], ti2[:, 0:1], 4, None, ALU.arith_shift_right)
                    nc.vector.tensor_scalar(trips[:, 1:2], ti2[:, 1:2], 3, None, ALU.arith_shift_right)
                    dve.wait_ge(c_down, 2)
                    nc.vector.tensor_scalar(trips[:, 2:3], down[0:1, 1:2], 1.0, None, ALU.min)
                    dve.wait_ge(c_far, 64)
                    nc.vector.tensor_scalar(base[:, NB:NB + XT], farb[:, :], float(P), None, ALU.mult)
                    nc.vector.memset(same[:, 0:1], 0.0)
                    nc.vector.tensor_tensor(same[:, 1:XT], farb[:, 1:XT], farb[:, 0:XT - 1], ALU.is_equal)


        end_section()

        def unordered(eng):
            return eng.value_load(trips[0:1, 2:3], min_val=0, max_val=1)

        srcdst_s = dram("srcdst_s", [EPAD, 2], I32)
        edge_s = dram("edge_s", [EPAD, DE])
        edge_ts = dram("edge_ts", [DE, EPAD])
        with ExitStack() as ctx:
            sb = sb_in(ctx)
            CT = 56
            CC = CT * P
            pairs = sb("pairs", [P, NB, 2], I32)
            dcol = sb("dcol", [P, NB])
            rowi = sb("rowi", [P, CC], I32)
            rowf = sb("rowf", [P, CC])
            jnk = sb("jnk", [P, CC], BF16)
            jnk2 = sb("jnk2", [P, P], BF16)
            mark = sb("mark", [P, 1])
            below = sb("below", [P, NB])
            ties = sb("ties", [P, NB])
            place = sb("place", [P, NB])
            placei = sb("placei", [P, NB], I32)
            ltri = sb("ltri", [P, P])
            pi = sb("pi", [P, 1], I32)
            pf = sb("pf", [P, 1])
            pl1 = sb("pl1", [P, 1], I32)
            pr1 = sb("pr1", [P, 2], I32)
            er1 = sb("er1", [P, DE])
            et1 = sb("et1", [DE, P])
            psE = ctx.enter_context(nc.psum_tensor("psEs", [DE, P], F32))
            g_in = sem("g_in")
            g_row = sem("g_row")
            g_chunk = sem("g_chunk")
            g_ch = sem("g_ch")
            g_pi = sem("g_pi")
            g_er = sem("g_er")
            g_cp = sem("g_cp")
            g_sc = sem("g_sc")
            g_lr = sem("g_lr")
            g_tp = sem("g_tp")
            g_ev = sem("g_ev")
            g_st = sem("g_st")

            with nc.Block() as block:
                @block.sync
                def _(sp):
                    with sp.If(unordered(sp) == 1):
                        sp.dma_start(pairs[:, :, :], srcdst.rearrange("(c p) k -> p c k", p=P)).then_inc(g_in, 16)
                        for c in range(NB // CT):
                            past(sp, g_chunk, c)
                            sp.dma_start(rowi[:, :], dst[c * CC:(c + 1) * CC].rearrange("(o n) -> o n", o=1)
                                         .to_broadcast([P, CC])).then_inc(g_row, 16)

                @block.gpsimd
                def _(pool):
                    with pool.If(unordered(pool) == 1):
                        nc.gpsimd.iota(pi[:, :], [[0, 1]], 0, 1).then_inc(g_pi, 1)

                @block.vector
                def _(dve):
                    with dve.If(unordered(dve) == 1):
                        done = [0]

                        def link(ins):
                            done[0] += 1
                            ins.then_inc(g_ch, 1)
                            dve.wait_ge(g_ch, done[0])

                        dve.wait_ge(g_pi, 1)
                        link(nc.vector.tensor_copy(pf[:, :], pi[:, :]))
                        link(nc.vector.tensor_scalar(ltri[:, :], iota_f[:, :], pf[:, :], None, ALU.is_lt))
                        dve.wait_ge(g_in, 16)
                        link(nc.vector.tensor_copy(dcol[:, :], pairs[:, :, 1]))
                        link(nc.vector.memset(place[:, :], 0.0))

                        def compare(t):
                            return nc.vector.tensor_scalar(jnk[:, :], rowf[:, :], dcol[:, bass.ds(t, 1)], 0.0, ALU.is_lt,
                                                           ALU.add, accum_out=below[:, bass.ds(t, 1)])
                        for c in range(NB // CT):
                            t0 = c * CT
                            dve.wait_ge(g_row, 16 * (c + 1))
                            link(nc.vector.tensor_copy(rowf[:, :], rowi[:, :]))
                            if c > 0:
                                with dve.Fori(0, t0) as t:
                                    compare(t).then_inc(g_ch, 1)
                                    dve.wait_ge(g_ch, done[0] + t + 1)
                                done[0] += t0
                            with dve.Fori(0, CT) as i:
                                tile = rowf[:, bass.ds(P * i, P)]
                                compare(i + t0).then_inc(g_ch, 1)
                                nc.vector.scalar_tensor_tensor(jnk2[:, :], tile, dcol[:, bass.ds(i + t0, 1)], ltri[:, :],
                                                               ALU.is_equal, ALU.mult,
                                                               accum_out=ties[:, bass.ds(i + t0, 1)]).then_inc(g_ch, 1)
                                dve.wait_ge(g_ch, done[0] + 3 * i + 2)
                                nc.vector.tensor_scalar(tile, tile, -0.5, None, ALU.add).then_inc(g_ch, 1)
                                dve.wait_ge(g_ch, done[0] + 3 * i + 3)
                            done[0] += 3 * CT
                            if t0 + CT < NB:
                                with dve.Fori(0, NB - CT - t0) as t:
                                    compare(t + (t0 + CT)).then_inc(g_ch, 1)
                                    dve.wait_ge(g_ch, done[0] + t + 1)
                                done[0] += NB - CT - t0
                            link(nc.vector.tensor_tensor(place[:, :], place[:, :], below[:, :], ALU.add))
                            nc.vector.memset(mark[:, :], 0.0).then_inc(g_chunk, 1)
                        link(nc.vector.tensor_tensor(place[:, :], place[:, :], ties[:, :], ALU.add))
                        link(nc.vector.tensor_copy(placei[:, :], place[:, :]))

            with nc.Block() as block:
                @block.gpsimd
                def _(pool):
                    with pool.If(unordered(pool) == 1):
                        with pool.Fori(0, NB) as i:
                            pool.dma_start(er1[:, :], edge_rows[bass.ds(P * i, P), :]).then_inc(g_er, 16)
                            nc.gpsimd.tensor_copy(pl1[:, :], placei[:, bass.ds(i, 1)]).then_inc(g_cp, 1)
                            nc.gpsimd.tensor_copy(pr1[:, :], pairs[:, bass.ds(i, 1), :].rearrange("p o k -> p (o k)")).then_inc(g_cp, 1)
                            held(pool, g_er, 16 * i + 16)
                            held(pool, g_cp, 2 * i + 2)
                            nc.gpsimd.indirect_dma_start(
                                out=srcdst_s[:, :], out_offset=bass.IndirectOffsetOnAxis(ap=pl1[:, 0:1], axis=0),
                                in_=pr1[:, :], in_offset=None).then_inc(g_sc, 16)
                            nc.gpsimd.indirect_dma_start(
                                out=edge_s[:, :], out_offset=bass.IndirectOffsetOnAxis(ap=pl1[:, 0:1], axis=0),
                                in_=er1[:, :], in_offset=None).then_inc(g_sc, 16)
                            held(pool, g_sc, 32 * i + 32)
                        pool.sem_inc(passed, 1)

            with nc.Block() as block:
                @block.sync
                def _(sp):
                    with sp.If(unordered(sp) == 1):
                        def body(i):
                            held(sp, g_st, 16 * i)
                            sp.dma_start(er1[:, :], edge_s[bass.ds(P * i, P), :]).then_inc(g_lr, 16)
                            held(sp, g_ev, i + 1)
                            sp.dma_start(edge_ts[:, bass.ds(P * i, P)], et1[:, :]).then_inc(g_st, 16)
                        looped(sp, body, NB)
                        sp.wait_ge(g_st, 16 * NB)
                        sp.sem_inc(passed, 1)

                @block.tensor
                def _(pe):
                    with pe.If(unordered(pe) == 1):
                        with pe.Fori(0, NB) as i:
                            held(pe, g_lr, 16 * i + 16)
                            nc.tensor.transpose(psE[:, :], er1[:, :], ident[:, :]).then_inc(g_tp, 1)
                        pe.sem_inc(passed, 1)

                @block.vector
                def _(dve):
                    with dve.If(unordered(dve) == 1):
                        with dve.Fori(0, NB) as i:
                            dve.wait_ge(g_tp, i + 1)
                            nc.vector.tensor_copy(et1[:, :], psE[:, :]).then_inc(g_ev, 1)
                        dve.sem_inc(passed, 1)


        end_section()

        with ExitStack() as ctx:
            sb = sb_in(ctx)
            xb = [sb(f"xb{q}", [P, 4, D]) for q in range(4)]
            hb = [sb(f"hb{q}", [P, 4, D]) for q in range(2)]
            hT = [sb(f"hT{q}", [P, 4, P]) for q in range(2)]
            pj = [sb(f"pj{q}", [P, 4, DP]) for q in range(4)]
            stat = [sb(f"stat{q}", [P, 4, 6]) for q in range(2)]
            mv = [sb(f"mv{q}", [P, 4, 2]) for q in range(2)]
            std = [sb(f"std{q}", [P, 4]) for q in range(2)]
            rstd = [sb(f"rstd{q}", [P, 4]) for q in range(2)]
            nmr = [sb(f"nmr{q}", [P, 4]) for q in range(2)]
            Wsb = sb("Wsb", [P, DP])
            s2c = sb("s2c", [P, NB])
            WT = sb("WT", [P, D])
            asb = sb("asb", [P, 2])
            eps = sb("eps", [P, 1])
            sT = sb("sT", [98, 4, P])
            psT = [ctx.enter_context(nc.psum_tensor(f"psT{q}", [P, 4, P], F32)) for q in range(2)]
            psW = [ctx.enter_context(nc.psum_tensor(f"psW{q}", [P, 4, 2 * P], F32)) for q in range(2)]
            psE = [ctx.enter_context(nc.psum_tensor(f"psE{q}", [P, 4, P], F32)) for q in range(2)]
            w_in = sem("a_w_in")
            x_in = [sem(f"a_x_in{q}") for q in range(4)]
            p_out = [sem(f"a_p_out{q}") for q in range(4)]
            wprep = sem("a_wprep")
            wt_ps = sem("a_wt_ps")
            stats = sem("a_stats")
            aggr = sem("a_aggr")
            stdev = sem("a_stdev")
            recip = sem("a_recip")
            shifted = sem("a_shifted")
            normed = sem("a_normed")
            turned = sem("a_turned")
            ht_ready = sem("a_ht_ready")
            projected = sem("a_projected")
            evacuated = sem("a_evacuated")
            s_turned = sem("a_s_turned")
            s_copied = sem("a_s_copied")
            s_stored = sem("a_s_stored")
            x_g = x.rearrange("(g j p) d -> g p j d", j=4, p=P)
            proj_g = h_proj.rearrange("(g j p) d -> g p j d", j=4, p=P)
            ITER, REST = NB // 16, 2

            with nc.Block() as block:
                @block.sync
                def _(sp):
                    sp.dma_start(Wsb[:, 0:D], W).then_inc(w_in, 16)
                    sp.dma_start(asb[:, :], a).then_inc(w_in, 16)

                    def emit(i, q, live):
                        g, _, _ = before(i, q, 0, 4)
                        g5, q5, _ = before(i, q, 5, 4)
                        if live(0):
                            past(sp, normed, g - 3)
                            sp.dma_start(xb[q][:, :, :], x_g[bass.ds(g, 1)].rearrange("g p j d -> (g p) j d")).then_inc(x_in[q], 16)
                        if live(5):
                            past(sp, evacuated, g5 + 1)
                            sp.dma_start(proj_g[bass.ds(g5, 1)].rearrange("g p j d -> (g p) j d"), pj[q5][:, :, :]).then_inc(p_out[q5], 16)
                    pipelined(sp, emit, ITER, 2, 4, REST)
                    for q in range(4):
                        sp.wait_ge(p_out[q], 16 * (ITER + (q < REST)))
                    sp.wait_ge(s_copied, 4)
                    sp.dma_start(s_dst.rearrange("(t c p) o -> c t (p o)", t=4, p=P), sT[:, :, :]).then_inc(s_stored, 16)
                    sp.wait_ge(s_stored, 16)

                @block.scalar
                def _(act):
                    act.wait_ge(wt_ps, 1)
                    nc.scalar.copy(WT[:, :], psE[0][:, 0, :]).then_inc(wprep, 1)
                    act.wait_ge(wt_ps, 2)
                    nc.scalar.copy(Wsb[:, D:DP], psE[1][:, 0, 0:2]).then_inc(wprep, 1)

                    def emit(i, q, live):
                        g, _, _ = before(i, q, 0, 4)
                        g2, x_q, _ = before(i, q, 2, 4)
                        q, q1, g3 = q % 2, (q - 1) % 2, g - 3
                        if live(2):
                            act.wait_ge(shifted, g2 + 1)
                            past(act, turned, g2 - 1)
                            for j in range(4):
                                ins = nc.scalar.activation(hb[q][:, j, :], xb[x_q][:, j, :], ACT.Relu, bias=nmr[q][:, j:j + 1],
                                                           scale=rstd[q][:, j:j + 1])
                            ins.then_inc(normed, 1)
                        if live(3):
                            act.wait_ge(turned, g3 + 1)
                            past(act, projected, g3 - 1)
                            nc.scalar.copy(hT[q1][:, :, :], psT[q1][:, :, :]).then_inc(ht_ready, 1)
                        if live(0):
                            act.wait_ge(aggr, g + 1)
                            past(act, recip, g - 1)
                            nc.scalar.activation(std[q][:, :], mv[q][:, :, 1], ACT.Sqrt, bias=eps[:, :]).then_inc(stdev, 1)
                    pipelined(act, emit, ITER, 2, 4, REST)

                @block.vector
                def _(dve):
                    nc.vector.memset(eps[:, :], EPS)

                    def emit(i, q, live):
                        g, x_q, turn = before(i, q, 0, 4)
                        g4, p_q, turn4 = before(i, q, 4, 4)
                        q, g2 = q % 2, g - 2
                        if live(2):
                            dve.wait_ge(stdev, g2 + 1)
                            past(dve, normed, g2 - 1)
                            nc.vector.reciprocal(rstd[q][:, :], std[q][:, :]).then_inc(recip, 1)
                        if live(0):
                            dve.wait_ge(x_in[x_q], 16 * turn)
                            past(dve, aggr, g - 1)
                            for j in range(4):
                                ins = nc.vector.bn_stats(stat[q][:, j, :], xb[x_q][:, j, :])
                            ins.then_inc(stats, 1)
                        if live(2):
                            dve.wait_ge(recip, g2 + 1)
                            nc.vector.scalar_tensor_tensor(nmr[q][:, :], mv[q][:, :, 0], -1.0, rstd[q][:, :], ALU.mult,
                                                           ALU.mult).then_inc(shifted, 1)
                        if live(0):
                            past(dve, shifted, g - 1)
                            held(dve, stats, g + 1)
                            for j in range(4):
                                ins = nc.vector.bn_aggr(mv[q][:, j, :], stat[q][:, j, :])
                            ins.then_inc(aggr, 1)
                        if live(4):
                            dve.wait_ge(projected, g4 + 1)
                            past(dve, p_out[p_q], 16 * (turn4 - 1))
                            nc.vector.tensor_copy(s2c[:, bass.ds(4 * g4, 4)], psW[q][:, :, D + 1])
                            nc.vector.tensor_copy(pj[p_q][:, :, :], psW[q][:, :, 0:DP]).then_inc(evacuated, 1)
                    pipelined(dve, emit, ITER, 2, 4, REST)
                    dve.wait_ge(s_turned, 4)
                    for t in range(4):
                        nc.vector.tensor_copy(sT[:, t, :], psE[1][0:98, t, :]).then_inc(s_copied, 1)

                @block.tensor
                def _(pe):
                    pe.wait_ge(w_in, 32)
                    nc.tensor.transpose(psE[0][:, 0, :], Wsb[:, 0:D], ident[:, :]).then_inc(wt_ps, 1)
                    pe.wait_ge(wprep, 1)
                    nc.tensor.matmul(psE[1][:, 0, 0:2], WT[:, :], asb[:, :], start=True, stop=True).then_inc(wt_ps, 1)
                    pe.wait_ge(wprep, 2)

                    def emit(i, q, live):
                        g, _, _ = before(i, q, 0, 4)
                        q, g1, q1, g2 = q % 2, g - 1, (q - 1) % 2, g - 2
                        if live(1):
                            pe.wait_ge(normed, g1 + 1)
                            past(pe, ht_ready, g1 - 1)
                            for j in range(4):
                                ins = nc.tensor.transpose(psT[q1][:, j, :], hb[q1][:, j, :], ident[:, :])
                            ins.then_inc(turned, 1)
                        if live(2):
                            pe.wait_ge(ht_ready, g2 + 1)
                            past(pe, evacuated, g2 - 1)
                            for j in range(4):
                                ins = nc.tensor.matmul(psW[q][:, j, 0:DP], hT[q][:, j, :], Wsb[:, :], start=True, stop=True)
                            ins.then_inc(projected, 1)
                    pipelined(pe, emit, ITER, 2, 4, REST)
                    pe.wait_ge(evacuated, 4 * ITER + REST)
                    for t in range(4):
                        nc.tensor.transpose(psE[1][0:98, t, :], s2c[:, 98 * t:98 * t + 98],
                                            ident[:, :]).then_inc(s_turned, 1)

        end_section()

        with ExitStack() as scores:
            sb = sb_in(scores)
            s1e = sb("s1e", [P, S])
            s2e = sb("s2e", [P, S])
            ok = sb("ok", [P, S])
            tmp = sb("tmp", [P, S])
            sm = sb("sm", [P, 6])
            for far in (False, True):
                with ExitStack() as ctx:
                    sb = sb_in(ctx)
                    t = "f" if far else "m"
                    step0 = NB if far else 0
                    K = 4 if far else 7
                    ON_SP = 4
                    idxk = [sb(f"idxk{t}{q}", [P, K, 2], I32) for q in range(4)]
                    rows = [sb(f"rows{t}{q}", [P, K, DP]) for q in range(4)]
                    sd = [sb(f"sd{t}{q}", [P, K, P]) for q in range(4)]
                    jnk = [sb(f"jnks{t}{q}", [P, K, P]) for q in range(4)]
                    e_idx = [sem(f"e_idx{t}{q}") for q in range(4)]
                    e_sd = [sem(f"e_sd{t}{q}") for q in range(4)]
                    e_got = [sem(f"e_got{t}{q}") for q in range(4)]
                    e_st = [sem(f"e_st{t}{q}") for q in range(4)]
                    e_init = sem(f"e_init{t}")
                    e_kept = sem(f"e_kept{t}")
                    e_sel = sem(f"e_sel{t}")
                    e_s1 = sem(f"e_s1{t}")
                    SD = K if far else 1

                    with nc.Block() as block:
                        def trip(eng):
                            return eng.value_load(trips[0:1, 0:1], min_val=2, max_val=NX // 16 - 1) + 1 if far else NB // 28

                        def load_indices(eng, i, q, ks, srcdst):
                            g, _, turn = before(i, q, 0, 4)
                            for k in ks:
                                start = eng.value_load(ctl[0:1, 0, bass.ds(K * g + (k + step0), 1)], min_val=0, max_val=E)
                                if k == ks[0]:
                                    held(eng, e_kept, g - 3)
                                    held(eng, e_got[q], 16 * K * (turn - 1))
                                eng.dma_start(idxk[q][:, k, :], srcdst[bass.ds(start, P), :]).then_inc(e_idx[q], 16)

                        def store_rows(eng, i, q):
                            g2, q2, turn2 = before(i, q, 2, 4)
                            held(eng, e_got[q2], 16 * K * turn2)
                            eng.dma_start(edge_proj[bass.ds(K * g2 + step0, K)].rearrange("s p d -> p s d"),
                                          rows[q2][:, :, 0:D]).then_inc(e_st[q2], 16)

                        @block.sync
                        def _(sp):
                            def emit(i, q, live, srcdst):
                                if live(0):
                                    load_indices(sp, i, q, range(ON_SP), srcdst)
                                if live(2) and not far:
                                    store_rows(sp, i, q)
                            n = trip(sp)
                            with sp.If(unordered(sp) == 0):
                                pipelined(sp, lambda i, q, live: emit(i, q, live, srcdst), n, 2, 4)
                                sp.sem_inc(passed, 1)
                            with sp.Else():
                                pipelined(sp, lambda i, q, live: emit(i, q, live, srcdst_s), n, 2, 4)
                                sp.sem_inc(passed, 1)
                            for q in range(4):
                                held(sp, e_st[q], 16 * n)

                        @block.scalar
                        def _(act):
                            def emit(i, q, live, srcdst):
                                g, _, _ = before(i, q, 0, 4)
                                if live(0):
                                    if ON_SP < K:
                                        load_indices(act, i, q, range(ON_SP, K), srcdst)
                                    if far:
                                        for k in range(K):
                                            blk = act.value_load(ctl[0:1, 1, bass.ds(K * g + (k + step0), 1)], min_val=0, max_val=NB - 1)
                                            if k == 0:
                                                past(act, e_sel, g - 3)
                                            act.dma_start(sd[q][:, k, :], s_dst.rearrange("(b p) o -> b (p o)", p=P)[bass.ds(blk, 1), :]
                                                          .to_broadcast([P, P])).then_inc(e_sd[q], 16)
                                    else:
                                        held(act, e_sel, g - 3)
                                        act.dma_start(sd[q][:, :, :], s_dst.rearrange("(g b p) o -> g b (p o)", p=P, b=K)[bass.ds(g, 1)]
                                                      .to_broadcast([P, K, P])).then_inc(e_sd[q], 16)
                            n = trip(act)
                            with act.If(unordered(act) == 0):
                                pipelined(act, lambda i, q, live: emit(i, q, live, srcdst), n, 2, 4)
                                act.sem_inc(passed, 1)
                            with act.Else():
                                pipelined(act, lambda i, q, live: emit(i, q, live, srcdst_s), n, 2, 4)
                                act.sem_inc(passed, 1)

                        @block.gpsimd
                        def _(pool):
                            def emit(i, q, live):
                                g, _, turn = before(i, q, 0, 4)
                                if live(0):
                                    past(pool, e_s1, g - 3)
                                    past(pool, e_st[q], 16 * (turn - 1))
                                    held(pool, e_idx[q], 16 * K * turn)
                                    for k in range(K):
                                        nc.gpsimd.indirect_dma_start(
                                            out=rows[q][:, k, :], out_offset=None, in_=h_proj[:, :],
                                            in_offset=bass.IndirectOffsetOnAxis(ap=idxk[q][:, k, 0:1], axis=0)).then_inc(e_got[q], 16)
                                if live(2) and far:
                                    store_rows(pool, i, q)
                            pipelined(pool, emit, trip(pool), 2, 4)

                        @block.vector
                        def _(dve):
                            if not far:
                                nc.vector.memset(s1e[:, :], 0.0).then_inc(e_init, 1)
                                nc.vector.memset(s2e[:, :], 0.0).then_inc(e_init, 1)
                                dve.wait_ge(e_init, 2)

                            def emit(i, q, live):
                                g, _, turn = before(i, q, 0, 4)
                                g2, q2, turn2 = before(i, q, 2, 4)
                                if live(2):
                                    dve.wait_ge(e_got[q2], 16 * K * turn2)
                                    nc.vector.tensor_copy(s1e[:, bass.ds(K * g2 + step0, K)], rows[q2][:, :, D]).then_inc(e_s1, 1)
                                if live(0):
                                    steps = bass.ds(K * g + step0, K)
                                    dve.wait_ge(e_idx[q], 16 * K * turn)
                                    nc.vector.tensor_copy(idx[:, steps, :], idxk[q][:, :, :])
                                    nc.vector.tensor_tensor(dloc[:, steps], idxk[q][:, :, 1], base[:, steps], ALU.subtract).then_inc(e_kept, 1)
                                    dve.wait_ge(e_kept, g + 1)
                                    dve.wait_ge(e_sd[q], 16 * SD * turn)
                                    for k in range(K):
                                        s = bass.ds(K * g + (k + step0), 1)
                                        ins = nc.vector.scalar_tensor_tensor(jnk[q][:, k, :], iota_f[:, :], dloc[:, s], sd[q][:, k, :],
                                                                             ALU.is_equal, ALU.mult, accum_out=s2e[:, s])
                                    ins.then_inc(e_sel, 1)
                            n = trip(dve)
                            pipelined(dve, emit, n, 2, 4)
                            held(dve, e_s1, 4 * n)
                            held(dve, e_sel, 4 * n)
                end_section()

            e_ch = sem("e_ch")
            e_red = sem("e_red")
            e_exp = sem("e_exp")

            with nc.Block() as block:
                @block.scalar
                def _(act):
                    act.wait_ge(e_red, 2)
                    nc.scalar.activation(wgt[:, :], tmp[:, :], ACT.Exp, bias=sm[:, 2:3], accum_out=sm[:, 3:4]).then_inc(e_exp, 1)

                @block.gpsimd
                def _(pool):
                    pool.wait_ge(e_ch, 7)
                    nc.gpsimd.partition_all_reduce(sm[:, 1:2], sm[:, 0:1], P, RMAX).then_inc(e_red, 1)
                    pool.wait_ge(e_exp, 1)
                    nc.gpsimd.partition_all_reduce(sm[:, 4:5], sm[:, 3:4], P, RADD).then_inc(e_red, 1)

                @block.vector
                def _(dve):
                    count = [0]

                    def link(ins):
                        count[0] += 1
                        ins.then_inc(e_ch, 1)
                        dve.wait_ge(e_ch, count[0])
                    link(nc.vector.tensor_tensor(tmp[:, :], s1e[:, :], s2e[:, :], ALU.add))
                    link(nc.vector.scalar_tensor_tensor(s1e[:, :], tmp[:, :], ALPHA, tmp[:, :], ALU.mult, ALU.max))
                    link(nc.vector.tensor_scalar(ok[:, :], dloc[:, :], float(P), None, ALU.is_lt))
                    link(nc.vector.tensor_tensor(s1e[:, :], s1e[:, :], ok[:, :], ALU.mult))
                    link(nc.vector.tensor_scalar(ok[:, :], ok[:, :], -1.0, 3.0e38, ALU.add, ALU.mult))
                    link(nc.vector.tensor_tensor(tmp[:, :], s1e[:, :], ok[:, :], ALU.add))
                    link(nc.vector.tensor_reduce(sm[:, 0:1], tmp[:, :], AX.X, ALU.max))
                    dve.wait_ge(e_red, 1)
                    nc.vector.tensor_scalar(sm[:, 2:3], sm[:, 1:2], -1.0, None, ALU.mult).then_inc(e_red, 1)
                    dve.wait_ge(e_red, 3)
                    link(nc.vector.reciprocal(sm[:, 5:6], sm[:, 4:5]))
                    nc.vector.tensor_scalar(wgt[:, :], wgt[:, :], sm[:, 5:6], None, ALU.mult)

        end_section()

        for far in (True, False):
            with ExitStack() as ctx:
                sb = sb_in(ctx)
                t = "f" if far else "m"
                step0 = NB if far else 0
                K = 4
                rows = [sb(f"rows4{t}{q}", [P, K, D]) for q in range(4)]
                oh = [sb(f"oh{t}{q}", [P, K, P]) for q in range(4)]
                psA = [ctx.enter_context(nc.psum_tensor(f"psA{t}{q}", [P, K, D], F32)) for q in range(4)]
                l_rows = [sem(f"l_rows{t}{q}") for q in range(4)]
                l_oh = sem(f"l_oh{t}")
                l_mm = sem(f"l_mm{t}")
                l_st = [sem(f"l_st{t}{q}") for q in range(4)]
                if far:
                    acc = [sb(f"acc{q}", [P, K, D]) for q in range(4)]
                    l_sum = sem("l_sum")
                    l_init = sem("l_init")
                else:
                    x4 = [sb(f"x4{q}", [P, K, D]) for q in range(4)]
                    part = [sb(f"partm{q}", [P, K, D]) for q in range(4)]
                    xo = [sb(f"xo{q}", [P, K, D]) for q in range(4)]
                    ho = [sb(f"ho{q}", [P, K, D]) for q in range(4)]
                    betaB = sb("betaB", [P, D])
                    stat = [sb(f"stat4{q}", [P, K, 6]) for q in range(4)]
                    mv = [sb(f"mv4{q}", [P, K, 2]) for q in range(4)]
                    std = [sb(f"std4{q}", [P, K]) for q in range(4)]
                    rstd = [sb(f"rstd4{q}", [P, K]) for q in range(4)]
                    nmr = [sb(f"nmr4{q}", [P, K]) for q in range(4)]
                    eps = sb("eps4", [P, 1])
                    l_x = [sem(f"l_x{q}") for q in range(4)]
                    l_part = [sem(f"l_part{q}") for q in range(4)]
                    l_ho = [sem(f"l_ho{q}") for q in range(4)]
                    l_c = sem("l_c")
                    l_new = sem("l_new")
                    l_stat = sem("l_stat")
                    l_aggr = sem("l_aggr")
                    l_std = sem("l_std")
                    l_rec = sem("l_rec")
                    l_shift = sem("l_shift")
                    l_h = sem("l_h")
                    x_g = x.rearrange("(g j p) d -> g p j d", j=K, p=P)
                    x1_g = x1b.rearrange("(g j p) d -> g p j d", j=K, p=P)
                    h1_g = h1[0:NPAD].rearrange("(g j p) d -> g p j d", j=K, p=P)

                with nc.Block() as block:
                    def trip(eng):
                        return eng.value_load(trips[0:1, 0:1], min_val=2, max_val=NX // 16 - 1) + 1 if far else NB // 16

                    def attention(dve, i, q):
                        g, _, _ = before(i, q, 0, 4)
                        past(dve, l_mm, g - 3)
                        for k in range(K):
                            s = bass.ds(K * g + (k + step0), 1)
                            ins = nc.vector.tensor_scalar(oh[q][:, k, :], iota_f[:, :], dloc[:, s], wgt[:, s], ALU.is_equal,
                                                          ALU.mult)
                        ins.then_inc(l_oh, 1)

                    def load_rows(sp, i, q):
                        g, _, _ = before(i, q, 0, 4)
                        held(sp, l_mm, g - 3)
                        sp.dma_start(rows[q][:, :, :], edge_proj[bass.ds(K * g + step0, K)].rearrange("s p d -> p s d")).then_inc(l_rows[q], 16)

                    if far:
                        @block.sync
                        def _(sp):
                            def emit(i, q, live):
                                g3, q3, _ = before(i, q, 3, 4)
                                if live(0):
                                    load_rows(sp, i, q)
                                if live(3):
                                    held(sp, l_sum, K * g3 + K)
                                    sp.dma_start(part0[bass.ds(K * g3 + 1, K)].rearrange("x p d -> p x d"), acc[q3][:, :, :]).then_inc(l_st[q3], 16)
                            n = trip(sp)
                            pipelined(sp, emit, n, 2, 4)
                            for q in range(4):
                                held(sp, l_st[q], 16 * n)

                        @block.tensor
                        def _(pe):
                            def emit(i, q, live):
                                g, _, turn = before(i, q, 0, 4)
                                if live(0):
                                    pe.wait_ge(l_oh, g + 1)
                                    pe.wait_ge(l_rows[q], 16 * turn)
                                    past(pe, l_sum, K * (g - 3))
                                    for k in range(K):
                                        ins = nc.tensor.matmul(psA[q][:, k, :], oh[q][:, k, :], rows[q][:, k, :], start=True, stop=True)
                                    ins.then_inc(l_mm, 1)
                            pipelined(pe, emit, trip(pe), 2, 4)

                        @block.vector
                        def _(dve):
                            nc.vector.memset(acc[3][:, K - 1, :], 0.0).then_inc(l_init, 1)
                            dve.wait_ge(l_init, 1)

                            def emit(i, q, live):
                                g1, q1, turn1 = before(i, q, 1, 4)
                                if live(0):
                                    attention(dve, i, q)
                                if live(1):
                                    dve.wait_ge(l_mm, g1 + 1)
                                    past(dve, l_st[q1], 16 * (turn1 - 1))
                                    for k in range(K):
                                        forerunner = acc[q1][:, k - 1, :] if k else acc[(q1 - 1) % 4][:, K - 1, :]
                                        past(dve, l_sum, K * g1 + k)
                                        nc.vector.scalar_tensor_tensor(acc[q1][:, k, :], forerunner,
                                                                       same[:, bass.ds(K * g1 + k, 1)], psA[q1][:, k, :],
                                                                       ALU.mult, ALU.add).then_inc(l_sum, 1)
                            pipelined(dve, emit, trip(dve), 2, 4)
                    else:
                        def has_far(eng, g):
                            return eng.value_load(some_far[0:1, bass.ds(g, 1)], min_val=0, max_val=1)

                        def load_parts(eng, g, q, ks):
                            with eng.If(has_far(eng, g) == 0):
                                eng.sem_inc(l_part[q], 16 * len(ks))
                            with eng.Else():
                                for k in ks:
                                    slot = eng.value_load(ctl[0:1, 2, bass.ds(K * g + k, 1)], min_val=0, max_val=NX)
                                    eng.dma_start(part[q][:, k, :], part0[bass.ds(slot, 1)].rearrange("x p d -> (x p) d")).then_inc(l_part[q], 16)

                        @block.sync
                        def _(sp):
                            sp.dma_start(betaB[:, :], beta.rearrange("(o d) -> o d", o=1).to_broadcast([P, D])).then_inc(l_c, 16)

                            def emit(i, q, live):
                                g, _, _ = before(i, q, 0, 4)
                                if live(0):
                                    load_rows(sp, i, q)
                                    sp.dma_start(x4[q][:, :, :], x_g[bass.ds(g, 1)].rearrange("g p j d -> (g p) j d")).then_inc(l_x[q], 16)
                                    load_parts(sp, g, q, (0, 1))
                            pipelined(sp, emit, NB // 16, 2, 4, 2)

                        @block.tensor
                        def _(pe):
                            def emit(i, q, live):
                                g, _, turn = before(i, q, 0, 4)
                                if live(0):
                                    pe.wait_ge(l_oh, g + 1)
                                    pe.wait_ge(l_rows[q], 16 * turn)
                                    pe.wait_ge(l_x[q], 16 * turn)
                                    past(pe, l_h, g - 3)
                                    held(pe, l_part[q], 64 * turn)

                                    def products(terms):
                                        for k in range(K):
                                            for n, (lhs, rhs) in enumerate(terms):
                                                ins = nc.tensor.matmul(psA[q][:, k, :], lhs(k), rhs[:, k, :], start=(n == 0),
                                                                       stop=(n == len(terms) - 1))
                                        ins.then_inc(l_mm, 1)
                                    main_terms = (lambda k: oh[q][:, k, :], rows[q]), (lambda k: ident[:, :], x4[q])
                                    with pe.If(has_far(pe, g) == 0):
                                        products(main_terms)
                                    with pe.Else():
                                        products(main_terms + ((lambda k: ident[:, :], part[q]),))
                            pipelined(pe, emit, NB // 16, 2, 4, 2)

                        @block.gpsimd
                        def _(pool):
                            def emit(i, q, live):
                                g2, q2, _ = before(i, q, 2, 4)
                                if live(2):
                                    held(pool, l_new, g2 + 1)
                                    pool.dma_start(x1_g[bass.ds(g2, 1)].rearrange("g p j d -> (g p) j d"), xo[q2][:, :, :]).then_inc(l_st[q2], 16)
                                    held(pool, l_h, g2 + 1)
                                    pool.dma_start(h1_g[bass.ds(g2, 1)].rearrange("g p j d -> (g p) j d"), ho[q2][:, :, :]).then_inc(l_ho[q2], 16)
                            pipelined(pool, emit, NB // 16, 2, 4, 2)
                            for q in range(4):
                                pool.wait_ge(l_st[q], 16 * (NB // 16 + (q < 2)))
                                pool.wait_ge(l_ho[q], 16 * (NB // 16 + (q < 2)))

                        @block.scalar
                        def _(act):
                            def emit(i, q, live):
                                g, _, _ = before(i, q, 0, 4)
                                g3, q3, _ = before(i, q, 3, 4)
                                g4, q4, turn4 = before(i, q, 4, 4)
                                if live(0):
                                    held(act, l_mm, g - 3)
                                    load_parts(act, g, q, (2, 3))
                                if live(4):
                                    act.wait_ge(l_shift, g4 + 1)
                                    past(act, l_ho[q4], 16 * (turn4 - 1))
                                    for k in range(K):
                                        ins = nc.scalar.activation(ho[q4][:, k, :], psA[q4][:, k, :], ACT.Relu,
                                                                   bias=nmr[q4][:, k:k + 1], scale=rstd[q4][:, k:k + 1])
                                    ins.then_inc(l_h, 1)
                                if live(3):
                                    act.wait_ge(l_aggr, g3 + 1)
                                    past(act, l_rec, g3 - 3)
                                    nc.scalar.activation(std[q3][:, :], mv[q3][:, :, 1], ACT.Sqrt, bias=eps[:, :]).then_inc(l_std, 1)
                            pipelined(act, emit, NB // 16, 2, 4, 2)

                        @block.vector
                        def _(dve):
                            nc.vector.memset(eps[:, :], EPS)
                            dve.wait_ge(l_c, 16)

                            def emit(i, q, live):
                                g1, q1, turn1 = before(i, q, 1, 4)
                                g3, q3, _ = before(i, q, 3, 4)
                                if live(3):
                                    dve.wait_ge(l_std, g3 + 1)
                                    past(dve, l_h, g3 - 3)
                                    nc.vector.reciprocal(rstd[q3][:, :], std[q3][:, :]).then_inc(l_rec, 1)
                                if live(0):
                                    attention(dve, i, q)
                                if live(3):
                                    dve.wait_ge(l_rec, g3 + 1)
                                    nc.vector.scalar_tensor_tensor(nmr[q3][:, :], mv[q3][:, :, 0], -1.0, rstd[q3][:, :], ALU.mult,
                                                                   ALU.mult).then_inc(l_shift, 1)
                                if live(1):
                                    dve.wait_ge(l_mm, g1 + 1)
                                    past(dve, l_aggr, g1 - 3)
                                    for k in range(K):
                                        ins = nc.vector.bn_stats(stat[q1][:, k, :], psA[q1][:, k, :])
                                    ins.then_inc(l_stat, 1)
                                    past(dve, l_st[q1], 16 * (turn1 - 1))
                                    nc.vector.tensor_tensor(xo[q1][:, :, :], psA[q1][:, :, :],
                                                            betaB[:, :].rearrange("p (o d) -> p o d", o=1).to_broadcast([P, K, D]),
                                                            ALU.add).then_inc(l_new, 1)
                                    past(dve, l_shift, g1 - 3)
                                    held(dve, l_stat, g1 + 1)
                                    for k in range(K):
                                        ins = nc.vector.bn_aggr(mv[q1][:, k, :], stat[q1][:, k, :])
                                    ins.then_inc(l_aggr, 1)
                            pipelined(dve, emit, NB // 16, 2, 4, 2)
            end_section()

        weights = ExitStack()
        with weights:
            sb = sb_in(weights)
            W1s = sb("W1s", [P, 2, HID])
            W1e = sb("W1e", [DE + 1, HID])
            W2s = sb("W2s", [P, 2, D])
            U1s = sb("U1s", [P, 2, HID])
            U2s = sb("U2s", [P, 2, D])
            b2B = sb("b2B", [P, D])
            b3c = sb("b3c", [P, 2])
            b4B = sb("b4B", [P, D])
            gammaB = sb("gammaB", [P, D])
            ones = sb("ones", [P, 2], BF16)
            half = sb("half", [P, 2])
            m_w = outer.enter_context(nc.semaphore("m_w"))
            idx5 = [sb(f"idx5{q}", [P, 2, 2], I32) for q in range(4)]
            got = [sb(f"got5{q}", [P, 2, 2, D]) for q in range(4)]
            ef = [sb(f"ef{q}", [DE + 1, 2, P]) for q in range(4)]
            oh = [sb(f"oh5{q}", [P, 2, P]) for q in range(4)]
            ohb = [sb(f"ohb5{q}", [P, 2, P], BF16) for q in range(4)]
            gT = [sb(f"gT{q}", [P, 2, 2, P]) for q in range(4)]
            G = [sb(f"G{q}", [P, 2, HID]) for q in range(4)]
            acc8 = sb("acc8", [P, 8, GW])

            for far in (True, False):
                with ExitStack() as ctx:
                    sb = sb_in(ctx)
                    t = "f" if far else "m"
                    step0 = NB if far else 0
                    ITER = NB // 8

                    def pb(name, shape, ctx=ctx, t=t):
                        return ctx.enter_context(nc.psum_tensor(f"{name}{t}", shape, F32))
                    psT = pb("psT5", [P, 2, 2, P])
                    psH = [pb(f"psH{k}", [P, HID]) for k in range(2)]
                    psG = [pb(f"psG{k}", [P, HID + 2]) for k in range(2)]

                    def m(name, t=t):
                        return sem(f"m_{name}{t}")
                    m_idx, m_oh, m_turn, m_gT = m("idx"), m("oh"), m("turn"), m("gT")
                    m_hid, m_gelu, m_sum, m_sumd = m("hid"), m("gelu"), m("sum"), m("sumd")
                    m_got = [m(f"got{q}") for q in range(4)]
                    m_ef = [m(f"ef{q}") for q in range(4)]
                    m_st = [m(f"st{q}") for q in range(4)]
                    m_init = m("init")
                    if not far:
                        hb = [sb(f"hb5{q}", [P, 2, D]) for q in range(4)]
                        h4 = [sb(f"h4{q}", [P, 2, D]) for q in range(4)]
                        xb5 = [sb(f"xb5{q}", [P, 2, D]) for q in range(4)]
                        part = [sb(f"part5{q}", [P, 2, GW]) for q in range(4)]
                        gt = [sb(f"gt{q}", [P, 2, HID + 1]) for q in range(4)]
                        cn = [sb(f"cn{q}", [P, 2]) for q in range(4)]
                        inv = [sb(f"inv{q}", [P, 2]) for q in range(4)]
                        some = [sb(f"some{q}", [P, 2]) for q in range(4)]
                        b2m = [sb(f"b2m{q}", [P, 2, D]) for q in range(4)]
                        ag = [sb(f"ag{q}", [P, 2, D]) for q in range(4)]
                        nT = [sb(f"nT{q}", [P, 4, P]) for q in range(4)]
                        uT = [sb(f"uT{q}", [P, 2, 2 * P]) for q in range(4)]
                        v = [sb(f"v{q}", [P, 2, D]) for q in range(4)]
                        y = [sb(f"y{q}", [P, 2, D]) for q in range(4)]
                        o = [sb(f"o{q}", [P, 2, D]) for q in range(4)]
                        stat = [sb(f"stat5{q}", [P, 2, 6]) for q in range(4)]
                        mv = [sb(f"mv5{q}", [P, 2, 2]) for q in range(4)]
                        rstd = [sb(f"rstd5{q}", [P, 2]) for q in range(4)]
                        ve = [sb(f"ve{q}", [P, 2]) for q in range(4)]
                        psM = pb("psM", [P, 2, D])
                        psN = pb("psN", [P, 4, P])
                        psU = pb("psU", [P, 2, 2 * P])
                        m_hb = [m(f"hb{q}") for q in range(4)]
                        m_xb = [m(f"xb{q}") for q in range(4)]
                        m_pt = [m(f"pt{q}") for q in range(4)]
                        m_cnt, m_inv, m_b2m = m("cnt"), m("inv"), m("b2m")
                        m_w2, m_ag, m_nt, m_nT = m("w2"), m("ag"), m("nt"), m("nT")
                        m_u, m_uT, m_v, m_vd = m("u"), m("uT"), m("v"), m("vd")
                        m_h4, m_stat, m_aggr, m_ve, m_rstd = m("h4"), m("stat"), m("aggr"), m("ve"), m("rstd")
                        m_y, m_o = m("y"), m("o")
                        hb_g = h1[0:NPAD].rearrange("(g j p) d -> g p j d", j=2, p=P)
                        xb_g = x1b.rearrange("(g j p) d -> g p j d", j=2, p=P)
                        out_g = out.rearrange("(g j p) d -> g p j d", j=2, p=P)

                    with nc.Block() as block:
                        def trip(eng):
                            return eng.value_load(trips[0:1, 1:2], min_val=2, max_val=NX // 8 - 1) + 1 if far else ITER

                        @block.sync
                        def _(sp):
                            if far:
                                sp.dma_start(W1s[:, :, :], W1[0:2 * D].rearrange("(c p) h -> p c h", p=P)).then_inc(m_w, 16)
                                sp.dma_start(W1e[0:DE, :], W1[2 * D:2 * D + DE]).then_inc(m_w, 16)
                                sp.dma_start(W1e[DE:DE + 1, :], b1.rearrange("(o h) -> o h", o=1)).then_inc(m_w, 16)
                                sp.dma_start(W2s[:, :, :], W2.rearrange("(c p) d -> p c d", p=P)).then_inc(m_w, 16)
                                sp.dma_start(U1s[:, :, :], U1.rearrange("(c p) h -> p c h", p=P)).then_inc(m_w, 16)
                                sp.dma_start(U2s[:, :, :], U2.rearrange("(c p) d -> p c d", p=P)).then_inc(m_w, 16)
                                sp.dma_start(b3c[:, :], b3).then_inc(m_w, 16)
                                for row, vec in ((b2B, b2), (b4B, b4), (gammaB, gamma)):
                                    sp.dma_start(row[:, :], vec.rearrange("(o d) -> o d", o=1).to_broadcast([P, D])).then_inc(m_w, 16)

                            def emit(i, q, live, edge_t):
                                p, _, _ = before(i, q, 0, 4)
                                if live(0):
                                    for k in range(2):
                                        start = sp.value_load(ctl[0:1, 0, bass.ds(2 * p + (k + step0), 1)], min_val=0, max_val=E)
                                        if k == 0:
                                            held(sp, m_hid, 2 * (p - 4) + 2)
                                        sp.dma_start(ef[q][0:DE, k, :], edge_t[:, bass.ds(start, P)]).then_inc(m_ef[q], 16)
                                    if not far:
                                        past(sp, m_nt, p - 3)
                                        held(sp, m_h4, p - 3)
                                        sp.dma_start(hb[q][:, :, :], hb_g[bass.ds(p, 1)].rearrange("g p j d -> (g p) j d")).then_inc(m_hb[q], 16)
                                        for k in range(2):
                                            slot = sp.value_load(ctl[0:1, 2, bass.ds(2 * p + k, 1)], min_val=0, max_val=NX)
                                            if k == 0:
                                                held(sp, m_sumd, 2 * (p - 4) + 2)
                                            sp.dma_start(part[q][:, k, :], part1[bass.ds(slot, 1)].rearrange("x p d -> (x p) d")).then_inc(m_pt[q], 16)
                                p3, q3, _ = before(i, q, 3, 4)
                                if not far and live(3):
                                    held(sp, m_o, p3 - 3)
                                    sp.dma_start(xb5[q3][:, :, :], xb_g[bass.ds(p3, 1)].rearrange("g p j d -> (g p) j d")).then_inc(m_xb[q3], 16)
                                if far and live(3):
                                    held(sp, m_sumd, 2 * p3 + 2)
                                    sp.dma_start(part1[bass.ds(2 * p3 + 1, 2)].rearrange("x p d -> p x d"),
                                                 acc8[:, 2 * q3:2 * q3 + 2, :]).then_inc(m_st[q3], 16)
                            n = trip(sp)
                            with sp.If(unordered(sp) == 0):
                                pipelined(sp, lambda i, q, live: emit(i, q, live, edge_t), n, 2, 4)
                                sp.sem_inc(passed, 1)
                            with sp.Else():
                                pipelined(sp, lambda i, q, live: emit(i, q, live, edge_ts), n, 2, 4)
                                sp.sem_inc(passed, 1)
                            if far:
                                for q in range(4):
                                    held(sp, m_st[q], 16 * n)

                        @block.gpsimd
                        def _(pool):
                            if far:
                                nc.gpsimd.memset(ones[:, :], 1.0).then_inc(m_init, 1)
                                nc.gpsimd.memset(half[:, :], -0.5).then_inc(m_init, 1)
                                nc.gpsimd.memset(acc8[:, :, :], 0.0).then_inc(m_init, 1)

                            def emit(i, q, live):
                                p, _, turn = before(i, q, 0, 4)
                                if live(0):
                                    held(pool, m_got[q], 64 * (turn - 1))
                                    nc.gpsimd.tensor_copy(idx5[q][:, :, :], idx[:, bass.ds(2 * p + step0, 2), :]).then_inc(m_idx, 1)
                                if live(1):
                                    p1, q1, _ = before(i, q, 1, 4)
                                    past(pool, m_turn, p1 - 3)
                                    held(pool, m_idx, p1 + 1)
                                    for k in range(2):
                                        for c in range(2):
                                            nc.gpsimd.indirect_dma_start(
                                                out=got[q1][:, k, c, :], out_offset=None, in_=h1[:, :],
                                                in_offset=bass.IndirectOffsetOnAxis(ap=idx5[q1][:, k, c:c + 1], axis=0)).then_inc(m_got[q1], 16)
                                if far:
                                    return
                                if live(2):
                                    p2, q2, turn2 = before(i, q, 2, 4)
                                    past(pool, m_vd, p2 - 3)
                                    held(pool, m_hb[q2], 16 * turn2)
                                    nc.gpsimd.tensor_tensor(h4[q2][:, :, :], hb[q2][:, :, :],
                                                            b4B[:, :].rearrange("p (o d) -> p o d", o=1).to_broadcast([P, 2, D]),
                                                            ALU.add).then_inc(m_h4, 1)
                                if live(5):
                                    p5, q5, _ = before(i, q, 5, 4)
                                    past(pool, m_o, p5 - 1)
                                    held(pool, m_ve, p5 + 1)
                                    nc.gpsimd.tensor_tensor(rstd[q5][:, :], ve[q5][:, :], half[:, :], ALU.pow).then_inc(m_rstd, 1)
                            pipelined(pool, emit, trip(pool), 2, 4)

                        @block.tensor
                        def _(pe):
                            if far:
                                pe.wait_ge(m_w, 160)
                                pe.wait_ge(m_init, 7)

                            def hidden(i, q, k):
                                p, q, turn = before(i, q, 1, 4)
                                if k == 0:
                                    pe.wait_ge(m_gT, p + 1)
                                    pe.wait_ge(m_ef[q], 32 * turn)
                                past(pe, m_gelu, 2 * p + (k - 1))
                                nc.tensor.matmul(psH[k][:, :], gT[q][:, k, 0, :], W1s[:, 0, :], start=True, stop=False)
                                nc.tensor.matmul(psH[k][:, :], gT[q][:, k, 1, :], W1s[:, 1, :], start=False, stop=False)
                                nc.tensor.matmul(psH[k][:, :], ef[q][:, k, :], W1e[:, :], start=False, stop=True).then_inc(m_hid, 1)

                            def emit(i, q, live):
                                p, _, turn = before(i, q, 0, 4)
                                p2, q2, turn2 = before(i, q, 2, 4)
                                p3, q3, _ = before(i, q, 3, 4)
                                if live(0):
                                    pe.wait_ge(m_got[q], 64 * turn)
                                    past(pe, m_gT, p)
                                    for k in range(2):
                                        for c in range(2):
                                            ins = nc.tensor.transpose(psT[:, k, c, :], got[q][:, k, c, :], ident[:, :])
                                    ins.then_inc(m_turn, 1)
                                if live(2):
                                    for k in range(2):
                                        pe.wait_ge(m_gelu, 2 * p2 + (k + 1))
                                        pe.wait_ge(m_oh, p2 + 1)
                                        past(pe, m_sumd, 2 * p2 + (k - 1))
                                        for c in range(2):
                                            nc.tensor.matmul(psG[k][:, c * P:(c + 1) * P], G[q2][:, k, c * P:(c + 1) * P],
                                                             oh[q2][:, k, :], start=True, stop=True)
                                        nc.tensor.matmul(psG[k][:, HID:HID + 2], ohb[q2][:, k, :], ones[:, :], start=True,
                                                         stop=True).then_inc(m_sum, 1)
                                if live(1):
                                    hidden(i, q, 0)
                                if not far and live(2):
                                    pe.wait_ge(m_sumd, 2 * p2 + 2)
                                    past(pe, m_vd, p2 - 1)
                                    for k in range(2):
                                        for c in range(2):
                                            ins = nc.tensor.matmul(psM[:, k, :], gt[q2][:, k, c * P:(c + 1) * P], W2s[:, c, :],
                                                                   start=(c == 0), stop=(c == 1))
                                    ins.then_inc(m_w2, 1)
                                if live(1):
                                    hidden(i, q, 1)
                                if far:
                                    return
                                if live(2):
                                    pe.wait_ge(m_ag, p2 + 1)
                                    pe.wait_ge(m_hb[q2], 16 * turn2)
                                    past(pe, m_nT, p2)
                                    for k in range(2):
                                        nc.tensor.transpose(psN[:, k, :], hb[q2][:, k, :], ident[:, :])
                                    for k in range(2):
                                        ins = nc.tensor.transpose(psN[:, 2 + k, :], ag[q2][:, k, :], ident[:, :])
                                    ins.then_inc(m_nt, 1)
                                if live(3):
                                    pe.wait_ge(m_uT, p3 + 1)
                                    if live(2):
                                        pe.wait_ge(m_ag, p2 + 1)
                                    else:
                                        past(pe, m_vd, p3)
                                    for k in range(2):
                                        for c in range(2):
                                            ins = nc.tensor.matmul(psM[:, k, :], uT[q3][:, c, k * P:(k + 1) * P], U2s[:, c, :],
                                                                   start=(c == 0), stop=(c == 1))
                                    ins.then_inc(m_v, 1)
                                if live(2):
                                    pe.wait_ge(m_nT, p2 + 1)
                                    past(pe, m_uT, p2)
                                    for c in range(2):
                                        nc.tensor.matmul(psU[:, c, :], U1s[:, 0, c * P:(c + 1) * P], nT[q2][:, 0:2, :],
                                                         start=True, stop=False)
                                        ins = nc.tensor.matmul(psU[:, c, :], U1s[:, 1, c * P:(c + 1) * P], nT[q2][:, 2:4, :],
                                                               start=False, stop=True)
                                    ins.then_inc(m_u, 1)
                            pipelined(pe, emit, trip(pe), 2, 4)

                        @block.scalar
                        def _(act):
                            def emit(i, q, live):
                                p, _, _ = before(i, q, 0, 4)
                                p1, q1, _ = before(i, q, 1, 4)
                                p2, q2, _ = before(i, q, 2, 4)
                                p5, q5, _ = before(i, q, 5, 4)
                                if live(0):
                                    act.wait_ge(m_turn, p + 1)
                                    past(act, m_hid, 2 * (p - 4) + 2)
                                    nc.scalar.copy(gT[q][:, :, :, :], psT[:, :, :, :]).then_inc(m_gT, 1)
                                if live(1):
                                    for k in range(2):
                                        act.wait_ge(m_hid, 2 * p1 + (k + 1))
                                        past(act, m_sum, 2 * (p1 - 4) + 2)
                                        nc.scalar.activation(G[q1][:, k, :], psH[k][:, :], ACT.Gelu).then_inc(m_gelu, 1)
                                if far:
                                    return
                                if live(2):
                                    act.wait_ge(m_nt, p2 + 1)
                                    past(act, m_u, p2 - 3)
                                    nc.scalar.copy(nT[q2][:, :, :], psN[:, :, :]).then_inc(m_nT, 1)
                                    act.wait_ge(m_u, p2 + 1)
                                    past(act, m_v, p2 - 3)
                                    for c in range(2):
                                        ins = nc.scalar.activation(uT[q2][:, c, :], psU[:, c, :], ACT.Gelu, bias=b3c[:, c:c + 1])
                                    ins.then_inc(m_uT, 1)
                                if live(5):
                                    act.wait_ge(m_o, p5 + 1)
                                    act.dma_start(out_g[bass.ds(p5, 1)].rearrange("g p j d -> (g p) j d"), o[q5][:, :, :]).then_inc(m_st[q5], 16)
                            pipelined(act, emit, trip(act), 2, 4)
                            if not far:
                                for q in range(4):
                                    act.wait_ge(m_st[q], 16 * ITER)

                        @block.vector
                        def _(dve):
                            if far:
                                for q in range(4):
                                    nc.vector.memset(ef[q][DE:DE + 1, :, :], 1.0).then_inc(m_init, 1)
                                dve.wait_ge(m_init, 7)

                            def emit(i, q, live):
                                p, _, _ = before(i, q, 0, 4)
                                p2, q2, turn2 = before(i, q, 2, 4)
                                p3, q3, _ = before(i, q, 3, 4)
                                p4, q4, turn4 = before(i, q, 4, 4)
                                if live(0):
                                    past(dve, m_sum, 2 * (p - 4) + 2)
                                    for k in range(2):
                                        of = dloc[:, bass.ds(2 * p + (k + step0), 1)]
                                        nc.vector.tensor_scalar(oh[q][:, k, :], iota_f[:, :], of, None, ALU.is_equal)
                                        ins = nc.vector.tensor_scalar(ohb[q][:, k, :], iota_f[:, :], of, None, ALU.is_equal)
                                    ins.then_inc(m_oh, 1)
                                if far and live(2):
                                    past(dve, m_st[q2], 16 * (turn2 - 1))
                                    for k in range(2):
                                        dve.wait_ge(m_sum, 2 * p2 + (k + 1))
                                        past(dve, m_sumd, 2 * p2 + k)
                                        a8 = 2 * q2 + k
                                        nc.vector.scalar_tensor_tensor(acc8[:, a8, 0:HID + 1], acc8[:, (a8 - 1) % 8, 0:HID + 1],
                                                                       same[:, bass.ds(2 * p2 + k, 1)], psG[k][:, 0:HID + 1],
                                                                       ALU.mult, ALU.add).then_inc(m_sumd, 1)
                                if far:
                                    return
                                if live(2):
                                    dve.wait_ge(m_pt[q2], 32 * turn2)
                                    past(dve, m_w2, p2 - 3)
                                    for k in range(2):
                                        dve.wait_ge(m_sum, 2 * p2 + (k + 1))
                                        nc.vector.tensor_tensor(gt[q2][:, k, :], psG[k][:, 0:HID + 1], part[q2][:, k, 0:HID + 1],
                                                                ALU.add).then_inc(m_sumd, 1)
                                    dve.wait_ge(m_sumd, 2 * p2 + 2)
                                    nc.vector.tensor_scalar(cn[q2][:, :], gt[q2][:, :, HID], 1.0, None, ALU.max).then_inc(m_cnt, 1)
                                    nc.vector.tensor_scalar(some[q2][:, :], gt[q2][:, :, HID], 1.0, None, ALU.min).then_inc(m_cnt, 1)
                                if live(4):
                                    for k in range(2):
                                        ins = nc.vector.scalar_tensor_tensor(y[q4][:, k, :], v[q4][:, k, :], mv[q4][:, k, 0:1],
                                                                             gammaB[:, :], ALU.subtract, ALU.mult)
                                    ins.then_inc(m_y, 1)
                                    dve.wait_ge(m_y, p4 + 1)
                                    dve.wait_ge(m_rstd, p4 + 1)
                                    dve.wait_ge(m_xb[q4], 16 * turn4)
                                    past(dve, m_st[q4], 16 * (turn4 - 1))
                                    for k in range(2):
                                        ins = nc.vector.scalar_tensor_tensor(o[q4][:, k, :], y[q4][:, k, :], rstd[q4][:, k:k + 1],
                                                                             xb5[q4][:, k, :], ALU.mult, ALU.add)
                                    ins.then_inc(m_o, 1)
                                if live(2):
                                    dve.wait_ge(m_cnt, 2 * p2 + 2)
                                    nc.vector.reciprocal(inv[q2][:, :], cn[q2][:, :]).then_inc(m_inv, 1)
                                    for k in range(2):
                                        ins = nc.vector.tensor_scalar(b2m[q2][:, k, :], b2B[:, :], some[q2][:, k:k + 1], None, ALU.mult)
                                    ins.then_inc(m_b2m, 1)
                                    dve.wait_ge(m_inv, p2 + 1)
                                    dve.wait_ge(m_b2m, p2 + 1)
                                    dve.wait_ge(m_w2, p2 + 1)
                                    past(dve, m_nt, p2 - 3)
                                    for k in range(2):
                                        ins = nc.vector.scalar_tensor_tensor(ag[q2][:, k, :], psM[:, k, :], inv[q2][:, k:k + 1],
                                                                             b2m[q2][:, k, :], ALU.mult, ALU.add)
                                    ins.then_inc(m_ag, 1)
                                if live(3):
                                    dve.wait_ge(m_v, p3 + 1)
                                    dve.wait_ge(m_h4, p3 + 1)
                                    nc.vector.tensor_tensor(v[q3][:, :, :], psM[:, :, :], h4[q3][:, :, :], ALU.add).then_inc(m_vd, 1)
                                    dve.wait_ge(m_vd, p3 + 1)
                                    for k in range(2):
                                        ins = nc.vector.bn_stats(stat[q3][:, k, :], v[q3][:, k, :])
                                    ins.then_inc(m_stat, 1)
                                    held(dve, m_stat, p3 + 1)
                                    for k in range(2):
                                        ins = nc.vector.bn_aggr(mv[q3][:, k, :], stat[q3][:, k, :])
                                    ins.then_inc(m_aggr, 1)
                                    dve.wait_ge(m_aggr, p3 + 1)
                                    nc.vector.tensor_scalar(ve[q3][:, :], mv[q3][:, :, 1], EPS, None, ALU.add).then_inc(m_ve, 1)
                            pipelined(dve, emit, trip(dve), 2, 4)
                end_section()



_OUT = "out_dram"


def kernel(**inputs):
    import concourse.bacc as _bacc
    from concourse.bass_utils import run_bass_kernel_spmd as _run

    def padded(v, rows, fill):
        return np.concatenate([v, np.full((rows - v.shape[0],) + v.shape[1:], fill, v.dtype)])

    g = {k: np.asarray(v) for k, v in inputs.items()}
    src, dst = padded(g["src"], EPAD, 0), padded(g["dst"], DT, SENT)
    arrays = {
        "x": padded(g["x"], NPAD, 0),
        "srcdst": np.stack([src, dst[:EPAD]], axis=1),
        "dst": dst,
        "edge_t": np.ascontiguousarray(padded(g["edge_attr_64"], EPAD, 0).T),
        "edge_rows": padded(g["edge_attr_64"], EPAD, 0),
        "W": g["L0_gnn_W"], "a": g["L0_gnn_a"].reshape(2, D).T,
        "W1": g["L1_gnn_W1"], "b1": g["L1_gnn_b1"], "W2": g["L1_gnn_W2"], "b2": g["L1_gnn_b2"],
        "U1": g["L1_gnn_U1"], "b3": g["L1_gnn_b3"].reshape(2, P).T, "U2": g["L1_gnn_U2"], "b4": g["L1_gnn_b4"],
        "gamma": g["L1_gnn_gamma"], "beta": g["L1_gnn_beta"],
    }
    nc = _bacc.Bacc("TRN2", target_bir_lowering=False, num_devices=1)
    named, args = {}, []
    for name, v in arrays.items():
        named[f"in_{name}"] = np.ascontiguousarray(v)
        args.append(nc.dram_tensor(f"in_{name}", v.shape, mybir.dt.from_np(v.dtype), kind="ExternalInput").ap())
    args.append(nc.dram_tensor(_OUT, (NPAD, D), F32, kind="ExternalOutput").ap())
    gnn_kernel(nc, *args)
    r = _run(nc, [named], core_ids=[0])
    return r.results[0][_OUT][:N]
```
